# Optimizing a Trainium2 kernel written in Bass

```python
import numpy as np
import jax
import jax.numpy as jnp

def _softmax(x, axis=-1):
    return jax.nn.softmax(x, axis=axis)

def _gelu(x):
    return jax.nn.gelu(x, approximate=True)

def _silu(x):
    return jax.nn.silu(x)

def _sigmoid(x):
    return jax.nn.sigmoid(x)

def _layernorm(x, axis=-1, eps=1e-05):
    m = jnp.mean(x, axis=axis, keepdims=True)
    v = jnp.var(x, axis=axis, keepdims=True)
    return (x - m) / jnp.sqrt(v + eps)

def _scatter_add(tgt, idx, src, axis=0):
    return tgt.at[idx].add(src)

def _segment_sum(src, seg, n):
    return jax.ops.segment_sum(src, seg, n)
kernel_name = 'mk_prb_d4_jaxref_r8_3b5ac8'

def setup_inputs(seed: int=0):
    np.random.seed(seed)
    _w = jnp.asarray

    def _L0_attn_setup():
        import jax, jax.numpy as jnp
        import numpy as np
        D_MODEL = 128
        D_STATE = 16
        D_CONV = 4
        D_INNER = 2 * D_MODEL
        BATCH = 2
        SEQ = 256
        LN_EPS = 1e-05

        def _layernorm(x, w, b):
            mu = jnp.mean(x, axis=-1, keepdims=True)
            var = jnp.mean(jnp.square(x - mu), axis=-1, keepdims=True)
            return (x - mu) * jax.lax.rsqrt(var + LN_EPS) * w + b

        def _forward(x, norm_w, norm_b, in_proj_w, conv_w, conv_b, x_proj_w, dt_w, dt_b, out_proj_w):
            residual = x
            xn = _layernorm(x, norm_w, norm_b)
            xz = xn @ in_proj_w.T
            x_in, z = jnp.split(xz, 2, axis=-1)
            x_conv = jax.lax.conv_general_dilated(jnp.swapaxes(x_in, 1, 2), conv_w, window_strides=(1,), padding=[(D_CONV - 1, 0)], dimension_numbers=('NCH', 'OIH', 'NCH'))
            x_conv = jnp.swapaxes(x_conv, 1, 2) + conv_b
            x_act = jax.nn.silu(x_conv)
            x_ssm = x_act @ x_proj_w.T
            delta_s = x_ssm[..., :1]
            B_mat = x_ssm[..., 1:1 + D_STATE].astype(jnp.float32)
            C = x_ssm[..., 1 + D_STATE:].astype(jnp.float32)
            delta = jax.nn.softplus(delta_s @ dt_w.T + dt_b).astype(jnp.float32)
            x_f32 = x_act.astype(jnp.float32)

            def step(h, inputs):
                d_t, b_t, c_t, u_t = inputs
                h = h * jnp.exp(-d_t)[..., None] + b_t[:, None, :] * u_t[..., None]
                y_t = jnp.einsum('bds,bs->bd', h, c_t)
                return (h, y_t)
            h0 = jnp.zeros((x.shape[0], D_INNER, D_STATE), jnp.float32)
            xs = (jnp.moveaxis(delta, 1, 0), jnp.moveaxis(B_mat, 1, 0), jnp.moveaxis(C, 1, 0), jnp.moveaxis(x_f32, 1, 0))
            _, y = jax.lax.scan(step, h0, xs)
            y = jnp.moveaxis(y, 0, 1).astype(x.dtype)
            return y * jax.nn.silu(z) @ out_proj_w.T + residual
        key = jax.random.key(seed)
        ks = jax.random.split(key, 10)
        s = lambda k, shape, fan: jax.random.normal(k, shape, jnp.float32) * (1.0 / np.sqrt(fan))
        return {'x': jax.random.normal(ks[0], (BATCH, SEQ, D_MODEL), jnp.float32), 'norm_w': jnp.ones((D_MODEL,), jnp.float32), 'norm_b': jnp.zeros((D_MODEL,), jnp.float32), 'in_proj_w': s(ks[1], (2 * D_INNER, D_MODEL), D_MODEL), 'conv_w': s(ks[2], (D_INNER, D_INNER, D_CONV), D_INNER * D_CONV), 'conv_b': s(ks[3], (D_INNER,), D_INNER * D_CONV), 'x_proj_w': s(ks[4], (2 * D_STATE + 1, D_INNER), D_INNER), 'dt_w': s(ks[5], (D_INNER, 1), 1), 'dt_b': s(ks[6], (D_INNER,), 1), 'out_proj_w': s(ks[7], (D_MODEL, D_INNER), D_INNER)}
    _L0_attn_in = _L0_attn_setup()

    def _L0_ffn_setup():
        import jax, jax.numpy as jnp
        import numpy as np
        DIM = 128
        E = 8
        K = 2
        EPS = 1e-05

        def _ln(x, g, b):
            mu = jnp.mean(x, axis=-1, keepdims=True)
            var = jnp.mean(jnp.square(x - mu), axis=-1, keepdims=True)
            return (x - mu) * jax.lax.rsqrt(var + EPS) * g + b
        key = jax.random.key(seed)
        ks = jax.random.split(key, 8)
        H = 2 * DIM
        s_in = 1.0 / np.sqrt(DIM)
        s_h = 1.0 / np.sqrt(H)
        return {'x': jax.random.normal(ks[0], (2, 256, DIM), dtype=jnp.float32), 'gate_w': jax.random.uniform(ks[1], (DIM, E), minval=-s_in, maxval=s_in, dtype=jnp.float32), 'w1': jax.random.uniform(ks[2], (E, DIM, H), minval=-s_in, maxval=s_in, dtype=jnp.float32), 'b1': jax.random.uniform(ks[3], (E, H), minval=-s_in, maxval=s_in, dtype=jnp.float32), 'ln1_g': jnp.ones((E, H), dtype=jnp.float32), 'ln1_b': jnp.zeros((E, H), dtype=jnp.float32), 'w2': jax.random.uniform(ks[4], (E, H, DIM), minval=-s_h, maxval=s_h, dtype=jnp.float32), 'b2': jax.random.uniform(ks[5], (E, DIM), minval=-s_h, maxval=s_h, dtype=jnp.float32), 'ln_g': jnp.ones((DIM,), dtype=jnp.float32), 'ln_b': jnp.zeros((DIM,), dtype=jnp.float32)}
    _L0_ffn_in = _L0_ffn_setup()

    def _L1_attn_setup():
        import jax, jax.numpy as jnp
        import numpy as np
        D_MODEL, D_STATE, D_CONV, EXPAND = (128, 16, 4, 2)
        D_INNER = EXPAND * D_MODEL
        EPS = 1e-06

        def _forward(x, norm_w, in_proj_w, conv_w, dt_w, dt_b, A_log, B_w, C_w, D_skip, out_proj_w):
            Bsz, T, _ = x.shape
            xn = x * jax.lax.rsqrt(jnp.mean(x * x, axis=-1, keepdims=True) + EPS) * norm_w
            xg = xn @ in_proj_w
            x_inner, gate = jnp.split(xg, 2, axis=-1)
            x_inner = x_inner * jax.nn.silu(gate)
            xc = jax.lax.conv_general_dilated(x_inner.transpose(0, 2, 1), conv_w, window_strides=(1,), padding=[(D_CONV - 1, 0)], feature_group_count=D_INNER, dimension_numbers=('NCH', 'OIH', 'NCH')).transpose(0, 2, 1)
            dt = jax.nn.softplus(xc @ dt_w + dt_b)
            A = -jnp.exp(A_log)
            Bm = xc @ B_w
            Cm = xc @ C_w
            A_bar = jnp.exp(dt[..., None] * A)
            B_bar = dt[..., None] * Bm[:, :, None, :]

            def step(h, inp):
                a_t, b_t, xc_t, c_t = inp
                h = a_t * h + b_t * xc_t[..., None]
                y = jnp.einsum('bds,bs->bd', h, c_t) + D_skip * xc_t
                return (h, y)
            h0 = jnp.zeros((Bsz, D_INNER, D_STATE), x.dtype)
            xs = (A_bar.transpose(1, 0, 2, 3), B_bar.transpose(1, 0, 2, 3), xc.transpose(1, 0, 2), Cm.transpose(1, 0, 2))
            _, ys = jax.lax.scan(step, h0, xs)
            out = ys.transpose(1, 0, 2) @ out_proj_w
            return out
        key = jax.random.key(seed)
        ks = jax.random.split(key, 8)
        B, T = (2, 128)
        s = lambda fan_in: 1.0 / np.sqrt(fan_in)
        x = jax.random.normal(ks[0], (B, T, D_MODEL), dtype=jnp.float32)
        norm_w = jnp.ones((D_MODEL,), jnp.float32)
        in_proj_w = jax.random.normal(ks[1], (D_MODEL, 2 * D_INNER), jnp.float32) * s(D_MODEL)
        conv_w = jax.random.normal(ks[2], (D_INNER, 1, D_CONV), jnp.float32) * s(D_CONV)
        dt_w = jax.random.normal(ks[3], (D_INNER, D_INNER), jnp.float32) * s(D_INNER)
        dt_b = jnp.zeros((D_INNER,), jnp.float32)
        A_log = jnp.log(jnp.broadcast_to(jnp.arange(1, D_STATE + 1, dtype=jnp.float32), (D_INNER, D_STATE)))
        B_w = jax.random.normal(ks[4], (D_INNER, D_STATE), jnp.float32) * s(D_INNER)
        C_w = jax.random.normal(ks[5], (D_INNER, D_STATE), jnp.float32) * s(D_INNER)
        D_skip = jnp.ones((D_INNER,), jnp.float32)
        out_proj_w = jax.random.normal(ks[6], (D_INNER, D_MODEL), jnp.float32) * s(D_INNER)
        return {'x': x, 'norm_w': norm_w, 'in_proj_w': in_proj_w, 'conv_w': conv_w, 'dt_w': dt_w, 'dt_b': dt_b, 'A_log': A_log, 'B_w': B_w, 'C_w': C_w, 'D_skip': D_skip, 'out_proj_w': out_proj_w}
    _L1_attn_in = _L1_attn_setup()

    def _L1_ffn_setup():
        import jax, jax.numpy as jnp
        import numpy as np
        B, S, D, E, H, DO = (4, 256, 128, 8, 512, 128)
        TOP_K = 2
        LN_EPS = 1e-05
        key = jax.random.key(seed)
        ks = jax.random.split(key, 9)
        s = 0.02
        return {'x': jax.random.normal(ks[0], (B, S, D), dtype=jnp.float32), 'W1': jax.random.normal(ks[1], (E, D, H), dtype=jnp.float32) * s, 'b1': jnp.zeros((E, H), dtype=jnp.float32), 'W2': jax.random.normal(ks[2], (E, H, DO), dtype=jnp.float32) * s, 'b2': jnp.zeros((E, DO), dtype=jnp.float32), 'gate_W': jax.random.normal(ks[3], (D, E), dtype=jnp.float32) * s, 'shared_W': jax.random.normal(ks[4], (D, DO), dtype=jnp.float32) * s, 'shared_b': jnp.zeros((DO,), dtype=jnp.float32), 'gamma': jnp.ones((DO,), dtype=jnp.float32), 'beta': jnp.zeros((DO,), dtype=jnp.float32)}
    _L1_ffn_in = _L1_ffn_setup()

    def _L2_attn_setup():
        import jax, jax.numpy as jnp
        import numpy as np
        B, S, E, H, D = (1, 256, 128, 16, 64)
        LAM_INIT = 0.8
        LN_EPS = 1e-05
        key = jax.random.key(seed)
        ks = jax.random.split(key, 6)
        w = 0.02
        return {'X': jax.random.normal(ks[0], (B, S, E), dtype=jnp.float32), 'Wq': jax.random.normal(ks[1], (H, E, 2 * D), dtype=jnp.float32) * w, 'bq': jnp.zeros((H, 2 * D), dtype=jnp.float32), 'Wk': jax.random.normal(ks[2], (H, E, 2 * D), dtype=jnp.float32) * w, 'bk': jnp.zeros((H, 2 * D), dtype=jnp.float32), 'Wv': jax.random.normal(ks[3], (H, E, D), dtype=jnp.float32) * w, 'bv': jnp.zeros((H, D), dtype=jnp.float32), 'Wo': jax.random.normal(ks[4], (H * D, E), dtype=jnp.float32) * w, 'bo': jnp.zeros((E,), dtype=jnp.float32), 'gamma': jnp.ones((E,), dtype=jnp.float32), 'beta': jnp.zeros((E,), dtype=jnp.float32), 'lam': jnp.float32(0.5)}
    _L2_attn_in = _L2_attn_setup()

    def _L2_ffn_setup():
        import jax, jax.numpy as jnp
        import numpy as np
        B, S, H = (2, 64, 128)
        E, I = (64, 64)
        K = 8
        G, TG = (8, 4)
        SCALE = 2.5
        T = B * S
        CAP = 64

        def _moe_forward(x, router_w, gate_w, up_w, down_w, shared_gate_w, shared_up_w, shared_down_w):
            b, s, h = x.shape
            tokens = x.reshape(-1, h)
            t = tokens.shape[0]
            logits = tokens @ router_w
            scores = jax.nn.sigmoid(logits)
            eg = E // G
            group_scores = scores.reshape(t, G, eg).max(axis=-1)
            _, sel_groups = jax.lax.top_k(group_scores, TG)
            group_mask = jnp.zeros((t, G), bool).at[jnp.arange(t)[:, None], sel_groups].set(True)
            expert_mask = jnp.repeat(group_mask, eg, axis=1)
            masked_scores = jnp.where(expert_mask, scores, 0.0)
            topk_w, topk_idx = jax.lax.top_k(masked_scores, K)
            topk_w = topk_w / jnp.clip(topk_w.sum(-1, keepdims=True), 1e-09)
            topk_w = topk_w * SCALE
            flat_e = topk_idx.reshape(-1)
            onehot = jax.nn.one_hot(flat_e, E, dtype=jnp.int32)
            prior = jnp.cumsum(onehot, axis=0) - onehot
            pos = jnp.take_along_axis(prior, flat_e[:, None], axis=1)[:, 0]
            valid = (pos < CAP).astype(tokens.dtype)
            pos_c = jnp.minimum(pos, CAP - 1)
            tidx = jnp.repeat(jnp.arange(t), K)
            dispatch = jnp.zeros((E, CAP, h), tokens.dtype)
            dispatch = dispatch.at[flat_e, pos_c].add(tokens[tidx] * valid[:, None])
            g = jnp.einsum('ech,ehi->eci', dispatch, gate_w)
            u = jnp.einsum('ech,ehi->eci', dispatch, up_w)
            expert_out = jnp.einsum('eci,eih->ech', jax.nn.silu(g) * u, down_w)
            gathered = expert_out[flat_e, pos_c]
            contrib = gathered * (topk_w.reshape(-1) * valid)[:, None]
            output = jnp.zeros((t, h), tokens.dtype).at[tidx].add(contrib)
            sg = jax.nn.silu(tokens @ shared_gate_w) * (tokens @ shared_up_w)
            output = output + sg @ shared_down_w
            return output.reshape(b, s, h)
        key = jax.random.key(seed)
        ks = jax.random.split(key, 9)
        s_h = 1.0 / np.sqrt(H)
        s_i = 1.0 / np.sqrt(I)
        return {'x': jax.random.normal(ks[0], (B, S, H), jnp.float32), 'router_w': jax.random.normal(ks[1], (H, E), jnp.float32) * s_h, 'gate_w': jax.random.normal(ks[2], (E, H, I), jnp.float32) * s_h, 'up_w': jax.random.normal(ks[3], (E, H, I), jnp.float32) * s_h, 'down_w': jax.random.normal(ks[4], (E, I, H), jnp.float32) * s_i, 'shared_gate_w': jax.random.normal(ks[5], (H, I), jnp.float32) * s_h, 'shared_up_w': jax.random.normal(ks[6], (H, I), jnp.float32) * s_h, 'shared_down_w': jax.random.normal(ks[7], (I, H), jnp.float32) * s_i}
    _L2_ffn_in = _L2_ffn_setup()

    def _L3_attn_setup():
        import jax, jax.numpy as jnp
        import numpy as np
        import math
        D_MODEL, D_STATE, D_CONV, EXPAND = (128, 16, 4, 2)
        D_INNER = EXPAND * D_MODEL
        HALF = D_INNER // 2
        DT_RANK = math.ceil(D_MODEL / 16)
        BATCH, SEQLEN = (8, 256)

        def _depthwise_conv1d(x, k):
            return jax.lax.conv_general_dilated(x, k, window_strides=(1,), padding='SAME', feature_group_count=x.shape[-1], dimension_numbers=('NWC', 'WIO', 'NWC'))

        def _selective_scan(u, delta, A, B, C, D):
            b, l, d = u.shape
            n = A.shape[1]

            def step(h, t):
                u_t, dt_t, B_t, C_t = t
                dA = jnp.exp(dt_t[..., None] * A)
                h = dA * h + (dt_t * u_t)[..., None] * B_t[:, None, :]
                y = jnp.einsum('bdn,bn->bd', h, C_t)
                return (h, y)
            h0 = jnp.zeros((b, d, n), u.dtype)
            xs = (jnp.swapaxes(u, 0, 1), jnp.swapaxes(delta, 0, 1), jnp.swapaxes(B, 0, 1), jnp.swapaxes(C, 0, 1))
            _, ys = jax.lax.scan(step, h0, xs)
            return jnp.swapaxes(ys, 0, 1) + u * D
        key = jax.random.key(seed)
        ks = jax.random.split(key, 10)
        x = jax.random.normal(ks[0], (BATCH, SEQLEN, D_MODEL), dtype=jnp.float32)
        W_in = jax.random.normal(ks[1], (D_MODEL, D_INNER), jnp.float32) / np.sqrt(D_MODEL)
        conv_x_k = jax.random.normal(ks[2], (D_CONV, 1, HALF), jnp.float32) / np.sqrt(D_CONV)
        conv_z_k = jax.random.normal(ks[3], (D_CONV, 1, HALF), jnp.float32) / np.sqrt(D_CONV)
        W_xproj = jax.random.normal(ks[4], (HALF, DT_RANK + 2 * D_STATE), jnp.float32) / np.sqrt(HALF)
        dt_init_std = DT_RANK ** (-0.5)
        W_dt = jax.random.uniform(ks[5], (DT_RANK, HALF), jnp.float32, -dt_init_std, dt_init_std)
        dt = jnp.exp(jax.random.uniform(ks[6], (HALF,)) * (math.log(0.1) - math.log(0.001)) + math.log(0.001))
        dt = jnp.clip(dt, 0.0001)
        b_dt = dt + jnp.log(-jnp.expm1(-dt))
        A_log = jnp.log(jnp.tile(jnp.arange(1, D_STATE + 1, dtype=jnp.float32), (HALF, 1)))
        D = jnp.ones((HALF,), jnp.float32)
        W_out = jax.random.normal(ks[7], (D_INNER, D_MODEL), jnp.float32) / np.sqrt(D_INNER)
        b_out = jnp.zeros((D_MODEL,), jnp.float32)
        return {'x': x, 'W_in': W_in, 'conv_x_k': conv_x_k, 'conv_z_k': conv_z_k, 'W_xproj': W_xproj, 'W_dt': W_dt, 'b_dt': b_dt, 'A_log': A_log, 'D': D, 'W_out': W_out, 'b_out': b_out}
    _L3_attn_in = _L3_attn_setup()

    def _L3_ffn_setup():
        import jax, jax.numpy as jnp
        import numpy as np
        BLOCK = 16
        _GRID = jnp.array([0.0, 0.5, 1.0, 1.5, 2.0, 3.0, 4.0, 6.0], dtype=jnp.float32)
        _MID = jnp.array([0.25, 0.75, 1.25, 1.75, 2.5, 3.5, 5.0], dtype=jnp.float32)

        def fp4_quant_dequant(x):
            shape = x.shape
            xb = x.reshape(shape[:-1] + (shape[-1] // BLOCK, BLOCK))
            scale = jnp.max(jnp.abs(xb), axis=-1, keepdims=True) / 6.0
            scale = jnp.maximum(scale, jnp.float32(1e-12))
            xn = xb / scale
            idx = jnp.searchsorted(_MID, jnp.abs(xn))
            q = _GRID[idx] * jnp.sign(xn) * scale
            return q.reshape(shape)

        def fp4_linear(x, w):
            xq = fp4_quant_dequant(x)
            wq = fp4_quant_dequant(w)
            return jnp.einsum('bsk,nk->bsn', xq, wq)
        key = jax.random.key(seed)
        k1, k2, k3, k4 = jax.random.split(key, 4)
        H, I = (128, 352)
        x = jax.random.normal(k1, (4, 512, H), dtype=jnp.float32)
        w_gate = jax.random.normal(k2, (I, H), dtype=jnp.float32) * 0.02
        w_up = jax.random.normal(k3, (I, H), dtype=jnp.float32) * 0.02
        w_down = jax.random.normal(k4, (H, I), dtype=jnp.float32) * 0.02
        return {'x': x, 'w_gate': w_gate, 'w_up': w_up, 'w_down': w_down}
    _L3_ffn_in = _L3_ffn_setup()
    _d = {'L0_attn_x': _L0_attn_in['x'], 'L0_attn_norm_w': _L0_attn_in['norm_w'], 'L0_attn_norm_b': _L0_attn_in['norm_b'], 'L0_attn_in_proj_w': _L0_attn_in['in_proj_w'], 'L0_attn_conv_w': _L0_attn_in['conv_w'], 'L0_attn_conv_b': _L0_attn_in['conv_b'], 'L0_attn_x_proj_w': _L0_attn_in['x_proj_w'], 'L0_attn_dt_w': _L0_attn_in['dt_w'], 'L0_attn_dt_b': _L0_attn_in['dt_b'], 'L0_attn_out_proj_w': _L0_attn_in['out_proj_w'], 'L0_ffn_gate_w': _L0_ffn_in['gate_w'], 'L0_ffn_w1': _L0_ffn_in['w1'], 'L0_ffn_b1': _L0_ffn_in['b1'], 'L0_ffn_ln1_g': _L0_ffn_in['ln1_g'], 'L0_ffn_ln1_b': _L0_ffn_in['ln1_b'], 'L0_ffn_w2': _L0_ffn_in['w2'], 'L0_ffn_b2': _L0_ffn_in['b2'], 'L0_ffn_ln_g': _L0_ffn_in['ln_g'], 'L0_ffn_ln_b': _L0_ffn_in['ln_b'], 'L1_attn_norm_w': _L1_attn_in['norm_w'], 'L1_attn_in_proj_w': _L1_attn_in['in_proj_w'], 'L1_attn_conv_w': _L1_attn_in['conv_w'], 'L1_attn_dt_w': _L1_attn_in['dt_w'], 'L1_attn_dt_b': _L1_attn_in['dt_b'], 'L1_attn_A_log': _L1_attn_in['A_log'], 'L1_attn_B_w': _L1_attn_in['B_w'], 'L1_attn_C_w': _L1_attn_in['C_w'], 'L1_attn_D_skip': _L1_attn_in['D_skip'], 'L1_attn_out_proj_w': _L1_attn_in['out_proj_w'], 'L1_ffn_W1': _L1_ffn_in['W1'], 'L1_ffn_b1': _L1_ffn_in['b1'], 'L1_ffn_W2': _L1_ffn_in['W2'], 'L1_ffn_b2': _L1_ffn_in['b2'], 'L1_ffn_gate_W': _L1_ffn_in['gate_W'], 'L1_ffn_shared_W': _L1_ffn_in['shared_W'], 'L1_ffn_shared_b': _L1_ffn_in['shared_b'], 'L1_ffn_gamma': _L1_ffn_in['gamma'], 'L1_ffn_beta': _L1_ffn_in['beta'], 'L2_attn_Wq': _L2_attn_in['Wq'], 'L2_attn_bq': _L2_attn_in['bq'], 'L2_attn_Wk': _L2_attn_in['Wk'], 'L2_attn_bk': _L2_attn_in['bk'], 'L2_attn_Wv': _L2_attn_in['Wv'], 'L2_attn_bv': _L2_attn_in['bv'], 'L2_attn_Wo': _L2_attn_in['Wo'], 'L2_attn_bo': _L2_attn_in['bo'], 'L2_attn_gamma': _L2_attn_in['gamma'], 'L2_attn_beta': _L2_attn_in['beta'], 'L2_attn_lam': _L2_attn_in['lam'], 'L2_ffn_router_w': _L2_ffn_in['router_w'], 'L2_ffn_gate_w': _L2_ffn_in['gate_w'], 'L2_ffn_up_w': _L2_ffn_in['up_w'], 'L2_ffn_down_w': _L2_ffn_in['down_w'], 'L2_ffn_shared_gate_w': _L2_ffn_in['shared_gate_w'], 'L2_ffn_shared_up_w': _L2_ffn_in['shared_up_w'], 'L2_ffn_shared_down_w': _L2_ffn_in['shared_down_w'], 'L3_attn_W_in': _L3_attn_in['W_in'], 'L3_attn_conv_x_k': _L3_attn_in['conv_x_k'], 'L3_attn_conv_z_k': _L3_attn_in['conv_z_k'], 'L3_attn_W_xproj': _L3_attn_in['W_xproj'], 'L3_attn_W_dt': _L3_attn_in['W_dt'], 'L3_attn_b_dt': _L3_attn_in['b_dt'], 'L3_attn_A_log': _L3_attn_in['A_log'], 'L3_attn_D': _L3_attn_in['D'], 'L3_attn_W_out': _L3_attn_in['W_out'], 'L3_attn_b_out': _L3_attn_in['b_out'], 'L3_ffn_w_gate': _L3_ffn_in['w_gate'], 'L3_ffn_w_up': _L3_ffn_in['w_up'], 'L3_ffn_w_down': _L3_ffn_in['w_down']}
    _x0 = _d['L0_attn_x']
    _d['L0_attn_x'] = jax.random.normal(jax.random.fold_in(jax.random.key(seed), 1), (2, 1024, 128), dtype=_x0.dtype)
    del _x0
    return _d

def reference(L0_attn_x, L0_attn_norm_w, L0_attn_norm_b, L0_attn_in_proj_w, L0_attn_conv_w, L0_attn_conv_b, L0_attn_x_proj_w, L0_attn_dt_w, L0_attn_dt_b, L0_attn_out_proj_w, L0_ffn_gate_w, L0_ffn_w1, L0_ffn_b1, L0_ffn_ln1_g, L0_ffn_ln1_b, L0_ffn_w2, L0_ffn_b2, L0_ffn_ln_g, L0_ffn_ln_b, L1_attn_norm_w, L1_attn_in_proj_w, L1_attn_conv_w, L1_attn_dt_w, L1_attn_dt_b, L1_attn_A_log, L1_attn_B_w, L1_attn_C_w, L1_attn_D_skip, L1_attn_out_proj_w, L1_ffn_W1, L1_ffn_b1, L1_ffn_W2, L1_ffn_b2, L1_ffn_gate_W, L1_ffn_shared_W, L1_ffn_shared_b, L1_ffn_gamma, L1_ffn_beta, L2_attn_Wq, L2_attn_bq, L2_attn_Wk, L2_attn_bk, L2_attn_Wv, L2_attn_bv, L2_attn_Wo, L2_attn_bo, L2_attn_gamma, L2_attn_beta, L2_attn_lam, L2_ffn_router_w, L2_ffn_gate_w, L2_ffn_up_w, L2_ffn_down_w, L2_ffn_shared_gate_w, L2_ffn_shared_up_w, L2_ffn_shared_down_w, L3_attn_W_in, L3_attn_conv_x_k, L3_attn_conv_z_k, L3_attn_W_xproj, L3_attn_W_dt, L3_attn_b_dt, L3_attn_A_log, L3_attn_D, L3_attn_W_out, L3_attn_b_out, L3_ffn_w_gate, L3_ffn_w_up, L3_ffn_w_down):

    def _L0_attn_ref(x, norm_w, norm_b, in_proj_w, conv_w, conv_b, x_proj_w, dt_w, dt_b, out_proj_w):
        import jax, jax.numpy as jnp
        import numpy as np
        D_MODEL = 128
        D_STATE = 16
        D_CONV = 4
        D_INNER = 2 * D_MODEL
        BATCH = 2
        SEQ = 256
        LN_EPS = 1e-05

        def _layernorm(x, w, b):
            mu = jnp.mean(x, axis=-1, keepdims=True)
            var = jnp.mean(jnp.square(x - mu), axis=-1, keepdims=True)
            return (x - mu) * jax.lax.rsqrt(var + LN_EPS) * w + b

        def _forward(x, norm_w, norm_b, in_proj_w, conv_w, conv_b, x_proj_w, dt_w, dt_b, out_proj_w):
            residual = x
            xn = _layernorm(x, norm_w, norm_b)
            xz = xn @ in_proj_w.T
            x_in, z = jnp.split(xz, 2, axis=-1)
            x_conv = jax.lax.conv_general_dilated(jnp.swapaxes(x_in, 1, 2), conv_w, window_strides=(1,), padding=[(D_CONV - 1, 0)], dimension_numbers=('NCH', 'OIH', 'NCH'))
            x_conv = jnp.swapaxes(x_conv, 1, 2) + conv_b
            x_act = jax.nn.silu(x_conv)
            x_ssm = x_act @ x_proj_w.T
            delta_s = x_ssm[..., :1]
            B_mat = x_ssm[..., 1:1 + D_STATE].astype(jnp.float32)
            C = x_ssm[..., 1 + D_STATE:].astype(jnp.float32)
            delta = jax.nn.softplus(delta_s @ dt_w.T + dt_b).astype(jnp.float32)
            x_f32 = x_act.astype(jnp.float32)

            def step(h, inputs):
                d_t, b_t, c_t, u_t = inputs
                h = h * jnp.exp(-d_t)[..., None] + b_t[:, None, :] * u_t[..., None]
                y_t = jnp.einsum('bds,bs->bd', h, c_t)
                return (h, y_t)
            h0 = jnp.zeros((x.shape[0], D_INNER, D_STATE), jnp.float32)
            xs = (jnp.moveaxis(delta, 1, 0), jnp.moveaxis(B_mat, 1, 0), jnp.moveaxis(C, 1, 0), jnp.moveaxis(x_f32, 1, 0))
            _, y = jax.lax.scan(step, h0, xs)
            y = jnp.moveaxis(y, 0, 1).astype(x.dtype)
            return y * jax.nn.silu(z) @ out_proj_w.T + residual
        return _forward(x, norm_w, norm_b, in_proj_w, conv_w, conv_b, x_proj_w, dt_w, dt_b, out_proj_w)

    def _L0_ffn_ref(x, gate_w, w1, b1, ln1_g, ln1_b, w2, b2, ln_g, ln_b):
        import jax, jax.numpy as jnp
        import numpy as np
        DIM = 128
        E = 8
        K = 2
        EPS = 1e-05

        def _ln(x, g, b):
            mu = jnp.mean(x, axis=-1, keepdims=True)
            var = jnp.mean(jnp.square(x - mu), axis=-1, keepdims=True)
            return (x - mu) * jax.lax.rsqrt(var + EPS) * g + b
        shape = x.shape
        xf = x.reshape(-1, shape[-1])
        gates = jax.nn.softmax(xf @ gate_w, axis=-1)
        topw, topi = jax.lax.top_k(gates, K)
        topw = topw / jnp.sum(topw, axis=-1, keepdims=True)
        combine = jnp.sum(topw[:, :, None] * jax.nn.one_hot(topi, E, dtype=xf.dtype), axis=1)
        h = jnp.einsum('td,edh->teh', xf, w1) + b1
        h = _ln(h, ln1_g, ln1_b)
        h = jax.nn.gelu(h, approximate=False)
        y = jnp.einsum('teh,ehd->ted', h, w2) + b2
        out = jnp.einsum('ted,te->td', y, combine)
        out = _ln(out + xf, ln_g, ln_b)
        return out.reshape(shape)

    def _L1_attn_ref(x, norm_w, in_proj_w, conv_w, dt_w, dt_b, A_log, B_w, C_w, D_skip, out_proj_w):
        import jax, jax.numpy as jnp
        import numpy as np
        D_MODEL, D_STATE, D_CONV, EXPAND = (128, 16, 4, 2)
        D_INNER = EXPAND * D_MODEL
        EPS = 1e-06

        def _forward(x, norm_w, in_proj_w, conv_w, dt_w, dt_b, A_log, B_w, C_w, D_skip, out_proj_w):
            Bsz, T, _ = x.shape
            xn = x * jax.lax.rsqrt(jnp.mean(x * x, axis=-1, keepdims=True) + EPS) * norm_w
            xg = xn @ in_proj_w
            x_inner, gate = jnp.split(xg, 2, axis=-1)
            x_inner = x_inner * jax.nn.silu(gate)
            xc = jax.lax.conv_general_dilated(x_inner.transpose(0, 2, 1), conv_w, window_strides=(1,), padding=[(D_CONV - 1, 0)], feature_group_count=D_INNER, dimension_numbers=('NCH', 'OIH', 'NCH')).transpose(0, 2, 1)
            dt = jax.nn.softplus(xc @ dt_w + dt_b)
            A = -jnp.exp(A_log)
            Bm = xc @ B_w
            Cm = xc @ C_w
            A_bar = jnp.exp(dt[..., None] * A)
            B_bar = dt[..., None] * Bm[:, :, None, :]

            def step(h, inp):
                a_t, b_t, xc_t, c_t = inp
                h = a_t * h + b_t * xc_t[..., None]
                y = jnp.einsum('bds,bs->bd', h, c_t) + D_skip * xc_t
                return (h, y)
            h0 = jnp.zeros((Bsz, D_INNER, D_STATE), x.dtype)
            xs = (A_bar.transpose(1, 0, 2, 3), B_bar.transpose(1, 0, 2, 3), xc.transpose(1, 0, 2), Cm.transpose(1, 0, 2))
            _, ys = jax.lax.scan(step, h0, xs)
            out = ys.transpose(1, 0, 2) @ out_proj_w
            return out
        return _forward(x, norm_w, in_proj_w, conv_w, dt_w, dt_b, A_log, B_w, C_w, D_skip, out_proj_w)

    def _L1_ffn_ref(x, W1, b1, W2, b2, gate_W, shared_W, shared_b, gamma, beta):
        import jax, jax.numpy as jnp
        import numpy as np
        B, S, D, E, H, DO = (4, 256, 128, 8, 512, 128)
        TOP_K = 2
        LN_EPS = 1e-05
        d = x.shape[-1]
        flat = x.reshape(-1, d)
        n_exp = gate_W.shape[-1]
        probs = jax.nn.softmax(flat @ gate_W, axis=-1)
        topk_w, topk_idx = jax.lax.top_k(probs, TOP_K)
        topk_w = topk_w / topk_w.sum(axis=-1, keepdims=True)
        combine = (jax.nn.one_hot(topk_idx, n_exp, dtype=flat.dtype) * topk_w[..., None]).sum(axis=1)
        out = 0.5 * jax.nn.gelu(flat @ shared_W + shared_b, approximate=False)
        for e in range(n_exp):
            h = jax.nn.gelu(flat @ W1[e] + b1[e], approximate=False)
            out = out + combine[:, e:e + 1] * (h @ W2[e] + b2[e])
        mean = out.mean(axis=-1, keepdims=True)
        var = ((out - mean) ** 2).mean(axis=-1, keepdims=True)
        out = (out - mean) * jax.lax.rsqrt(var + LN_EPS) * gamma + beta
        return out.reshape(*x.shape[:-1], out.shape[-1])

    def _L2_attn_ref(X, Wq, bq, Wk, bk, Wv, bv, Wo, bo, gamma, beta, lam):
        import jax, jax.numpy as jnp
        import numpy as np
        B, S, E, H, D = (1, 256, 128, 16, 64)
        LAM_INIT = 0.8
        LN_EPS = 1e-05
        Q = jnp.einsum('bse,hec->bhsc', X, Wq) + bq[None, :, None, :]
        K = jnp.einsum('bse,hec->bhsc', X, Wk) + bk[None, :, None, :]
        V = jnp.einsum('bse,hed->bhsd', X, Wv) + bv[None, :, None, :]
        d = Wv.shape[-1]
        Q1, Q2 = (Q[..., :d], Q[..., d:])
        K1, K2 = (K[..., :d], K[..., d:])
        s = 1.0 / jnp.sqrt(jnp.float32(d))
        A1 = jnp.einsum('bhqd,bhkd->bhqk', Q1, K1) * s
        A2 = jnp.einsum('bhqd,bhkd->bhqk', Q2, K2) * s
        P = jax.nn.softmax(A1, axis=-1) - lam * jax.nn.softmax(A2, axis=-1)
        O = jnp.einsum('bhqk,bhkd->bhqd', P, V)
        Ocat = jnp.transpose(O, (0, 2, 1, 3)).reshape(O.shape[0], O.shape[2], -1)
        Y = Ocat @ Wo + bo
        mu = jnp.mean(Y, axis=-1, keepdims=True)
        var = jnp.var(Y, axis=-1, keepdims=True)
        Yn = (Y - mu) * jax.lax.rsqrt(var + LN_EPS) * gamma + beta
        return Yn * (1.0 - LAM_INIT)

    def _L2_ffn_ref(x, router_w, gate_w, up_w, down_w, shared_gate_w, shared_up_w, shared_down_w):
        import jax, jax.numpy as jnp
        import numpy as np
        B, S, H = (2, 64, 128)
        E, I = (64, 64)
        K = 8
        G, TG = (8, 4)
        SCALE = 2.5
        T = B * S
        CAP = 64

        def _moe_forward(x, router_w, gate_w, up_w, down_w, shared_gate_w, shared_up_w, shared_down_w):
            b, s, h = x.shape
            tokens = x.reshape(-1, h)
            t = tokens.shape[0]
            logits = tokens @ router_w
            scores = jax.nn.sigmoid(logits)
            eg = E // G
            group_scores = scores.reshape(t, G, eg).max(axis=-1)
            _, sel_groups = jax.lax.top_k(group_scores, TG)
            group_mask = jnp.zeros((t, G), bool).at[jnp.arange(t)[:, None], sel_groups].set(True)
            expert_mask = jnp.repeat(group_mask, eg, axis=1)
            masked_scores = jnp.where(expert_mask, scores, 0.0)
            topk_w, topk_idx = jax.lax.top_k(masked_scores, K)
            topk_w = topk_w / jnp.clip(topk_w.sum(-1, keepdims=True), 1e-09)
            topk_w = topk_w * SCALE
            flat_e = topk_idx.reshape(-1)
            onehot = jax.nn.one_hot(flat_e, E, dtype=jnp.int32)
            prior = jnp.cumsum(onehot, axis=0) - onehot
            pos = jnp.take_along_axis(prior, flat_e[:, None], axis=1)[:, 0]
            valid = (pos < CAP).astype(tokens.dtype)
            pos_c = jnp.minimum(pos, CAP - 1)
            tidx = jnp.repeat(jnp.arange(t), K)
            dispatch = jnp.zeros((E, CAP, h), tokens.dtype)
            dispatch = dispatch.at[flat_e, pos_c].add(tokens[tidx] * valid[:, None])
            g = jnp.einsum('ech,ehi->eci', dispatch, gate_w)
            u = jnp.einsum('ech,ehi->eci', dispatch, up_w)
            expert_out = jnp.einsum('eci,eih->ech', jax.nn.silu(g) * u, down_w)
            gathered = expert_out[flat_e, pos_c]
            contrib = gathered * (topk_w.reshape(-1) * valid)[:, None]
            output = jnp.zeros((t, h), tokens.dtype).at[tidx].add(contrib)
            sg = jax.nn.silu(tokens @ shared_gate_w) * (tokens @ shared_up_w)
            output = output + sg @ shared_down_w
            return output.reshape(b, s, h)
        return _moe_forward(x, router_w, gate_w, up_w, down_w, shared_gate_w, shared_up_w, shared_down_w)

    def _L3_attn_ref(x, W_in, conv_x_k, conv_z_k, W_xproj, W_dt, b_dt, A_log, D, W_out, b_out):
        import jax, jax.numpy as jnp
        import numpy as np
        import math
        D_MODEL, D_STATE, D_CONV, EXPAND = (128, 16, 4, 2)
        D_INNER = EXPAND * D_MODEL
        HALF = D_INNER // 2
        DT_RANK = math.ceil(D_MODEL / 16)
        BATCH, SEQLEN = (8, 256)

        def _depthwise_conv1d(x, k):
            return jax.lax.conv_general_dilated(x, k, window_strides=(1,), padding='SAME', feature_group_count=x.shape[-1], dimension_numbers=('NWC', 'WIO', 'NWC'))

        def _selective_scan(u, delta, A, B, C, D):
            b, l, d = u.shape
            n = A.shape[1]

            def step(h, t):
                u_t, dt_t, B_t, C_t = t
                dA = jnp.exp(dt_t[..., None] * A)
                h = dA * h + (dt_t * u_t)[..., None] * B_t[:, None, :]
                y = jnp.einsum('bdn,bn->bd', h, C_t)
                return (h, y)
            h0 = jnp.zeros((b, d, n), u.dtype)
            xs = (jnp.swapaxes(u, 0, 1), jnp.swapaxes(delta, 0, 1), jnp.swapaxes(B, 0, 1), jnp.swapaxes(C, 0, 1))
            _, ys = jax.lax.scan(step, h0, xs)
            return jnp.swapaxes(ys, 0, 1) + u * D
        xz = x @ W_in
        xh, z = jnp.split(xz, 2, axis=-1)
        A = -jnp.exp(A_log)
        xh = jax.nn.silu(_depthwise_conv1d(xh, conv_x_k))
        z = jax.nn.silu(_depthwise_conv1d(z, conv_z_k))
        x_dbl = xh @ W_xproj
        dt, Bm, Cm = jnp.split(x_dbl, [DT_RANK, DT_RANK + D_STATE], axis=-1)
        dt = dt @ W_dt + b_dt
        delta = jax.nn.softplus(dt + b_dt)
        y = _selective_scan(xh, delta, A, Bm, Cm, D)
        y = jnp.concatenate([y, z], axis=-1)
        return y @ W_out + b_out

    def _L3_ffn_ref(x, w_gate, w_up, w_down):
        import jax, jax.numpy as jnp
        import numpy as np
        BLOCK = 16
        _GRID = jnp.array([0.0, 0.5, 1.0, 1.5, 2.0, 3.0, 4.0, 6.0], dtype=jnp.float32)
        _MID = jnp.array([0.25, 0.75, 1.25, 1.75, 2.5, 3.5, 5.0], dtype=jnp.float32)

        def fp4_quant_dequant(x):
            shape = x.shape
            xb = x.reshape(shape[:-1] + (shape[-1] // BLOCK, BLOCK))
            scale = jnp.max(jnp.abs(xb), axis=-1, keepdims=True) / 6.0
            scale = jnp.maximum(scale, jnp.float32(1e-12))
            xn = xb / scale
            idx = jnp.searchsorted(_MID, jnp.abs(xn))
            q = _GRID[idx] * jnp.sign(xn) * scale
            return q.reshape(shape)

        def fp4_linear(x, w):
            xq = fp4_quant_dequant(x)
            wq = fp4_quant_dequant(w)
            return jnp.einsum('bsk,nk->bsn', xq, wq)
        gate = fp4_linear(x, w_gate)
        y = fp4_linear(x, w_up)
        h = jax.nn.silu(gate) * y
        return fp4_linear(h, w_down)
    x = L0_attn_x
    xn = _layernorm(x, axis=-1)
    x = x + _L0_attn_ref(xn, L0_attn_norm_w, L0_attn_norm_b, L0_attn_in_proj_w, L0_attn_conv_w, L0_attn_conv_b, L0_attn_x_proj_w, L0_attn_dt_w, L0_attn_dt_b, L0_attn_out_proj_w) + _L0_ffn_ref(xn, L0_ffn_gate_w, L0_ffn_w1, L0_ffn_b1, L0_ffn_ln1_g, L0_ffn_ln1_b, L0_ffn_w2, L0_ffn_b2, L0_ffn_ln_g, L0_ffn_ln_b)
    xn = _layernorm(x, axis=-1)
    x = x + _L1_attn_ref(xn, L1_attn_norm_w, L1_attn_in_proj_w, L1_attn_conv_w, L1_attn_dt_w, L1_attn_dt_b, L1_attn_A_log, L1_attn_B_w, L1_attn_C_w, L1_attn_D_skip, L1_attn_out_proj_w) + _L1_ffn_ref(xn, L1_ffn_W1, L1_ffn_b1, L1_ffn_W2, L1_ffn_b2, L1_ffn_gate_W, L1_ffn_shared_W, L1_ffn_shared_b, L1_ffn_gamma, L1_ffn_beta)
    xn = _layernorm(x, axis=-1)
    x = x + _L2_attn_ref(xn, L2_attn_Wq, L2_attn_bq, L2_attn_Wk, L2_attn_bk, L2_attn_Wv, L2_attn_bv, L2_attn_Wo, L2_attn_bo, L2_attn_gamma, L2_attn_beta, L2_attn_lam) + _L2_ffn_ref(xn, L2_ffn_router_w, L2_ffn_gate_w, L2_ffn_up_w, L2_ffn_down_w, L2_ffn_shared_gate_w, L2_ffn_shared_up_w, L2_ffn_shared_down_w)
    xn = _layernorm(x, axis=-1)
    x = x + _L3_attn_ref(xn, L3_attn_W_in, L3_attn_conv_x_k, L3_attn_conv_z_k, L3_attn_W_xproj, L3_attn_W_dt, L3_attn_b_dt, L3_attn_A_log, L3_attn_D, L3_attn_W_out, L3_attn_b_out) + _L3_ffn_ref(xn, L3_ffn_w_gate, L3_ffn_w_up, L3_ffn_w_down)
    return x

_drawn_inputs = setup_inputs


def setup_inputs(seed=0):
    import zlib

    import numpy as np

    out = dict(_drawn_inputs(seed))
    spreads = {'L0_attn_norm_w': (1.0, 0.2),
     'L0_attn_norm_b': (0.0, 0.1),
     'L0_ffn_ln1_g': (1.0, 0.2),
     'L0_ffn_ln1_b': (0.0, 0.1),
     'L0_ffn_ln_g': (1.0, 0.2),
     'L0_ffn_ln_b': (0.0, 0.1),
     'L1_attn_norm_w': (1.0, 0.2),
     'L1_attn_dt_b': (0.0, 0.295),
     'L1_attn_D_skip': (1.0, 0.2),
     'L1_ffn_b1': (0.0, 0.1),
     'L1_ffn_b2': (0.0, 0.1),
     'L1_ffn_shared_b': (0.0, 0.1),
     'L1_ffn_gamma': (1.0, 0.2),
     'L1_ffn_beta': (0.0, 0.1),
     'L2_attn_bq': (0.0, 0.8),
     'L2_attn_bk': (0.0, 2.0),
     'L2_attn_bv': (0.0, 0.448),
     'L2_attn_bo': (0.0, 0.8),
     'L2_attn_gamma': (1.0, 0.6),
     'L2_attn_beta': (0.0, 0.8),
     'L3_attn_D': (1.0, 0.6),
     'L3_attn_b_out': (0.0, 2.0)}
    factors = {'L2_attn_Wq': 8.0,
     'L2_attn_Wk': 8.0,
     'L2_attn_Wv': 8.0,
     'L2_attn_Wo': 3.296,
     'L3_attn_W_xproj': 8.0,
     'L3_attn_W_dt': 8.0,
     'L3_attn_b_dt': 8.0,
     'L3_attn_A_log': 8.0,
     'L3_ffn_w_gate': 8.0,
     'L3_ffn_w_up': 8.0,
     'L3_ffn_w_down': 8.0,
     'L3_attn_conv_z_k': 27.977}
    for name, (base, spread) in spreads.items():
        noise = np.random.default_rng([zlib.crc32(name.encode()), seed]).standard_normal(out[name].shape)
        drawn = base * np.exp(spread * noise) if base else spread * noise
        out[name] = jnp.asarray(drawn.astype(out[name].dtype))
    for name, factor in factors.items():
        out[name] = (out[name] * factor).astype(out[name].dtype)
    return out
```

```python
from contextlib import ExitStack

import concourse.bass as bass
from concourse import mybir

ALU = mybir.AluOpType
ACT = mybir.ActivationFunctionType
AX = mybir.AxisListType
F32 = mybir.dt.float32
BF16 = mybir.dt.bfloat16
I32 = mybir.dt.int32

P = 128
NB, SEQ = 2, 1024
T = NB * SEQ
CH = 512
NCH = T // CH
NT = T // P
NS = 16
DI = 2
NE = 8


def chunk(j):
    return slice(CH * j, CH * j + CH)


def tile(t):
    return slice(P * t, P * t + P)


class Kit:

    def __init__(self, nc, ctx, views):
        self.nc, self.ctx, self.views, self.norms = nc, ctx, views, 0
        self.counted = []
        self.x = self.sb(ctx, "x", [P, T])
        self.xn = self.sb(ctx, "xn", [P, T])
        self.t1 = self.sb(ctx, "t1", [P, T])
        self.t2 = self.sb(ctx, "t2", [P, T])
        self.t3 = self.sb(ctx, "t3", [P, T])
        self.ones = self.sb(ctx, "ones", [P, P])
        self.ident = self.sb(ctx, "ident", [P, P])
        self.eps5 = self.sb(ctx, "eps5", [P, 1])
        self.eps6 = self.sb(ctx, "eps6", [P, 1])
        self.sel = self.sb(ctx, "sel", [96, 2 * NS, P], BF16)
        self.ps = ctx.enter_context(nc.psum_tensor("ps", [P, 8, CH], F32))
        self.pad = self.sem(ctx, "loop_wait_carrier")
        self.ln = {n: self.sem(ctx, "ln_" + n) for n in ("mean", "centred", "squared", "var", "log", "rstd", "out")}

    def sb(self, ctx, name, shape, dt=F32):
        return ctx.enter_context(self.nc.sbuf_tensor(name, shape, dt))

    def sem(self, ctx, name):
        s = ctx.enter_context(self.nc.semaphore(name))
        if ctx is self.ctx:
            self.counted.append(s)
        return s

    def clear_counts(self):
        with self.nc.Block() as block:

            @block.gpsimd
            def _(pool):
                for s in self.counted:
                    pool.sem_clear(s)

    def sems(self, ctx, prefix, names):
        return [self.sem(self.ctx, prefix + n) for n in names.split()]

    def hold(self, eng, sem, count):
        eng.wait_ge(sem, count)
        eng.sem_inc(self.pad, 1)


def layer_norm(k, src, dst, eps, gain=None, bias=None, rms=False):
    base = 4 * k.norms
    k.norms += 1
    ln, ps = k.ln, k.ps
    cen = src if rms else k.t1
    with k.nc.Block() as block:

        @block.tensor
        def _(pe):
            for j in range(NCH):
                if not rms:
                    pe.matmul(ps[:, j, :], k.ones[:, :], src[:, chunk(j)], start=True, stop=True).then_inc(ln["mean"], 1)
            for j in range(NCH):
                pe.wait_ge(ln["squared"], base + j + 1)
                pe.matmul(ps[:, 4 + j, :], k.ones[:, :], k.t2[:, chunk(j)], start=True, stop=True).then_inc(ln["var"], 1)
            if rms:
                pe.sem_inc(ln["mean"], 4)

        @block.scalar
        def _(act):
            for j in range(NCH):
                if not rms:
                    act.wait_ge(ln["centred"], base + j + 1)
                act.activation(k.t2[:, chunk(j)], cen[:, chunk(j)], ACT.Square).then_inc(ln["squared"], 1)
            for j in range(NCH):
                act.wait_ge(ln["var"], base + j + 1)
                act.activation(k.t3[:, chunk(j)], ps[:, 4 + j, :], ACT.Ln, bias=eps[:, 0:1]).then_inc(ln["log"], 1)
                act.wait_ge(ln["log"], base + j + 1)
                act.activation(k.t3[:, chunk(j)], k.t3[:, chunk(j)], ACT.Exp, scale=-0.5).then_inc(ln["rstd"], 1)

        @block.vector
        def _(dve):
            for j in range(NCH):
                if not rms:
                    dve.wait_ge(ln["mean"], base + j + 1)
                    dve.tensor_tensor(k.t1[:, chunk(j)], src[:, chunk(j)], ps[:, j, :], ALU.subtract).then_inc(ln["centred"], 1)
            for j in range(NCH):
                dve.wait_ge(ln["rstd"], base + j + 1)
                if gain is None:
                    dve.tensor_tensor(dst[:, chunk(j)], cen[:, chunk(j)], k.t3[:, chunk(j)], ALU.mult).then_inc(ln["out"], 1)
                else:
                    dve.scalar_tensor_tensor(out=dst[:, chunk(j)], in0=cen[:, chunk(j)], scalar=gain,
                                             in1=k.t3[:, chunk(j)], op0=ALU.mult, op1=ALU.mult).then_inc(ln["out"], 1)
            if bias is not None:
                dve.wait_ge(ln["out"], base + 4)
                dve.tensor_scalar(dst[:, :], dst[:, :], bias, None, ALU.add)
            if rms:
                dve.sem_inc(ln["centred"], 4)


def load(k, ctx, name):
    src, places = k.views[name]
    w = k.sb(ctx, "w_" + name, [P, src.shape[1]])
    loaded = k.sem(k.ctx, "loaded_" + name)
    with k.nc.Block() as block:

        @block.sync
        def _(sp):
            sp.dma_start(w[:, :], src).then_inc(loaded, 16)
            sp.wait_ge(loaded, 16)

    k.w3 = w

    def get(n):
        a, shape = places[n]
        cols = 1
        for d in shape[1:]:
            cols *= d
        v = w[0:shape[0], a:a + cols]
        if len(shape) == 3:
            v = v.rearrange("p (a b) -> p a b", b=shape[2])
        if len(shape) == 4:
            v = v.rearrange("p (a b c) -> p a b c", b=shape[2], c=shape[3])
        return v

    return get


def split_rows(k, ctx, bc3, name):
    s = k.sem(k.ctx, "split_" + name)
    mid = k.t2[0:96, :].bitcast(BF16)[:, 0:T]
    rest = k.t1[0:96, :]
    rows = k.ps[0:96, 0:4, :].rearrange("p a b -> p (a b)")
    return s, mid, rest, rows


def split_steps(dve, k, s, mid, rest, rows, bc3):
    dve.tensor_copy(bc3[:, :], rows).then_inc(s, 1)
    dve.wait_ge(s, 1)
    dve.tensor_tensor(rest, rows, bc3[:, :], ALU.subtract).then_inc(s, 1)
    dve.wait_ge(s, 2)
    dve.tensor_copy(mid, rest).then_inc(s, 1)
    dve.wait_ge(s, 3)
    dve.tensor_tensor(rest, rest, mid, ALU.subtract).then_inc(s, 1)
    dve.tensor_copy(bc3[32:64, :], mid[32:64, :])
    dve.wait_ge(s, 4)
    dve.tensor_copy(bc3[64:96, :], rest[64:96, :])


def softplus_steps(dve, k, dt, low, up, upped, soft, n, summed, m):
    dve.tensor_scalar(up[:, :], low[:, :], 1.0, None, ALU.add).then_inc(upped, 1)
    dve.wait_ge(upped, 2 * m + 1)
    dve.scalar_tensor_tensor(out=low[:, :], in0=up[:, :], scalar=-1.0, in1=low[:, :], op0=ALU.add,
                             op1=ALU.subtract).then_inc(upped, 1)
    dve.wait_ge(upped, 2 * m + 2)
    dve.wait_ge(soft, n)
    dve.scalar_tensor_tensor(out=k.t3[:, :], in0=up[:, :], scalar=1.0, in1=k.t3[:, :], op0=ALU.is_gt,
                             op1=ALU.mult).then_inc(summed, 1)
    dve.wait_ge(summed, 3 * m + 1)
    dve.tensor_tensor(low[:, :], k.t3[:, :], low[:, :], ALU.subtract).then_inc(summed, 1)
    dve.wait_ge(summed, 3 * m + 2)
    dve.tensor_tensor(dt, dt, low[:, :], ALU.add).then_inc(summed, 1)
    dve.wait_ge(summed, 3 * m + 3)


def scan_loop(k, ctx, name, halves, u, bc3, finish, decay=None, dt=None, rate=None):
    nc, ps = k.nc, k.ps
    w = k.sb(ctx, name + "_w", [P, 2, halves, SEQ])
    h = k.sb(ctx, name + "_h", [P, 2, halves, SEQ])
    hc = k.sb(ctx, name + "_hc", [P, 2, halves, SEQ])
    cs = k.sb(ctx, name + "_c", [P, 2, SEQ])
    a = k.sb(ctx, name + "_a", [P, 2, halves, SEQ]) if dt is not None else None
    b_ready, c_ready, w_done, scanned, cs_done, hc_done, summed, y_out, a_done = k.sems(
        ctx, name + "_", "b_ready c_ready w_done scanned cs_done hc_done summed y_out a_done")
    H = halves
    bank_b, bank_c, bank_y = 0, 2, 4

    def spread(bank):
        return ps[:, bank:bank + 2, :].rearrange("p a b -> p (a b)")

    with nc.Block() as block:

        @block.tensor
        def _(pe):
            pe.sem_inc(summed, 2 * H)

            def add_state(b, s):
                for hf in range(H):
                    k.hold(pe, hc_done, (b * NS + s) * H + hf + 1 + 2 * H)
                    if s == 0 and hf == 0:
                        k.hold(pe, y_out, b * H + 1)
                    for q in range(2):
                        mm = pe.matmul(ps[:, bank_y + 2 * hf + q, :], k.ident[:, :], hc[:, s % 2, hf, chunk(q)],
                                       start=(s == 0), stop=(s == NS - 1))
                    mm.then_inc(summed, 1)

            with pe.Fori(0, NB) as b:
                for s in range(NS + 1):
                    if s < NS:
                        g = b * NS + s
                        k.hold(pe, w_done, g * H + H)
                        for q in range(2):
                            mm = pe.matmul(ps[:, bank_b + q, :], k.sel[:, s, :], bc3[:, bass.ds(b * SEQ + CH * q, CH)],
                                           start=True, stop=True)
                        mm.then_inc(b_ready, 1)
                        k.hold(pe, cs_done, g + 1)
                        for q in range(2):
                            mm = pe.matmul(ps[:, bank_c + q, :], k.sel[:, NS + s, :],
                                           bc3[:, bass.ds(b * SEQ + CH * q, CH)], start=True, stop=True)
                        mm.then_inc(c_ready, 1)
                    if s >= 1:
                        add_state(b, s - 1)

        @block.scalar
        def _(act):
            act.sem_inc(cs_done, 1)
            with act.Fori(0, NB) as b:
                for s in range(NS):
                    g = b * NS + s
                    if dt is not None:
                        for hf in range(H):
                            k.hold(act, w_done, (g * H + hf) + 1)
                            k.hold(act, hc_done, g * H + hf + 1)
                            act.activation(a[:, s % 2, hf, :], dt[:, hf, bass.ds(b * SEQ, SEQ)], ACT.Exp,
                                           scale=rate[:, hf, s:s + 1]).then_inc(a_done, 1)
                    k.hold(act, c_ready, g + 1)
                    k.hold(act, hc_done, g * H + H)
                    act.activation(cs[:, s % 2, :], spread(bank_c), ACT.Copy).then_inc(cs_done, 1)

        @block.vector
        def _(dve):
            dve.sem_inc(w_done, H)
            dve.sem_inc(y_out, 1)
            with dve.Fori(0, NB) as b:
                for s in range(NS):
                    g = b * NS + s
                    k.hold(dve, b_ready, g + 1)
                    for hf in range(H):
                        dve.tensor_tensor(w[:, s % 2, hf, :], u[:, hf, bass.ds(b * SEQ, SEQ)], spread(bank_b),
                                          ALU.mult).then_inc(w_done, 1)
                    for hf in range(H):
                        k.hold(dve, w_done, g * H + hf + 1 + H)
                        if dt is not None:
                            k.hold(dve, a_done, g * H + hf + 1)
                        k.hold(dve, hc_done, g * H + hf + 1)
                        d0 = a[:, s % 2, hf, :] if dt is not None else decay[:, hf, bass.ds(b * SEQ, SEQ)]
                        dve.tensor_tensor_scan(h[:, s % 2, hf, :], d0, w[:, s % 2, hf, :], 0.0, ALU.mult,
                                               ALU.add).then_inc(scanned, 1)
                k.hold(dve, summed, (b + 1) * NS * H + 2 * H)
                for hf in range(H):
                    finish(dve, b, hf, spread(bank_y + 2 * hf)).then_inc(y_out, 1)

        @block.gpsimd
        def _(pool):
            pool.sem_inc(hc_done, 2 * H)
            with pool.Fori(0, NB) as b:
                for s in range(NS):
                    g = b * NS + s
                    k.hold(pool, cs_done, g + 2)
                    for hf in range(H):
                        k.hold(pool, scanned, g * H + hf + 1)
                        k.hold(pool, summed, g * H + hf + 1)
                        pool.tensor_tensor(hc[:, s % 2, hf, :], h[:, s % 2, hf, :], cs[:, s % 2, :],
                                           ALU.mult).then_inc(hc_done, 1)


def route_top2(k, ctx, name, gate, comb_t):
    nc, ps = k.nc, k.ps
    logits = ps[:, 0, 0:NT * NE].rearrange("p (t e) -> p t e", e=NE)
    top = k.sb(ctx, name + "_top", [P, NT, 8])
    shifted = k.sb(ctx, name + "_shifted", [P, NT, NE])
    mask = k.sb(ctx, name + "_mask", [P, NT, NE])
    ex = k.sb(ctx, name + "_ex", [P, NT, NE])
    total = k.sb(ctx, name + "_total", [P, NT])
    logit, topped, shift, masked, expd, kept, summed, inv, comb, turned = k.sems(
        ctx, name + "_", "logit topped shift masked expd kept summed inv comb turned")
    with nc.Block() as block:

        @block.tensor
        def _(pe):
            for t in range(NT):
                mm = pe.matmul(logits[:, t, :], k.xn[:, tile(t)], gate, start=True, stop=True)
            mm.then_inc(logit, 1)
            pe.wait_ge(comb, 1)
            for t in range(NT):
                mm = pe.transpose(ps[0:NE, 1 + t // 4, P * (t % 4):P * (t % 4) + P], mask[:, t, :], k.ident[:, :])
            mm.then_inc(turned, 1)

        @block.vector
        def _(dve):
            dve.wait_ge(logit, 1)
            for t in range(NT):
                dve.max(top[:, t, :], logits[:, t, :]).then_inc(topped, 1)
            dve.wait_ge(topped, NT)
            dve.tensor_tensor(shifted[:, :, :], logits, top[:, :, 0:1].to_broadcast([P, NT, NE]), ALU.subtract).then_inc(shift, 1)
            dve.tensor_tensor(mask[:, :, :], logits, top[:, :, 1:2].to_broadcast([P, NT, NE]), ALU.is_ge).then_inc(masked, 1)
            dve.wait_ge(expd, 1)
            dve.wait_ge(masked, 1)
            dve.tensor_tensor(ex[:, :, :], ex[:, :, :], mask[:, :, :], ALU.mult).then_inc(kept, 1)
            dve.wait_ge(kept, 1)
            dve.tensor_reduce(total[:, :], ex[:, :, :], AX.X, ALU.add).then_inc(summed, 1)
            dve.wait_ge(summed, 1)
            dve.reciprocal(total[:, :], total[:, :]).then_inc(inv, 1)
            dve.wait_ge(inv, 1)
            dve.tensor_tensor(mask[:, :, :], ex[:, :, :], total[:, :].unsqueeze(2).to_broadcast([P, NT, NE]),
                              ALU.mult).then_inc(comb, 1)

        @block.scalar
        def _(act):
            act.wait_ge(shift, 1)
            act.activation(ex[:, :, :], shifted[:, :, :], ACT.Exp).then_inc(expd, 1)
            act.wait_ge(turned, 1)
            act.activation(comb_t[:, :], ps[0:NE, 1:5, :].rearrange("p a b -> p (a b)"), ACT.Copy)


def project_out(k, ctx, name, weight, src, extra=None):
    ready, added = k.sems(ctx, name + "_", "ready added")
    with k.nc.Block() as block:

        @block.tensor
        def _(pe):
            for j in range(NCH):
                for hf in range(DI):
                    mm = pe.matmul(k.ps[:, j, :], weight[:, hf, :], src[:, hf, chunk(j)], start=(hf == 0), stop=(hf == DI - 1))
                mm.then_inc(ready, 1)

        @block.vector
        def _(dve):
            for j in range(NCH):
                dve.wait_ge(ready, j + 1)
                dve.tensor_tensor(k.x[:, chunk(j)], k.x[:, chunk(j)], k.ps[:, j, :], ALU.add).then_inc(added, 1)
            if extra is not None:
                dve.wait_ge(added, NCH)
                dve.tensor_tensor(k.x[:, :], k.x[:, :], extra[:, :], ALU.add)


def layer0_attn(k, W):
    nc, ps = k.nc, k.ps
    with ExitStack() as ctx:
        w = {n: W(n) for n in ("a0_norm_w", "a0_norm_b", "a0_in", "a0_conv", "a0_conv_b", "a0_bc", "a0_ds", "a0_dt_w",
                               "a0_dt_b", "a0_out")}
        xn2 = k.t2
        u = k.sb(ctx, "a0_u", [P, DI, T])
        decay = k.sb(ctx, "a0_decay", [P, DI, T])
        sz = k.sb(ctx, "a0_sz", [P, DI, T])
        bc3 = k.sb(ctx, "a0_bc3", [96, T], BF16)
        layer_norm(k, k.xn, xn2, k.eps5, w["a0_norm_w"][:, 0:1], w["a0_norm_b"][:, 0:1])
        with ExitStack() as sub:
            padded = k.sb(sub, "a0_padded", [P, DI, NB, SEQ + 3])
            proj, x_out, z_out = k.sems(ctx, "a0_", "proj x_out z_out")
            with nc.Block() as block:

                @block.tensor
                def _(pe):
                    for m in range(4):
                        for j in range(NCH):
                            n = 4 * m + j
                            if n >= 8:
                                pe.wait_ge(x_out, n - 7)
                            pe.matmul(ps[:, n % 8, :], w["a0_in"][:, tile(m)], xn2[:, chunk(j)], start=True,
                                      stop=True).then_inc(proj, 1)

                @block.vector
                def _(dve):
                    dve.memset(padded[:, :, :, 0:3], 0.0)
                    for n in range(8):
                        dve.wait_ge(proj, n + 1)
                        dve.tensor_copy(padded[:, n // 4, n % 4 // 2, 3 + CH * (n % 2):3 + CH * (n % 2) + CH],
                                        ps[:, n, :]).then_inc(x_out, 1)

                @block.scalar
                def _(act):
                    for n in range(8):
                        act.wait_ge(proj, n + 9)
                        act.activation(sz[:, n // 4, chunk(n % 4)], ps[:, n, :], ACT.Silu).then_inc(z_out, 1)

            conv, = k.sems(ctx, "a0_", "conv")
            with nc.Block() as block:

                @block.tensor
                def _(pe):
                    for m in range(DI):
                        for n in range(4):
                            for hf in range(DI):
                                for tap in range(4):
                                    lo = CH * (n % 2) + tap
                                    mm = pe.matmul(ps[:, 4 * m + n, :], w["a0_conv"][:, tap * DI + hf, tile(m)],
                                                   padded[:, hf, n // 2, lo:lo + CH],
                                                   start=(hf == 0 and tap == 0), stop=(hf == 1 and tap == 3))
                            mm.then_inc(conv, 1)

                @block.scalar
                def _(act):
                    for n in range(8):
                        act.wait_ge(conv, n + 1)
                        act.activation(u[:, n // 4, chunk(n % 4)], ps[:, n, :], ACT.Silu, bias=w["a0_conv_b"][:, n // 4:n // 4 + 1])
        rows, delta, neg = k.sems(ctx, "a0_", "rows delta neg")
        s, mid, rest, psrows = split_rows(k, ctx, bc3, "a0")
        nw = k.sb(ctx, "a0_negw", [P, DI])
        nb = k.sb(ctx, "a0_negb", [P, DI])
        with nc.Block() as block:

            @block.tensor
            def _(pe):
                for weight, bank, done, m in ((w["a0_bc"], 0, rows, 96), (w["a0_ds"], 4, delta, P)):
                    for j in range(NCH):
                        for hf in range(DI):
                            mm = pe.matmul(ps[0:m, bank + j, :], weight[:, hf, :], u[:, hf, chunk(j)], start=(hf == 0),
                                           stop=(hf == 1))
                        mm.then_inc(done, 1)

            @block.vector
            def _(dve):
                dve.tensor_scalar(nw[:, :], w["a0_dt_w"], -1.0, None, ALU.mult).then_inc(neg, 1)
                dve.tensor_scalar(nb[:, :], w["a0_dt_b"], -1.0, None, ALU.mult).then_inc(neg, 1)
                dve.wait_ge(rows, NCH)
                split_steps(dve, k, s, mid, rest, psrows, bc3)

            @block.scalar
            def _(act):
                act.wait_ge(neg, 2)
                act.wait_ge(delta, NCH)
                for hf in range(DI):
                    act.activation(decay[:, hf, :], ps[:, 4:8, :].rearrange("p a b -> p (a b)"), ACT.Sigmoid,
                                   scale=nw[:, hf:hf + 1], bias=nb[:, hf:hf + 1])
        with ExitStack() as sub:
            def finish(dve, b, hf, y):
                return dve.tensor_tensor(sz[:, hf, bass.ds(b * SEQ, SEQ)], sz[:, hf, bass.ds(b * SEQ, SEQ)], y, ALU.mult)

            scan_loop(k, sub, "a0s", DI, u, bc3, finish, decay=decay)
        project_out(k, ctx, "a0p", w["a0_out"], sz, extra=k.xn)


def layer0_ffn(k, W):
    nc, ps = k.nc, k.ps
    HID = 2
    with ExitStack() as ctx:
        w = {n: W(n) for n in ("f0_gate", "f0_w1", "f0_b1", "f0_g", "f0_b", "f0_w2", "f0_b2", "f0_ln_g", "f0_ln_b", "f0_sel")}
        comb_t = k.sb(ctx, "f0_comb_t", [NE, T])
        acc = k.sb(ctx, "f0_acc", [P, T])
        w1c = k.sb(ctx, "f0_w1c", [P, NE, HID * P])
        b1c = k.sb(ctx, "f0_b1c", [P, NE, HID])
        mean = k.sb(ctx, "f0_mean", [P, NE])
        mean2 = k.sb(ctx, "f0_mean2", [P, NE])
        route_top2(k, ctx, "f0r", w["f0_gate"], comb_t)
        wm, wh, wc, bm, bh, acc0 = k.sems(ctx, "f0_", "w_mean w_half w_centred b_mean b_half acc_init")
        with nc.Block() as block:

            @block.tensor
            def _(pe):
                pe.matmul(ps[:, 0, 0:NE * HID], k.ones[:, :], w["f0_b1"].rearrange("p e m -> p (e m)"), start=True,
                          stop=True).then_inc(bm, 1)

            @block.vector
            def _(dve):
                dve.tensor_reduce(mean[:, :], w["f0_w1"], AX.X, ALU.add).then_inc(wm, 1)
                dve.wait_ge(wm, 1)
                dve.tensor_scalar(mean[:, :], mean[:, :], 1.0 / (HID * P), None, ALU.mult).then_inc(wh, 1)
                dve.wait_ge(wh, 1)
                dve.tensor_tensor(w1c[:, :, :], w["f0_w1"], mean[:, :].unsqueeze(2).to_broadcast([P, NE, HID * P]), ALU.subtract)
                dve.wait_ge(bm, 1)
                dve.tensor_reduce(mean2[:, :], ps[:, 0, 0:NE * HID].rearrange("p (e m) -> p e m", m=HID), AX.X, ALU.add).then_inc(bh, 1)
                dve.wait_ge(bh, 1)
                dve.tensor_scalar(mean2[:, :], mean2[:, :], 1.0 / HID, None, ALU.mult).then_inc(bh, 1)
                dve.wait_ge(bh, 2)
                dve.tensor_tensor(b1c[:, :, :], w["f0_b1"], mean2[:, :].unsqueeze(2).to_broadcast([P, NE, HID]), ALU.subtract)

            @block.gpsimd
            def _(pool):
                pool.tensor_copy(acc[:, :], k.xn[:, :])

        hn = k.sb(ctx, "f0_hn", [P, NE, HID, CH])
        sq = k.sb(ctx, "f0_sq", [P, 2, HID, CH])
        rs = k.sb(ctx, "f0_rs", [P, 2, CH])
        gl = k.sb(ctx, "f0_gl", [P, 2, HID, CH])
        yb = k.sb(ctx, "f0_yb", [P, 2, CH])
        tmp = k.sb(ctx, "f0_tmp", [P, 2, CH])
        h_done, sq_done, var_done, log_done, rs_done, hn_done, gl_done, y_done, cb_done, yb_done, tmp_done, acc_done = k.sems(
            ctx, "f0l_", "h sq var log rs hn gl y cb yb tmp acc")
        with nc.Block() as block:

            @block.tensor
            def _(pe):
                pe.sem_inc(var_done, 2)
                pe.sem_inc(y_done, 2)
                with pe.Fori(0, NCH) as i:
                    def hidden(e):
                        for m in range(HID):
                            k.hold(pe, hn_done, (i * NE + e) * HID + m + 1)
                            pe.matmul(ps[:, 2 * (e % 2) + m, :], w1c[:, e, tile(m)], k.xn[:, bass.ds(i * CH, CH)], start=True,
                                      stop=True).then_inc(h_done, 1)

                    def variance(e):
                        k.hold(pe, sq_done, (i * NE + e) * HID + HID)
                        k.hold(pe, log_done, i * NE + e + 1)
                        for m in range(HID):
                            mm = pe.matmul(ps[:, 4 + e % 2, :], k.ones[:, :], sq[:, e % 2, m, :], start=(m == 0), stop=(m == HID - 1))
                        mm.then_inc(var_done, 1)

                    for e in range(NE + 1):
                        if e < NE:
                            hidden(e)
                        if e >= 1:
                            variance(e - 1)
                    for e in range(NE):
                        g = i * NE + e
                        k.hold(pe, tmp_done, g + 1)
                        if e < 2:
                            k.hold(pe, log_done, i * NE + NE + 2)
                        pe.matmul(ps[:, 6 + e % 2, :], w["f0_sel"][:, e, :], comb_t[:, bass.ds(i * CH, CH)], start=True,
                                  stop=True).then_inc(cb_done, 1)
                        k.hold(pe, gl_done, g * HID + HID + NE * HID)
                        k.hold(pe, yb_done, g + 1)
                        for m in range(HID):
                            mm = pe.matmul(ps[:, 4 + e % 2, :], w["f0_w2"][:, e * HID + m, :], gl[:, e % 2, m, :], start=(m == 0),
                                           stop=(m == HID - 1))
                        mm.then_inc(y_done, 1)

            @block.scalar
            def _(act):
                act.sem_inc(log_done, 2)
                act.sem_inc(gl_done, NE * HID)
                act.sem_inc(yb_done, 2)
                with act.Fori(0, NCH) as i:
                    def squares(e):
                        for m in range(HID):
                            k.hold(act, h_done, (i * NE + e) * HID + m + 1)
                            k.hold(act, var_done, i * NE + e + 1)
                            act.activation(sq[:, e % 2, m, :], ps[:, 2 * (e % 2) + m, :], ACT.Square,
                                           bias=b1c[:, e, m:m + 1]).then_inc(sq_done, 1)

                    def rstd(e):
                        g = i * NE + e
                        k.hold(act, var_done, g + 3)
                        k.hold(act, hn_done, g * HID + HID)
                        act.activation(rs[:, e % 2, :], ps[:, 4 + e % 2, :], ACT.Ln, scale=1.0 / HID,
                                       bias=k.eps5[:, 0:1]).then_inc(log_done, 1)
                        k.hold(act, log_done, g + 3)
                        act.activation(rs[:, e % 2, :], rs[:, e % 2, :], ACT.Exp, scale=-0.5).then_inc(rs_done, 1)

                    for e in range(NE + 1):
                        if e < NE:
                            squares(e)
                        if e >= 1:
                            rstd(e - 1)

                    def add_b2(e):
                        g = i * NE + e
                        k.hold(act, y_done, g + 3)
                        k.hold(act, tmp_done, g + 1)
                        act.activation(yb[:, e % 2, :], ps[:, 4 + e % 2, :], ACT.Identity,
                                       bias=w["f0_b2"][:, e:e + 1]).then_inc(yb_done, 1)

                    for e in range(NE + 1):
                        if e < NE:
                            for m in range(HID):
                                k.hold(act, hn_done, (i * NE + e) * HID + m + 1 + 2 * HID)
                                k.hold(act, y_done, i * NE + e + 1)
                                act.activation(gl[:, e % 2, m, :], hn[:, e, m, :], ACT.Gelu, scale=w["f0_g"][:, e, m:m + 1],
                                               bias=w["f0_b"][:, e, m:m + 1]).then_inc(gl_done, 1)
                        if e >= 1:
                            add_b2(e - 1)

            @block.vector
            def _(dve):
                dve.sem_inc(hn_done, 2 * HID)
                dve.sem_inc(tmp_done, 2)
                with dve.Fori(0, NCH) as i:
                    for e in range(NE):
                        g = i * NE + e
                        k.hold(dve, rs_done, g + 1)
                        for m in range(HID):
                            k.hold(dve, gl_done, g * HID + m + 1)
                            dve.scalar_tensor_tensor(out=hn[:, e, m, :], in0=ps[:, 2 * (e % 2) + m, :],
                                                     scalar=b1c[:, e, m:m + 1], in1=rs[:, e % 2, :], op0=ALU.add,
                                                     op1=ALU.mult).then_inc(hn_done, 1)
                    for e in range(NE):
                        g = i * NE + e
                        k.hold(dve, yb_done, g + 3)
                        k.hold(dve, cb_done, g + 1)
                        k.hold(dve, acc_done, g + 1)
                        dve.tensor_tensor(tmp[:, e % 2, :], yb[:, e % 2, :], ps[:, 6 + e % 2, :], ALU.mult).then_inc(tmp_done, 1)

            @block.gpsimd
            def _(pool):
                pool.sem_inc(acc_done, 2)
                with pool.Fori(0, NCH) as i:
                    for e in range(NE):
                        g = i * NE + e
                        k.hold(pool, tmp_done, g + 3)
                        k.hold(pool, acc_done, g + 2)
                        pool.tensor_tensor(acc[:, bass.ds(i * CH, CH)], acc[:, bass.ds(i * CH, CH)], tmp[:, e % 2, :],
                                           ALU.add).then_inc(acc_done, 1)

        layer_norm(k, acc, acc, k.eps5, w["f0_ln_g"][:, 0:1], w["f0_ln_b"][:, 0:1])
        with nc.Block() as block:

            @block.vector
            def _(dve):
                dve.tensor_tensor(k.x[:, :], k.x[:, :], acc[:, :], ALU.add)


def layer1_attn(k, W):
    nc, ps = k.nc, k.ps
    with ExitStack() as ctx:
        w = {n: W(n) for n in ("a1_norm_w", "a1_in", "a1_conv", "a1_dt_w", "a1_dt_b", "a1_alog", "a1_bc", "a1_D", "a1_out")}
        xc = k.sb(ctx, "a1_xc", [P, DI, T])
        dt = k.sb(ctx, "a1_dt", [P, DI, T])
        du = k.sb(ctx, "a1_du", [P, DI, T])
        bc3 = k.sb(ctx, "a1_bc3", [96, T], BF16)
        A = k.sb(ctx, "a1_A", [P, DI, NS])
        layer_norm(k, k.xn, k.t2, k.eps6, w["a1_norm_w"][:, 0:1], rms=True)
        with ExitStack() as sub:
            padded = k.sb(sub, "a1_padded", [P, DI, NB, SEQ + 3])
            gate = k.sb(sub, "a1_gate", [P, DI, T])
            proj, g_out, x_out, zero, conv = k.sems(ctx, "a1_", "proj g_out x_out zero conv")
            with nc.Block() as block:

                @block.tensor
                def _(pe):
                    for m in range(4):
                        for j in range(NCH):
                            n = 4 * m + j
                            if n >= 8:
                                pe.wait_ge(g_out, n - 7)
                            pe.matmul(ps[:, n % 8, :], w["a1_in"][:, tile((m + 2) % 4)], k.t2[:, chunk(j)], start=True,
                                      stop=True).then_inc(proj, 1)

                @block.scalar
                def _(act):
                    for n in range(8):
                        act.wait_ge(proj, n + 1)
                        act.activation(gate[:, n // 4, chunk(n % 4)], ps[:, n, :], ACT.Silu).then_inc(g_out, 1)

                @block.vector
                def _(dve):
                    dve.memset(padded[:, :, :, 0:3], 0.0).then_inc(zero, 1)
                    for n in range(8):
                        dve.wait_ge(proj, n + 9)
                        dve.wait_ge(g_out, n + 1)
                        dve.tensor_tensor(padded[:, n // 4, n % 4 // 2, 3 + CH * (n % 2):3 + CH * (n % 2) + CH],
                                          gate[:, n // 4, chunk(n % 4)], ps[:, n, :], ALU.mult).then_inc(x_out, 1)
                    dve.wait_ge(x_out, 8)
                    dve.wait_ge(zero, 1)
                    for tap in range(4):
                        for hf in range(DI):
                            dst = xc[:, hf, :].rearrange("p (b t) -> p b t", b=NB)
                            src = padded[:, hf, :, tap:tap + SEQ]
                            kern = w["a1_conv"][:, hf, tap:tap + 1]
                            if tap == 0:
                                dve.tensor_scalar(dst, src, kern, None, ALU.mult).then_inc(conv, 1)
                            else:
                                dve.wait_ge(conv, 2 * (tap - 1) + hf + 1)
                                dve.scalar_tensor_tensor(out=dst, in0=src, scalar=kern, in1=dst, op0=ALU.mult,
                                                         op1=ALU.add).then_inc(conv, 1)
        with ExitStack() as sub:
            low = k.sb(sub, "a1_low", [P, T])
            up = k.sb(sub, "a1_up", [P, T])
            upped, = k.sems(ctx, "a1_", "upped")
            pre, rows, soft, aexp, relu_done, logd, summed = k.sems(ctx, "a1_", "pre rows soft aexp relu logd summed")
            s, mid, rest, psrows = split_rows(k, ctx, bc3, "a1")
            with nc.Block() as block:

                @block.tensor
                def _(pe):
                    for j in range(NCH):
                        for hf in range(DI):
                            mm = pe.matmul(ps[0:96, j, :], w["a1_bc"][:, hf, :], xc[:, hf, chunk(j)], start=(hf == 0), stop=(hf == 1))
                        mm.then_inc(rows, 1)
                    for m in range(DI):
                        if m:
                            pe.wait_ge(relu_done, 1)
                            pe.wait_ge(soft, 1)
                        for j in range(NCH):
                            for hf in range(DI):
                                mm = pe.matmul(ps[:, 4 + j, :], w["a1_dt_w"][:, hf, tile(m)], xc[:, hf, chunk(j)], start=(hf == 0),
                                               stop=(hf == 1))
                            mm.then_inc(pre, 1)

                @block.scalar
                def _(act):
                    act.activation(A[:, :, :], w["a1_alog"], ACT.Exp).then_inc(aexp, 1)
                    for m in range(DI):
                        act.wait_ge(pre, NCH * (m + 1))
                        v = ps[:, 4:8, :].rearrange("p a b -> p (a b)")
                        bias = w["a1_dt_b"][:, m:m + 1]
                        if m:
                            act.wait_ge(summed, 3)
                        act.activation(dt[:, m, :], v, ACT.Relu, bias=bias).then_inc(relu_done, 1)
                        act.activation(low[:, :], v, ACT.Abs, bias=bias).then_inc(soft, 1)
                        act.wait_ge(soft, 3 * m + 1)
                        act.activation(low[:, :], low[:, :], ACT.Exp, scale=-1.0).then_inc(soft, 1)
                        act.wait_ge(upped, 2 * m + 1)
                        act.activation(k.t3[:, :], up[:, :], ACT.Ln).then_inc(soft, 1)

                @block.vector
                def _(dve):
                    dve.wait_ge(rows, NCH)
                    split_steps(dve, k, s, mid, rest, psrows, bc3)
                    for m in range(DI):
                        dve.wait_ge(soft, 3 * m + 2)
                        dve.wait_ge(relu_done, m + 1)
                        softplus_steps(dve, k, dt[:, m, :], low, up, upped, soft, 3 * m + 3, summed, m)
                        dve.tensor_tensor(du[:, m, :], dt[:, m, :], xc[:, m, :], ALU.mult)
                    dve.wait_ge(aexp, 1)
                    dve.tensor_scalar(A[:, :, :], A[:, :, :], -1.0, None, ALU.mult)
        with ExitStack() as sub:
            def finish(dve, b, hf, y):
                v = xc[:, hf, bass.ds(b * SEQ, SEQ)]
                return dve.scalar_tensor_tensor(out=v, in0=v, scalar=w["a1_D"][:, hf:hf + 1], in1=y, op0=ALU.mult, op1=ALU.add)

            scan_loop(k, sub, "a1s", DI, du, bc3, finish, dt=dt, rate=A)
        project_out(k, ctx, "a1p", w["a1_out"], xc)


def layer1_ffn(k, W):
    nc, ps = k.nc, k.ps
    HID = 4
    with ExitStack() as ctx:
        w = {n: W(n) for n in ("f1_gate", "f1_w1", "f1_b1", "f1_w2", "f1_b2", "f1_sw", "f1_sb", "f1_g", "f1_b", "f1_sel")}
        comb_t = k.sb(ctx, "f1_comb_t", [NE, T])
        acc = k.sb(ctx, "f1_acc", [P, T])
        route_top2(k, ctx, "f1r", w["f1_gate"], comb_t)
        shared, gelud = k.sems(ctx, "f1_", "shared gelud")
        with nc.Block() as block:

            @block.tensor
            def _(pe):
                for j in range(NCH):
                    pe.matmul(ps[:, j, :], w["f1_sw"], k.xn[:, chunk(j)], start=True, stop=True).then_inc(shared, 1)

            @block.scalar
            def _(act):
                for j in range(NCH):
                    act.wait_ge(shared, j + 1)
                    act.activation(acc[:, chunk(j)], ps[:, j, :], ACT.Gelu, bias=w["f1_sb"][:, 0:1]).then_inc(gelud, 1)

            @block.vector
            def _(dve):
                dve.wait_ge(gelud, NCH)
                dve.tensor_scalar(acc[:, :], acc[:, :], 0.5, None, ALU.mult)

        gl = k.sb(ctx, "f1_gl", [P, 2, HID, CH])
        yb = k.sb(ctx, "f1_yb", [P, 2, CH])
        tmp = k.sb(ctx, "f1_tmp", [P, 2, CH])
        h_done, gl_done, y_done, cb_done, yb_done, tmp_done, acc_done = k.sems(ctx, "f1l_", "h gl y cb yb tmp acc")
        with nc.Block() as block:

            @block.tensor
            def _(pe):
                pe.sem_inc(y_done, 2)
                with pe.Fori(0, NCH) as i:
                    for e in range(NE + 1):
                        if e < NE:
                            for m in range(HID):
                                k.hold(pe, gl_done, (i * NE + e) * HID + m + 1)
                                pe.matmul(ps[:, m, :], w["f1_w1"][:, e * HID + m, :], k.xn[:, bass.ds(i * CH, CH)], start=True,
                                          stop=True).then_inc(h_done, 1)
                        if e >= 1:
                            f, g = e - 1, i * NE + e - 1
                            k.hold(pe, tmp_done, g + 1)
                            pe.matmul(ps[:, 6 + f % 2, :], w["f1_sel"][:, f, :], comb_t[:, bass.ds(i * CH, CH)], start=True,
                                      stop=True).then_inc(cb_done, 1)
                            k.hold(pe, gl_done, g * HID + 2 * HID)
                            k.hold(pe, yb_done, g + 1)
                            for m in range(HID):
                                mm = pe.matmul(ps[:, 4 + f % 2, :], w["f1_w2"][:, f * HID + m, :], gl[:, f % 2, m, :],
                                               start=(m == 0), stop=(m == HID - 1))
                            mm.then_inc(y_done, 1)

            @block.scalar
            def _(act):
                act.sem_inc(gl_done, HID)
                act.sem_inc(yb_done, 2)
                with act.Fori(0, NCH) as i:
                    for e in range(NE + 1):
                        if e < NE:
                            for m in range(HID):
                                k.hold(act, h_done, (i * NE + e) * HID + m + 1)
                                k.hold(act, y_done, i * NE + e + 1)
                                act.activation(gl[:, e % 2, m, :], ps[:, m, :], ACT.Gelu,
                                               bias=w["f1_b1"][:, e, m:m + 1]).then_inc(gl_done, 1)
                        if e >= 1:
                            f, g = e - 1, i * NE + e - 1
                            k.hold(act, y_done, g + 3)
                            k.hold(act, tmp_done, g + 1)
                            act.activation(yb[:, f % 2, :], ps[:, 4 + f % 2, :], ACT.Identity,
                                           bias=w["f1_b2"][:, f:f + 1]).then_inc(yb_done, 1)

            @block.vector
            def _(dve):
                dve.sem_inc(tmp_done, 2)
                with dve.Fori(0, NCH) as i:
                    for e in range(NE):
                        g = i * NE + e
                        k.hold(dve, yb_done, g + 3)
                        k.hold(dve, cb_done, g + 1)
                        k.hold(dve, acc_done, g + 1)
                        dve.tensor_tensor(tmp[:, e % 2, :], yb[:, e % 2, :], ps[:, 6 + e % 2, :], ALU.mult).then_inc(tmp_done, 1)

            @block.gpsimd
            def _(pool):
                pool.sem_inc(acc_done, 2)
                with pool.Fori(0, NCH) as i:
                    for e in range(NE):
                        g = i * NE + e
                        k.hold(pool, tmp_done, g + 3)
                        k.hold(pool, acc_done, g + 2)
                        pool.tensor_tensor(acc[:, bass.ds(i * CH, CH)], acc[:, bass.ds(i * CH, CH)], tmp[:, e % 2, :],
                                           ALU.add).then_inc(acc_done, 1)

        layer_norm(k, acc, acc, k.eps5, w["f1_g"][:, 0:1], w["f1_b"][:, 0:1])
        with nc.Block() as block:

            @block.vector
            def _(dve):
                dve.tensor_tensor(k.x[:, :], k.x[:, :], acc[:, :], ALU.add)

LAYERS = (0, 1, 2, 3)


NH, HD = 16, 64
PAIRS = NH // 2
PAIR_COLS = 2 * P + 2 * P + P + 2 + 2 + 2


def layer2_attn(k, W):
    nc, ps = k.nc, k.ps
    pairs_dram, _ = k.views["a2w"]
    with ExitStack() as ctx:
        w = {n: W(n) for n in ("a2_wo", "a2_bo", "a2_g", "a2_b", "a2_lam")}
        ocat = k.sb(ctx, "a2_ocat", [P, PAIRS, T])
        wp = k.sb(ctx, "a2_wp", [P, PAIR_COLS])
        wq, wk, wv = wp[:, 0:2 * P], wp[:, 2 * P:4 * P], wp[:, 4 * P:5 * P]
        bq, bk, bv = wp[:, 5 * P:5 * P + 2], wp[:, 5 * P + 2:5 * P + 4], wp[0:HD, 5 * P + 4:5 * P + 6]
        qt = k.sb(ctx, "a2_qt", [P, 2, T])
        kt = k.sb(ctx, "a2_kt", [P, 2, T])
        qb = k.sb(ctx, "a2_qb", [P, 2, T], BF16)
        kb = k.sb(ctx, "a2_kb", [P, 2, T], BF16)
        v = k.sb(ctx, "a2_v", [P, NT, 2, P])
        prob = k.t1[:, :].rearrange("p (n c) -> p n c", n=4)
        prob2 = k.t2[:, :].rearrange("p (n c) -> p n c", n=4)
        rden = k.t3[0:HD, :].rearrange("p (a c) -> p a c", a=2)
        o = k.sb(ctx, "a2_o", [HD, 2, SEQ])
        mx2 = k.sb(ctx, "a2_mx2", [P, 2, 8, 2])
        mx = k.sb(ctx, "a2_mx", [P, 2, 8])
        mrow = k.sb(ctx, "a2_mrow", [1, 2, 2, SEQ], BF16)
        onerow = k.sb(ctx, "a2_onerow", [1, P], BF16)
        negid = k.sb(ctx, "a2_negid", [P, P])
        lam = k.sb(ctx, "a2_lam2", [P, 2])
        bvl = k.sb(ctx, "a2_bvl", [HD, 2])
        (w_loaded, placed, qkv_ready, qkv_out, bf_done, max_ready, reduced, mx_done, mrow_ready, mrow_out, s_ready,
         exp_done, pv_done, ln_done, r_done, fin, comb, init, bvl_done) = k.sems(
            ctx, "a2_", "w_loaded placed qkv_ready qkv_out bf_done max_ready reduced mx_done mrow_ready mrow_out "
            "s_ready exp_done pv_done ln_done r_done fin comb init bvl")
        UNITS = [(hh, b) for hh in range(2) for b in range(NB)]
        STEPS = 32
        QKV = 20

        def p_buf(st):
            return (prob if st % 8 < 4 else prob2)[:, st % 4, :]

        with nc.Block() as block:

            @block.sync
            def _(sp):
                with sp.Fori(0, PAIRS) as pr:
                    k.hold(sp, placed, 4 * pr + 1)
                    sp.dma_start(wp[:, :], pairs_dram[:, bass.ds(pr * PAIR_COLS, PAIR_COLS)]).then_inc(w_loaded, 16)
                sp.wait_ge(w_loaded, 16 * PAIRS)

            @block.gpsimd
            def _(pool):
                pool.memset(v[:, :, :, HD:P], 1.0).then_inc(init, 1)
                pool.memset(onerow[:, :], 1.0).then_inc(init, 1)
                with pool.Fori(0, PAIRS) as pr:
                    for n, (dst, src) in enumerate(((qb, qt), (kb, kt))):
                        for hh in range(2):
                            k.hold(pool, qkv_out, pr * QKV + 8 * n + 4 * hh + 4 + 2)
                            pool.tensor_copy(dst[:, hh, :], src[:, hh, :]).then_inc(bf_done, 1)

            @block.tensor
            def _(pe):
                pe.sem_inc(pv_done, 8)
                pe.wait_ge(init, 3)

                def max_block(g, n, mb):
                    hh, b = UNITS[n]
                    a, qi, kc = mb // 16, mb % 16 // 2, mb % 2
                    k.hold(pe, reduced, g * STEPS + mb + 1)
                    rows = slice(HD * a, HD * a + HD)
                    pe.matmul(ps[:, 6 + mb % 2, :], qb[rows, hh, SEQ * b + P * qi:SEQ * b + P * qi + P],
                              kb[rows, hh, SEQ * b + CH * kc:SEQ * b + CH * kc + CH], start=True, stop=True).then_inc(max_ready, 1)

                def max_rows(g):
                    k.hold(pe, mx_done, g + 1)
                    for a in range(2):
                        if a:
                            k.hold(pe, mrow_out, 2 * g + 2)
                        for qi in range(8):
                            mm = pe.matmul(ps[0:1, 6 + qi // 4, P * (qi % 4):P * (qi % 4) + P], mx[:, a, qi:qi + 1],
                                           negid[:, :], start=True, stop=True)
                        mm.then_inc(mrow_ready, 1)

                def score(g, n, st):
                    hh, b = UNITS[n]
                    a, ki, qc = st // 16, st % 16 // 2, st % 2
                    rows = slice(HD * a, HD * a + HD)
                    k.hold(pe, exp_done, g * STEPS + st + 1)
                    pe.matmul(ps[:, st % 2, :], kt[rows, hh, SEQ * b + P * ki:SEQ * b + P * ki + P],
                              qt[rows, hh, SEQ * b + CH * qc:SEQ * b + CH * qc + CH], start=True, stop=False)
                    pe.matmul(ps[:, st % 2, :], onerow[:, :], mrow[:, n % 2, a, chunk(qc)], start=False, stop=True).then_inc(s_ready, 1)

                def weigh(g, n, st):
                    hh, b = UNITS[n]
                    a, ki, qc = st // 16, st % 16 // 2, st % 2
                    k.hold(pe, exp_done, g * STEPS + st + 3)
                    if st % 16 == 0:
                        k.hold(pe, fin, 2 * g + a + 1)
                    pe.matmul(ps[:, 2 + 2 * a + qc, :], v[:, 8 * b + ki, hh, :], p_buf(st), start=(ki == 0),
                              stop=(ki == 7)).then_inc(pv_done, 1)

                with pe.Fori(0, PAIRS) as pr:
                    k.hold(pe, w_loaded, 16 * (pr + 1))
                    for idx in range(QKV):
                        k.hold(pe, qkv_out, pr * QKV + idx + 1)
                        bank = 6 + idx % 2
                        if idx < 16:
                            wt, hh, j = (wq, wk)[idx // 8], idx // 4 % 2, idx % 4
                            mm = pe.matmul(ps[:, bank, :], wt[:, tile(hh)], k.xn[:, chunk(j)], start=True, stop=True)
                        else:
                            for q in range(4):
                                mm = pe.matmul(ps[:, bank, tile(q)], k.xn[:, tile(4 * (idx - 16) + q)], wv, start=True, stop=True)
                        mm.then_inc(qkv_ready, 1)
                    k.hold(pe, bf_done, 4 * pr + 4)
                    k.hold(pe, qkv_out, (pr + 1) * QKV + 2)
                    for mb in range(STEPS):
                        max_block(pr * 4, 0, mb)
                    max_rows(pr * 4)
                    for n in range(4):
                        g = pr * 4 + n
                        k.hold(pe, mrow_out, 2 * g + 3)
                        for st in range(STEPS + 1):
                            if st < STEPS:
                                score(g, n, st)
                                if n < 3:
                                    max_block(g + 1, n + 1, st)
                            if st >= 1:
                                weigh(g, n, st - 1)
                        if n < 3:
                            max_rows(g + 1)

            @block.scalar
            def _(act):
                act.sem_inc(qkv_out, 2)
                act.sem_inc(exp_done, 2)
                act.sem_inc(mrow_out, 1)

                def row_out(g, n):
                    for a in range(2):
                        k.hold(act, mrow_ready, 2 * g + a + 1)
                        act.activation(mrow[:, n % 2, a, :], ps[0:1, 6:8, :].rearrange("p a b -> p (a b)"),
                                       ACT.Copy).then_inc(mrow_out, 1)

                def invert_sum(g, a):
                    k.hold(act, pv_done, g * STEPS + 16 * a + 16 + 8)
                    k.hold(act, fin, 2 * g + a + 1)
                    act.activation(rden[:, a, :], ps[HD:P, 2 + 2 * a:4 + 2 * a, :].rearrange("p a b -> p (a b)"), ACT.Ln).then_inc(ln_done, 1)
                    k.hold(act, ln_done, 2 * g + a + 1)
                    act.activation(rden[:, a, :], rden[:, a, :], ACT.Exp, scale=-1.0).then_inc(r_done, 1)

                with act.Fori(0, PAIRS) as pr:
                    for idx in range(QKV):
                        k.hold(act, qkv_ready, pr * QKV + idx + 1)
                        bank = 6 + idx % 2
                        if idx < 16:
                            (dst, bias), hh, j = ((qt, bq), (kt, bk))[idx // 8], idx // 4 % 2, idx % 4
                            ins = act.activation(dst[:, hh, chunk(j)], ps[:, bank, :], ACT.Identity, bias=bias[:, hh:hh + 1])
                        else:
                            t0 = 4 * (idx - 16)
                            ins = act.activation(v[:, t0:t0 + 4, :, 0:HD],
                                                 ps[:, bank, :].rearrange("p (t h d) -> p t h d", t=4, h=2), ACT.Copy)
                        ins.then_inc(qkv_out, 1)
                    row_out(pr * 4, 0)
                    for n in range(4):
                        g = pr * 4 + n
                        for st in range(STEPS):
                            k.hold(act, s_ready, g * STEPS + st + 1)
                            k.hold(act, pv_done, g * STEPS + st + 1)
                            act.activation(p_buf(st), ps[:, st % 2, :], ACT.Exp, scale=float(HD) ** -0.5).then_inc(exp_done, 1)
                            if st == 19:
                                invert_sum(g, 0)
                        invert_sum(g, 1)
                        if n < 3:
                            row_out(g + 1, n + 1)

            @block.vector
            def _(dve):
                dve.sem_inc(reduced, 2)
                dve.sem_inc(fin, 2)
                dve.sem_inc(placed, 1)
                dve.tensor_scalar(negid[:, :], k.ident[:, :], -1.0, None, ALU.mult).then_inc(init, 1)
                dve.tensor_scalar(lam[:, 0:1], w["a2_lam"], -1.0, None, ALU.mult).then_inc(bvl_done, 1)
                dve.tensor_scalar(lam[:, 1:2], w["a2_lam"], -1.0, 1.0, ALU.mult, ALU.add).then_inc(bvl_done, 1)
                dve.wait_ge(bvl_done, 2)

                def reduce_block(g, mb):
                    a, qi, kc = mb // 16, mb % 16 // 2, mb % 2
                    k.hold(dve, max_ready, g * STEPS + mb + 1)
                    dve.tensor_reduce(mx2[:, a, qi, kc:kc + 1], ps[:, 6 + mb % 2, :], AX.X, ALU.max).then_inc(reduced, 1)

                def both_chunks(g):
                    k.hold(dve, reduced, (g + 1) * STEPS + 2)
                    k.hold(dve, mrow_out, 2 * g + 1)
                    dve.tensor_reduce(mx[:, :, :], mx2[:, :, :, :], AX.X, ALU.max).then_inc(mx_done, 1)

                def normalise(g, a):
                    k.hold(dve, r_done, 2 * g + a + 1)
                    k.hold(dve, placed, g + 1)
                    dve.tensor_tensor(o[:, a, :], rden[:, a, :], ps[0:HD, 2 + 2 * a:4 + 2 * a, :].rearrange("p a b -> p (a b)"),
                                      ALU.mult).then_inc(fin, 1)

                with dve.Fori(0, PAIRS) as pr:
                    for mb in range(STEPS):
                        reduce_block(pr * 4, mb)
                    both_chunks(pr * 4)
                    k.hold(dve, w_loaded, 16 * (pr + 1))
                    dve.tensor_scalar(bvl[:, :], bv, lam[0:HD, 1:2], None, ALU.mult).then_inc(bvl_done, 1)
                    for n, (hh, b) in enumerate(UNITS):
                        g = pr * 4 + n
                        for mb in range(STEPS):
                            if n < 3:
                                reduce_block(g + 1, mb)
                            if mb == 20:
                                normalise(g, 0)
                        if n < 3:
                            both_chunks(g + 1)
                        normalise(g, 1)
                        k.hold(dve, fin, 2 * g + 4)
                        dve.scalar_tensor_tensor(out=o[:, 0, :], in0=o[:, 1, :], scalar=lam[0:HD, 0:1], in1=o[:, 0, :],
                                                 op0=ALU.mult, op1=ALU.add).then_inc(comb, 1)
                        k.hold(dve, comb, g + 1)
                        k.hold(dve, bvl_done, pr + 3)
                        ins = dve.tensor_scalar(ocat[HD * hh:HD * hh + HD, bass.ds(pr, 1), SEQ * b:SEQ * b + SEQ].rearrange("p a t -> p (a t)"),
                                                o[:, 0, :], bvl[:, hh:hh + 1], None, ALU.add)
                        ins.then_inc(placed, 1)

        y, = k.sems(ctx, "a2_", "y")
        with nc.Block() as block:

            @block.tensor
            def _(pe):
                for j in range(NCH):
                    for pr in range(PAIRS):
                        mm = pe.matmul(ps[:, j, :], w["a2_wo"][:, pr, :], ocat[:, pr, chunk(j)], start=(pr == 0), stop=(pr == PAIRS - 1))
                    mm.then_inc(y, 1)

            @block.scalar
            def _(act):
                for j in range(NCH):
                    act.wait_ge(y, j + 1)
                    act.activation(qt[:, 0, chunk(j)], ps[:, j, :], ACT.Identity, bias=w["a2_bo"][:, 0:1])

        layer_norm(k, qt[:, 0, :], qt[:, 0, :], k.eps5, w["a2_g"][:, 0:1], w["a2_b"][:, 0:1])
        with nc.Block() as block:

            @block.vector
            def _(dve):
                dve.scalar_tensor_tensor(out=k.x[:, :], in0=qt[:, 0, :], scalar=1.0 - 0.8, in1=k.x[:, :], op0=ALU.mult, op1=ALU.add)


def layer2_ffn(k, W):
    nc, ps = k.nc, k.ps
    E, GR, CAP, PR = 64, 8, 64, 32
    with ExitStack() as ctx:
        w = {n: W(n) for n in ("f2_router", "f2_gate", "f2_up", "f2_down", "f2_sg", "f2_su", "f2_sd", "f2_sel")}
        comb_t = k.sb(ctx, "f2_comb_t", [E, T])
        with ExitStack() as sub:
            sc = k.sb(sub, "f2_scores", [P, NT, E])
            rep = k.sb(sub, "f2_rep", [P, NT, E])
            mask = k.sb(sub, "f2_mask", [P, NT, E])
            gs = k.sb(sub, "f2_gs", [P, NT, GR])
            gtop = k.sb(sub, "f2_gtop", [P, NT, 8])
            top = k.sb(sub, "f2_top", [P, NT, 8])
            tot = k.sb(sub, "f2_tot", [P, NT])
            logit, scored, step, turned_w, turned_m, copied = k.sems(ctx, "f2r_", "logit scored step turned_w turned_m copied")
            flat = lambda v: v.rearrange("p t e -> p (t e)")
            with nc.Block() as block:

                @block.tensor
                def _(pe):
                    for t in range(NT):
                        mm = pe.matmul(ps[:, t // 8, E * (t % 8):E * (t % 8) + E], k.xn[:, tile(t)], w["f2_router"], start=True, stop=True)
                    mm.then_inc(logit, 1)
                    pe.wait_ge(step, 66)
                    for t in range(NT):
                        mm = pe.transpose(ps[0:E, t // 4, P * (t % 4):P * (t % 4) + P], sc[:, t, :], k.ident[:, :])
                    mm.then_inc(turned_w, 1)
                    for t in range(NT):
                        mm = pe.transpose(ps[0:E, 4 + t // 4, P * (t % 4):P * (t % 4) + P], mask[:, t, :], k.ident[:, :])
                    mm.then_inc(turned_m, 1)

                @block.scalar
                def _(act):
                    act.wait_ge(logit, 1)
                    act.activation(flat(sc[:, :, :]), ps[:, 0:2, :].rearrange("p a b -> p (a b)"), ACT.Sigmoid).then_inc(scored, 1)
                    act.wait_ge(turned_w, 1)
                    act.activation(comb_t[:, :], ps[0:E, 0:4, :].rearrange("p a b -> p (a b)"), ACT.Copy).then_inc(copied, 1)

                @block.vector
                def _(dve):
                    dve.wait_ge(scored, 1)
                    dve.tensor_reduce(flat(gs[:, :, :]), sc[:, :, :].rearrange("p t (g e) -> p (t g) e", g=GR), AX.X, ALU.max).then_inc(step, 1)
                    dve.wait_ge(step, 1)
                    for t in range(NT):
                        dve.max(gtop[:, t, :], gs[:, t, :]).then_inc(step, 1)
                    dve.wait_ge(step, 1 + NT)
                    dve.tensor_tensor(gs[:, :, :], gs[:, :, :], gtop[:, :, 3:4].to_broadcast([P, NT, GR]), ALU.is_ge).then_inc(step, 1)
                    dve.wait_ge(step, 2 + NT)
                    dve.tensor_tensor(sc[:, :, :].rearrange("p t (g e) -> p (t g) e", g=GR),
                                      sc[:, :, :].rearrange("p t (g e) -> p (t g) e", g=GR),
                                      flat(gs[:, :, :]).unsqueeze(2).to_broadcast([P, NT * GR, GR]), ALU.mult).then_inc(step, 1)
                    dve.wait_ge(step, 3 + NT)
                    for t in range(NT):
                        dve.max(top[:, t, :], sc[:, t, :]).then_inc(step, 1)
                    dve.wait_ge(step, 3 + 2 * NT)
                    for t in range(NT):
                        dve.match_replace(out=rep[:, t, :], in_to_replace=top[:, t, :], in_values=sc[:, t, :], imm_value=-1.0).then_inc(step, 1)
                    dve.tensor_reduce(tot[:, :], top[:, :, :], AX.X, ALU.add).then_inc(step, 1)
                    dve.wait_ge(step, 4 + 3 * NT)
                    dve.tensor_scalar(tot[:, :], tot[:, :], 1e-9, None, ALU.max).then_inc(step, 1)
                    dve.tensor_scalar(flat(mask[:, :, :]), flat(rep[:, :, :]), 0.0, None, ALU.is_lt).then_inc(step, 1)
                    dve.wait_ge(step, 6 + 3 * NT)
                    dve.reciprocal(tot[:, :], tot[:, :]).then_inc(step, 1)
                    dve.tensor_tensor(sc[:, :, :], sc[:, :, :], mask[:, :, :], ALU.mult).then_inc(step, 1)
                    dve.wait_ge(step, 8 + 3 * NT)
                    dve.tensor_scalar(tot[:, :], tot[:, :], 2.5, None, ALU.mult).then_inc(step, 1)
                    dve.wait_ge(step, 9 + 3 * NT)
                    dve.tensor_tensor(sc[:, :, :], sc[:, :, :], tot[:, :].unsqueeze(2).to_broadcast([P, NT, E]), ALU.mult).then_inc(step, 9)
                    dve.memset(k.t1[0:E, :], 1.0).then_inc(step, 1)
                    dve.wait_ge(step, 19 + 3 * NT)
                    dve.wait_ge(turned_m, 1)
                    dve.tensor_tensor_scan(k.t2[0:E, :], k.t1[0:E, :], ps[0:E, 4:8, :].rearrange("p a b -> p (a b)"), 0.0,
                                           ALU.mult, ALU.add).then_inc(step, 1)
                    dve.wait_ge(step, 20 + 3 * NT)
                    dve.wait_ge(copied, 1)
                    dve.scalar_tensor_tensor(out=comb_t[:, :], in0=k.t2[0:E, :], scalar=float(CAP), in1=comb_t[:, :],
                                             op0=ALU.is_le, op1=ALU.mult)

        sg = k.sb(ctx, "f2_sgb", [P, 2, CH])
        h1 = k.sb(ctx, "f2_h1", [P, 2, CH])
        hw = k.sb(ctx, "f2_hw", [P, 2, CH])
        g_s, silu_s, h_s, y_s = k.sems(ctx, "f2s_", "gated silu hidden y")
        hs = k.t2[0:HD, :]
        with nc.Block() as block:

            @block.tensor
            def _(pe):
                for j in range(NCH):
                    pe.matmul(ps[0:HD, j, :], w["f2_sg"], k.xn[:, chunk(j)], start=True, stop=True)
                    pe.matmul(ps[0:HD, 4 + j, :], w["f2_su"], k.xn[:, chunk(j)], start=True, stop=True).then_inc(g_s, 1)
                pe.wait_ge(h_s, 1)
                for j in range(NCH):
                    mm = pe.matmul(ps[:, j, :], w["f2_sd"], hs[:, chunk(j)], start=True, stop=True)
                mm.then_inc(y_s, 1)

            @block.scalar
            def _(act):
                act.wait_ge(g_s, NCH)
                act.activation(k.t1[0:HD, :], ps[0:HD, 0:4, :].rearrange("p a b -> p (a b)"), ACT.Silu).then_inc(silu_s, 1)

            @block.vector
            def _(dve):
                dve.wait_ge(silu_s, 1)
                dve.tensor_tensor(hs, k.t1[0:HD, :], ps[0:HD, 4:8, :].rearrange("p a b -> p (a b)"), ALU.mult).then_inc(h_s, 1)
                dve.wait_ge(y_s, 1)
                dve.tensor_tensor(k.x[:, :], k.x[:, :], ps[:, 0:4, :].rearrange("p a b -> p (a b)"), ALU.add)

        gu, cb, silu, mul1, mul2, y_done, y_out = k.sems(ctx, "f2l_", "gu cb silu mul1 mul2 y_done y_out")
        with nc.Block() as block:

            @block.tensor
            def _(pe):
                pe.sem_inc(y_done, 2)
                with pe.Fori(0, NCH) as i:
                    for p in range(PR + 1):
                        if p < PR:
                            g = i * PR + p
                            k.hold(pe, silu, g + 1)
                            k.hold(pe, mul1, g + 1)
                            pe.matmul(ps[:, p % 2, :], w["f2_gate"][:, p, :], k.xn[:, bass.ds(i * CH, CH)], start=True, stop=True)
                            pe.matmul(ps[:, 2 + p % 2, :], w["f2_up"][:, p, :], k.xn[:, bass.ds(i * CH, CH)], start=True,
                                      stop=True).then_inc(gu, 1)
                            k.hold(pe, mul2, g + 1)
                            pe.matmul(ps[:, 4 + p % 2, :], w["f2_sel"][:, p, :], comb_t[:, bass.ds(i * CH, CH)], start=True,
                                      stop=True).then_inc(cb, 1)
                        if p >= 1:
                            f, g = p - 1, i * PR + p - 1
                            k.hold(pe, mul2, g + 3)
                            if f == 0:
                                k.hold(pe, y_out, i + 1)
                            pe.matmul(ps[:, 6, :], w["f2_down"][:, f, :], hw[:, f % 2, :], start=(f == 0),
                                      stop=(f == PR - 1)).then_inc(y_done, 1)

            @block.scalar
            def _(act):
                act.sem_inc(silu, 2)
                with act.Fori(0, NCH) as i:
                    for p in range(PR):
                        g = i * PR + p
                        k.hold(act, gu, g + 1)
                        k.hold(act, mul1, g + 1)
                        act.activation(sg[:, p % 2, :], ps[:, p % 2, :], ACT.Silu).then_inc(silu, 1)

            @block.vector
            def _(dve):
                dve.sem_inc(mul1, 2)
                dve.sem_inc(mul2, 2)
                dve.sem_inc(y_out, 1)
                with dve.Fori(0, NCH) as i:
                    for p in range(PR):
                        g = i * PR + p
                        k.hold(dve, silu, g + 3)
                        k.hold(dve, mul2, g + 1)
                        dve.tensor_tensor(h1[:, p % 2, :], sg[:, p % 2, :], ps[:, 2 + p % 2, :], ALU.mult).then_inc(mul1, 1)
                        k.hold(dve, mul1, g + 3)
                        k.hold(dve, cb, g + 1)
                        k.hold(dve, y_done, g + 1)
                        dve.tensor_tensor(hw[:, p % 2, :], h1[:, p % 2, :], ps[:, 4 + p % 2, :], ALU.mult).then_inc(mul2, 1)
                    k.hold(dve, y_done, (i + 1) * PR + 2)
                    dve.tensor_tensor(k.x[:, bass.ds(i * CH, CH)], k.x[:, bass.ds(i * CH, CH)], ps[:, 6, :], ALU.add).then_inc(y_out, 1)


def layer3_attn(k, W):
    nc, ps = k.nc, k.ps
    with ExitStack() as ctx:
        w = {n: W(n) for n in ("a3_in", "a3_conv", "a3_bc", "a3_dtr", "a3_dt_w", "a3_dt_b", "a3_alog", "a3_D", "a3_out", "a3_bout")}
        xz = k.sb(ctx, "a3_xz", [P, 2, T])
        dt = k.sb(ctx, "a3_dt", [P, 1, T])
        du = k.sb(ctx, "a3_du", [P, 1, T])
        bc3 = k.sb(ctx, "a3_bc3", [96, T], BF16)
        A = k.sb(ctx, "a3_A", [P, 1, NS])
        with ExitStack() as sub:
            padded = k.sb(sub, "a3_padded", [P, 2, NB, SEQ + 3])
            proj, x_out, zero, conv = k.sems(ctx, "a3_", "proj x_out zero conv")
            with nc.Block() as block:

                @block.tensor
                def _(pe):
                    for n in range(8):
                        pe.matmul(ps[:, n, :], w["a3_in"][:, tile(n // 4)], k.xn[:, chunk(n % 4)], start=True, stop=True).then_inc(proj, 1)

                @block.scalar
                def _(act):
                    for n in range(8):
                        act.wait_ge(proj, n + 1)
                        act.activation(padded[:, n // 4, n % 4 // 2, 1 + CH * (n % 2):1 + CH * (n % 2) + CH], ps[:, n, :],
                                       ACT.Copy).then_inc(x_out, 1)
                    for m in range(2):
                        act.wait_ge(conv, 7 + m)
                        act.activation(xz[:, m, :], xz[:, m, :], ACT.Silu)

                @block.vector
                def _(dve):
                    dve.memset(padded[:, :, :, 0:1], 0.0).then_inc(zero, 1)
                    dve.memset(padded[:, :, :, SEQ + 1:SEQ + 3], 0.0).then_inc(zero, 1)
                    dve.wait_ge(zero, 2)
                    dve.wait_ge(x_out, 8)
                    for tap in range(4):
                        for m in range(2):
                            dst = xz[:, m, :].rearrange("p (b t) -> p b t", b=NB)
                            src = padded[:, m, :, tap:tap + SEQ]
                            kern = w["a3_conv"][:, m, tap:tap + 1]
                            if tap == 0:
                                dve.tensor_scalar(dst, src, kern, None, ALU.mult).then_inc(conv, 1)
                            else:
                                dve.wait_ge(conv, 2 * (tap - 1) + m + 1)
                                dve.scalar_tensor_tensor(out=dst, in0=src, scalar=kern, in1=dst, op0=ALU.mult,
                                                         op1=ALU.add).then_inc(conv, 1)
        with ExitStack() as sub:
            low = k.sb(sub, "a3_low", [P, T])
            up = k.sb(sub, "a3_up", [P, T])
            upped, = k.sems(ctx, "a3_", "upped")
            dtr = k.sb(sub, "a3_dtrows", [8, T])
            b2 = k.sb(sub, "a3_b2", [P, 1])
            rows, drows, dcopy, pre, soft, aexp, summed, biased = k.sems(ctx, "a3_", "rows drows dcopy pre soft aexp summed biased")
            s, mid, rest, psrows = split_rows(k, ctx, bc3, "a3")
            with nc.Block() as block:

                @block.tensor
                def _(pe):
                    for j in range(NCH):
                        pe.matmul(ps[0:8, 4 + j, :], w["a3_dtr"], xz[:, 0, chunk(j)], start=True, stop=True).then_inc(drows, 1)
                    for j in range(NCH):
                        pe.matmul(ps[0:96, j, :], w["a3_bc"][:, 0, :], xz[:, 0, chunk(j)], start=True, stop=True).then_inc(rows, 1)
                    pe.wait_ge(dcopy, 1)
                    for j in range(NCH):
                        pe.matmul(ps[:, 4 + j, :], w["a3_dt_w"], dtr[:, chunk(j)], start=True, stop=True).then_inc(pre, 1)

                @block.scalar
                def _(act):
                    act.activation(A[:, 0, :], w["a3_alog"], ACT.Exp).then_inc(aexp, 1)
                    act.wait_ge(drows, NCH)
                    act.activation(dtr[:, :], ps[0:8, 4:8, :].rearrange("p a b -> p (a b)"), ACT.Copy).then_inc(dcopy, 1)
                    act.wait_ge(pre, NCH)
                    act.wait_ge(biased, 1)
                    v = ps[:, 4:8, :].rearrange("p a b -> p (a b)")
                    act.activation(dt[:, 0, :], v, ACT.Relu, bias=b2[:, 0:1]).then_inc(soft, 1)
                    act.activation(low[:, :], v, ACT.Abs, bias=b2[:, 0:1]).then_inc(soft, 1)
                    act.wait_ge(soft, 2)
                    act.activation(low[:, :], low[:, :], ACT.Exp, scale=-1.0).then_inc(soft, 1)
                    act.wait_ge(upped, 1)
                    act.activation(k.t3[:, :], up[:, :], ACT.Ln).then_inc(soft, 1)

                @block.vector
                def _(dve):
                    dve.tensor_scalar(b2[:, :], w["a3_dt_b"], 2.0, None, ALU.mult).then_inc(biased, 1)
                    dve.wait_ge(rows, NCH)
                    split_steps(dve, k, s, mid, rest, psrows, bc3)
                    dve.wait_ge(soft, 3)
                    softplus_steps(dve, k, dt[:, 0, :], low, up, upped, soft, 4, summed, 0)
                    dve.tensor_tensor(du[:, 0, :], dt[:, 0, :], xz[:, 0, :], ALU.mult)
                    dve.wait_ge(aexp, 1)
                    dve.tensor_scalar(A[:, 0, :], A[:, 0, :], -1.0, None, ALU.mult)
        with ExitStack() as sub:
            def finish(dve, b, hf, y):
                v = xz[:, 0, bass.ds(b * SEQ, SEQ)]
                return dve.scalar_tensor_tensor(out=v, in0=v, scalar=w["a3_D"][:, 0:1], in1=y, op0=ALU.mult, op1=ALU.add)

            scan_loop(k, sub, "a3s", 1, du, bc3, finish, dt=dt, rate=A)
        with nc.Block() as block:

            @block.scalar
            def _(act):
                act.activation(k.x[:, :], k.x[:, :], ACT.Identity, bias=w["a3_bout"][:, 0:1])
        project_out(k, ctx, "a3p", w["a3_out"], xz)


MIDS = (5.0, 3.5, 2.5, 1.75, 1.25, 0.75, 0.25)


class Fp4:

    STEPS, PARTS = 14, 2

    def __init__(self, k, ctx, name, nblk):
        self.k, self.n = k, nblk
        self.step, self.parts = k.sems(ctx, name + "_", "step parts")
        self.amax = k.sb(ctx, name + "_amax", [P, nblk])
        self.rec = k.sb(ctx, name + "_rec", [P, nblk])
        self.ab = k.sb(ctx, name + "_ab", [P, nblk * 16])
        self.sg = k.sb(ctx, name + "_sg", [P, nblk * 16])
        self.xs = k.sb(ctx, name + "_xs", [P, nblk * 16])

    def blocks(self, v):
        return v.rearrange("p (n c) -> p n c", c=16)

    def scalar(self, act, wait, n0):
        wait(act, self.step, n0 * self.STEPS + 4)
        act.activation(self.ab[:, :], self.xs[:, :], ACT.Abs).then_inc(self.parts, 1)
        act.activation(self.sg[:, :], self.xs[:, :], ACT.Sign).then_inc(self.parts, 1)

    def vector(self, dve, wait, n0, src, dst):
        base = n0 * self.STEPS
        bc = lambda v: v.unsqueeze(2).to_broadcast([P, self.n, 16])
        count = [0]

        def done(ins):
            ins.then_inc(self.step, 1)
            count[0] += 1
            wait(dve, self.step, base + count[0])

        done(dve.tensor_reduce(self.amax[:, :], self.blocks(src), AX.X, ALU.max, apply_absolute_value=True))
        done(dve.tensor_scalar(self.amax[:, :], self.amax[:, :], 1.0 / 6.0, 1e-12, ALU.mult, ALU.max))
        done(dve.reciprocal(self.rec[:, :], self.amax[:, :]))
        done(dve.tensor_tensor(self.blocks(self.xs[:, :]), self.blocks(src), bc(self.rec[:, :]), ALU.mult))
        wait(dve, self.parts, n0 * self.PARTS + 2)
        ab, q = self.ab[:, :], self.xs[:, :]
        done(dve.tensor_scalar(q, ab, MIDS[0], 2.0, ALU.is_gt, ALU.mult))
        for m in MIDS[1:3]:
            done(dve.scalar_tensor_tensor(out=q, in0=ab, scalar=m, in1=q, op0=ALU.is_gt, op1=ALU.add))
        done(dve.tensor_scalar(q, q, 2.0, None, ALU.mult))
        for m in MIDS[3:]:
            done(dve.scalar_tensor_tensor(out=q, in0=ab, scalar=m, in1=q, op0=ALU.is_gt, op1=ALU.add))
        done(dve.scalar_tensor_tensor(out=q, in0=q, scalar=0.5, in1=self.sg[:, :], op0=ALU.mult, op1=ALU.mult))
        done(dve.tensor_tensor(self.blocks(dst), self.blocks(q), bc(self.amax[:, :]), ALU.mult))
        assert count[0] == self.STEPS


def static_wait(eng, sem, n):
    eng.wait_ge(sem, n)


def layer3_ffn(k, W):
    nc, ps = k.nc, k.ps
    I = 352
    PARTS = [(0, P), (P, P), (2 * P, I - 2 * P)]
    with ExitStack() as ctx:
        wgu, wd = W("f3_gu"), W("f3_down")
        wt = k.sb(ctx, "f3_wt", [P, 6, P])
        wdt = k.sb(ctx, "f3_wdt", [P, 3, P])
        xq = k.sb(ctx, "f3_xq", [P, T])
        NW = 6 * P + I
        allw = k.sb(ctx, "f3_wq", [P, NW])
        with ExitStack() as sub:
            fq = Fp4(k, sub, "f3w", NW // 16)
            turned, out = k.sems(ctx, "f3w_", "turned out")
            with nc.Block() as block:

                @block.vector
                def _(dve):
                    fq.vector(dve, static_wait, 0, k.w3[:, 0:NW], allw[:, :])

                @block.scalar
                def _(act):
                    fq.scalar(act, static_wait, 0)
                    act.wait_ge(turned, 1)
                    act.activation(wt[:, :, :].rearrange("p m c -> p (m c)"), ps[:, 0:2, 0:3 * P], ACT.Copy)
                    act.activation(wdt[:, 0:2, :], ps[:, 2, 0:2 * P].rearrange("p (m c) -> p m c", m=2), ACT.Copy)
                    act.activation(wdt[0:96, 2, :], ps[0:96, 3, 0:P], ACT.Copy)

                @block.tensor
                def _(pe):
                    pe.wait_ge(fq.step, fq.STEPS)
                    for m in range(6):
                        pe.transpose(ps[:, m // 3, tile(m % 3)], allw[:, tile(m)], k.ident[:, :])
                    for m, (a, n) in enumerate(PARTS):
                        mm = pe.transpose(ps[0:n, 2 if m < 2 else 3, tile(m if m < 2 else 0)], allw[:, 6 * P + a:6 * P + a + n], k.ident[:, :])
                    mm.then_inc(turned, 1)
        with ExitStack() as sub:
            fq = Fp4(k, sub, "f3x", T // 16)
            turned, copied, back = k.sems(ctx, "f3x_", "turned copied back")
            with nc.Block() as block:

                @block.tensor
                def _(pe):
                    for t in range(NT):
                        mm = pe.transpose(ps[:, t // 4, tile(t % 4)], k.xn[:, tile(t)], k.ident[:, :])
                    mm.then_inc(turned, 1)
                    pe.wait_ge(fq.step, fq.STEPS)
                    for t in range(NT):
                        mm = pe.transpose(ps[:, 4 + t // 4, tile(t % 4)], k.t1[:, tile(t)], k.ident[:, :])
                    mm.then_inc(back, 1)

                @block.vector
                def _(dve):
                    dve.wait_ge(turned, 1)
                    fq.vector(dve, static_wait, 0, ps[:, 0:4, :].rearrange("p a b -> p (a b)"), k.t1[:, :])

                @block.scalar
                def _(act):
                    fq.scalar(act, static_wait, 0)
                    act.wait_ge(back, 1)
                    act.activation(xq[:, :], ps[:, 4:8, :].rearrange("p a b -> p (a b)"), ACT.Copy)
        xs = k.sb(ctx, "f3_xs", [P, CH])
        sg = k.sb(ctx, "f3_sg", [P, 4, I])
        h = k.sb(ctx, "f3_h", [P, 4 * I])
        ht = k.sb(ctx, "f3_ht", [P, 3, CH])
        fq = Fp4(k, ctx, "f3h", 4 * I // 16)
        x_in, prod, silu, hid, turned, ht_done, y, added = k.sems(ctx, "f3l_", "x_in prod silu hid turned ht y added")
        h4 = h[:, :].rearrange("p (t i) -> p t i", t=4)
        with nc.Block() as block:

            @block.scalar
            def _(act):
                with act.Fori(0, NCH) as i:
                    k.hold(act, added, i + 1)
                    act.activation(xs[:, :], xq[:, bass.ds(i * CH, CH)], ACT.Copy).then_inc(x_in, 1)
                    k.hold(act, prod, i + 1)
                    act.activation(sg[:, :, :], ps[:, 0:4, 0:I], ACT.Silu).then_inc(silu, 1)
                    fq.scalar(act, k.hold, i)
                    k.hold(act, turned, i + 1)
                    act.activation(ht[:, 0:2, :], ps[:, 0:2, :], ACT.Copy).then_inc(ht_done, 1)
                    act.activation(ht[0:96, 2, :], ps[0:96, 2, :], ACT.Copy).then_inc(ht_done, 1)

            @block.tensor
            def _(pe):
                with pe.Fori(0, NCH) as i:
                    k.hold(pe, x_in, i + 1)
                    for t in range(4):
                        pe.matmul(ps[:, t, 0:I], xs[:, tile(t)], wt[:, 0:3, :].rearrange("p m c -> p (m c)")[:, 0:I], start=True, stop=True)
                        mm = pe.matmul(ps[:, 4 + t, 0:I], xs[:, tile(t)], wt[:, 3:6, :].rearrange("p m c -> p (m c)")[:, 0:I], start=True, stop=True)
                    mm.then_inc(prod, 1)
                    k.hold(pe, fq.step, (i + 1) * fq.STEPS)
                    for m, (a, n) in enumerate(PARTS):
                        for t in range(4):
                            mm = pe.transpose(ps[0:n, m, tile(t)], h4[:, t, a:a + n], k.ident[:, :])
                    mm.then_inc(turned, 1)
                    k.hold(pe, ht_done, 2 * i + 2)
                    for m, (a, n) in enumerate(PARTS):
                        mm = pe.matmul(ps[:, 3, :], wdt[0:n, m, :], ht[0:n, m, :], start=(m == 0), stop=(m == 2))
                    mm.then_inc(y, 1)

            @block.vector
            def _(dve):
                dve.sem_inc(added, 1)
                with dve.Fori(0, NCH) as i:
                    k.hold(dve, silu, i + 1)
                    dve.tensor_tensor(h4, sg[:, :, :], ps[:, 4:8, 0:I], ALU.mult).then_inc(hid, 1)
                    k.hold(dve, hid, i + 1)
                    fq.vector(dve, k.hold, i, h[:, :], h[:, :])
                    k.hold(dve, y, i + 1)
                    dve.tensor_tensor(k.x[:, bass.ds(i * CH, CH)], k.x[:, bass.ds(i * CH, CH)], ps[:, 3, :], ALU.add).then_inc(added, 1)


def more_layouts(np, a, L, f, col, kt, three, choose, eh):
    g = lambda n: f(a["L2_attn_" + n])
    L["a2"] = dict(a2_wo=kt(g("Wo")), a2_bo=col(g("bo")), a2_g=col(g("gamma")), a2_b=col(g("beta")),
                   a2_lam=np.full((128, 1), g("lam"), np.float32))
    wq, wk, wv, bq, bk, bv = (g(n) for n in ("Wq", "Wk", "Wv", "bq", "bk", "bv"))
    pairs = {}
    for p in range(8):
        two = slice(2 * p, 2 * p + 2)
        side = lambda v: v[two].transpose(1, 0, 2).reshape(128, -1)
        pairs[f"pair{p}"] = np.concatenate([side(wq), side(wk), side(wv), bq[two].T, bk[two].T,
                                            np.concatenate([bv[two].T, np.zeros((64, 2), np.float32)])], axis=1)
    L["a2w"] = pairs
    g = lambda n: f(a["L2_ffn_" + n])
    two = lambda v: v.reshape(32, 2, 128, 64).transpose(2, 0, 1, 3).reshape(128, 32, 128)
    sel = np.zeros((64, 32, 128), np.float32)
    for e in range(64):
        sel[e, e // 2, 64 * (e % 2):64 * (e % 2) + 64] = 1
    L["f2"] = dict(f2_router=g("router_w"), f2_gate=two(g("gate_w")), f2_up=two(g("up_w")),
                   f2_down=g("down_w").reshape(32, 128, 128).transpose(1, 0, 2), f2_sg=g("shared_gate_w"),
                   f2_su=g("shared_up_w"), f2_sd=g("shared_down_w"), f2_sel=sel)
    g = lambda n: f(a["L3_attn_" + n])
    L["a3"] = dict(a3_in=g("W_in"), a3_conv=np.stack([g("conv_x_k")[:, 0, :].T, g("conv_z_k")[:, 0, :].T], axis=1),
                   a3_bc=three(g("W_xproj")[:, 8:40]), a3_dtr=g("W_xproj")[:, 0:8], a3_dt_w=g("W_dt"), a3_dt_b=col(g("b_dt")),
                   a3_alog=g("A_log"), a3_D=col(g("D")), a3_out=kt(g("W_out")), a3_bout=col(g("b_out")))
    g = lambda n: f(a["L3_ffn_" + n])

    def rows(v):
        out = np.zeros((384, 128), np.float32)
        out[:352] = v
        return out.reshape(3, 128, 128).transpose(1, 0, 2)

    L["f3"] = dict(f3_gu=np.concatenate([rows(g("w_gate")), rows(g("w_up"))], axis=1), f3_down=g("w_down"))


def program(nc, views, x_dram, sel_dram, out_dram):
    with ExitStack() as ctx:
        k = Kit(nc, ctx, views)
        x_loaded, consts, turned, stored = k.sems(ctx, "main_", "x_loaded consts turned stored")
        with nc.Block() as block:

            @block.sync
            def _(sp):
                sp.dma_start(k.x[:, :], x_dram).then_inc(x_loaded, 16)
                sp.dma_start(k.sel[:, :, :], sel_dram).then_inc(x_loaded, 16)
                sp.wait_ge(x_loaded, 32)

            @block.gpsimd
            def _(pool):
                pool.memset(k.ones[:, :], 1.0 / P)
                pool.memset(k.eps5[:, :], 1e-5)
                pool.memset(k.eps6[:, :], 1e-6)
                pool.memset(k.ident[:, :], 0.0).then_inc(consts, 1)
                pool.wait_ge(consts, 1)
                pool.affine_select(out=k.ident[:, :], in_=k.ident[:, :], compare_op=ALU.not_equal, fill=1.0, base=0,
                                   pattern=[[-1, P]], channel_multiplier=1)

        for n, (attn, ffn) in enumerate(((layer0_attn, layer0_ffn), (layer1_attn, layer1_ffn), (layer2_attn, layer2_ffn),
                                         (layer3_attn, layer3_ffn))):
            if n not in LAYERS:
                continue
            layer_norm(k, k.x, k.xn, k.eps5)
            for part, half in ((attn, "a"), (ffn, "f")):
                with ExitStack() as sub:
                    k.ctx, k.counted = sub, []
                    part(k, load(k, sub, f"{half}{n}"))
                    k.clear_counts()
        with nc.Block() as block:

            @block.sync
            def _(sp):
                sp.dma_start(out_dram, k.x[:, :]).then_inc(stored, 16)
                sp.wait_ge(stored, 16)


def layouts(np, a):
    f = lambda v: np.asarray(v)
    col = lambda v: f(v).reshape(-1, 128).T
    kt = lambda v: f(v).reshape(-1, 128, f(v).shape[-1]).transpose(1, 0, 2)

    def three(v):
        return np.concatenate([kt(v)] * 3, axis=2)

    def choose(n, m):
        out = np.zeros((n, m, 128), np.float32)
        for r in range(n):
            out[r, r * m // n, :] = 1.0
        return out

    L = {}
    g = lambda n: f(a["L0_attn_" + n])
    xp = g("x_proj_w").T
    L["a0"] = dict(a0_norm_w=col(g("norm_w")), a0_norm_b=col(g("norm_b")), a0_in=g("in_proj_w").T,
                   a0_conv=g("conv_w").transpose(1, 2, 0).reshape(2, 128, 4, 256).transpose(1, 2, 0, 3).reshape(128, 8, 256),
                   a0_conv_b=col(g("conv_b")), a0_bc=three(xp[:, 1:33]), a0_ds=kt(np.repeat(xp[:, 0:1], 128, axis=1)),
                   a0_dt_w=col(g("dt_w")), a0_dt_b=col(g("dt_b")), a0_out=kt(g("out_proj_w").T))
    g = lambda n: f(a["L0_ffn_" + n])
    eh = lambda v, m: v.reshape(v.shape[0], m, 128).transpose(2, 0, 1)
    L["f0"] = dict(f0_gate=g("gate_w"), f0_w1=g("w1").transpose(1, 0, 2), f0_b1=eh(g("b1"), 2), f0_g=eh(g("ln1_g"), 2),
                   f0_b=eh(g("ln1_b"), 2), f0_w2=g("w2").reshape(16, 128, 128).transpose(1, 0, 2), f0_b2=g("b2").T,
                   f0_ln_g=col(g("ln_g")), f0_ln_b=col(g("ln_b")), f0_sel=choose(8, 8))
    g = lambda n: f(a["L1_attn_" + n])
    L["a1"] = dict(a1_norm_w=col(g("norm_w")), a1_in=g("in_proj_w"), a1_conv=g("conv_w")[:, 0, :].reshape(2, 128, 4).transpose(1, 0, 2),
                   a1_dt_w=kt(g("dt_w")), a1_dt_b=col(g("dt_b")), a1_alog=kt(g("A_log")),
                   a1_bc=three(np.concatenate([g("B_w"), g("C_w")], axis=1)), a1_D=col(g("D_skip")), a1_out=kt(g("out_proj_w")))
    g = lambda n: f(a["L1_ffn_" + n])
    L["f1"] = dict(f1_gate=g("gate_W"), f1_w1=g("W1").reshape(8, 128, 4, 128).transpose(1, 0, 2, 3).reshape(128, 32, 128),
                   f1_b1=eh(g("b1"), 4), f1_w2=g("W2").reshape(32, 128, 128).transpose(1, 0, 2), f1_b2=g("b2").T,
                   f1_sw=g("shared_W"), f1_sb=col(g("shared_b")), f1_g=col(g("gamma")), f1_b=col(g("beta")), f1_sel=choose(8, 8))
    more_layouts(np, a, L, f, col, kt, three, choose, eh)
    return L


def kernel(**inputs):
    import numpy as _np
    import concourse.bacc as _bacc
    from concourse import mybir as _mybir
    from concourse.bass_utils import run_bass_kernel_spmd as _run

    nc = _bacc.Bacc("TRN2", target_bir_lowering=False, num_devices=1)
    arrays, views = {}, {}
    for name, parts in layouts(_np, inputs).items():
        cols, places, blocks = 0, {}, []
        for part, v in parts.items():
            places[part] = (cols, v.shape)
            v = v.reshape(v.shape[0], -1)
            full = _np.zeros((128, v.shape[1]), _np.float32)
            full[:v.shape[0]] = v
            blocks.append(full)
            cols += v.shape[1]
        packed = _np.ascontiguousarray(_np.concatenate(blocks, axis=1))
        arrays[f"in_{name}_dram"] = packed
        views[name] = (nc.dram_tensor(f"in_{name}_dram", packed.shape, _mybir.dt.float32, kind="ExternalInput").ap(), places)
    x = _np.ascontiguousarray(_np.asarray(inputs["L0_attn_x"]).reshape(2048, 128).T)
    arrays["in_x_dram"] = x
    x_dram = nc.dram_tensor("in_x_dram", x.shape, _mybir.dt.float32, kind="ExternalInput").ap()
    sel = _np.zeros((96, 32, 128), _mybir.dt.np(_mybir.dt.bfloat16))
    for r in range(96):
        sel[r, r % 32, :] = 1
    arrays["in_sel_dram"] = sel
    sel_dram = nc.dram_tensor("in_sel_dram", sel.shape, _mybir.dt.bfloat16, kind="ExternalInput").ap()
    out_dram = nc.dram_tensor("out_0_dram", (128, 2048), _mybir.dt.float32, kind="ExternalOutput").ap()
    program(nc, views, x_dram, sel_dram, out_dram)
    r = _run(nc, [arrays], core_ids=[0])
    return _np.ascontiguousarray(r.results[0]["out_0_dram"].T).reshape(2, 1024, 128)
```

```python
from contextlib import ExitStack

import concourse.bass as bass
from concourse import mybir

ALU = mybir.AluOpType
ACT = mybir.ActivationFunctionType
AX = mybir.AxisListType
F32 = mybir.dt.float32
BF16 = mybir.dt.bfloat16
I32 = mybir.dt.int32

P = 128
NB, SEQ = 2, 1024
T = NB * SEQ
CH = 512
NCH = T // CH
NT = T // P
NS = 16
DI = 2
NE = 8


def chunk(j):
    return slice(CH * j, CH * j + CH)


def tile(t):
    return slice(P * t, P * t + P)


class Kit:

    def __init__(self, nc, ctx, views):
        self.nc, self.ctx, self.views, self.norms = nc, ctx, views, 0
        self.counted = []
        self.x = self.sb(ctx, "x", [P, T])
        self.xn = self.sb(ctx, "xn", [P, T])
        self.t1 = self.sb(ctx, "t1", [P, T])
        self.t2 = self.sb(ctx, "t2", [P, T])
        self.t3 = self.sb(ctx, "t3", [P, T])
        self.ones = self.sb(ctx, "ones", [P, P])
        self.ident = self.sb(ctx, "ident", [P, P])
        self.eps5 = self.sb(ctx, "eps5", [P, 1])
        self.eps6 = self.sb(ctx, "eps6", [P, 1])
        self.sel = self.sb(ctx, "sel", [96, 2 * NS, P], BF16)
        self.ps = ctx.enter_context(nc.psum_tensor("ps", [P, 8, CH], F32))
        self.pad = self.sem(ctx, "loop_wait_carrier")
        self.ln = {n: self.sem(ctx, "ln_" + n) for n in ("mean", "centred", "squared", "var", "log", "rstd", "out")}

    def sb(self, ctx, name, shape, dt=F32):
        return ctx.enter_context(self.nc.sbuf_tensor(name, shape, dt))

    def sem(self, ctx, name):
        s = ctx.enter_context(self.nc.semaphore(name))
        if ctx is self.ctx:
            self.counted.append(s)
        return s

    def clear_counts(self):
        with self.nc.Block() as block:

            @block.gpsimd
            def _(pool):
                for s in self.counted:
                    pool.sem_clear(s)

    def sems(self, ctx, prefix, names):
        return [self.sem(self.ctx, prefix + n) for n in names.split()]

    def hold(self, eng, sem, count):
        eng.wait_ge(sem, count)
        eng.sem_inc(self.pad, 1)


def layer_norm(k, src, dst, eps, gain=None, bias=None, rms=False):
    base = 4 * k.norms
    k.norms += 1
    ln, ps = k.ln, k.ps
    cen = src if rms else k.t1
    with k.nc.Block() as block:

        @block.tensor
        def _(pe):
            for j in range(NCH):
                if not rms:
                    pe.matmul(ps[:, j, :], k.ones[:, :], src[:, chunk(j)], start=True, stop=True).then_inc(ln["mean"], 1)
            for j in range(NCH):
                pe.wait_ge(ln["squared"], base + j + 1)
                pe.matmul(ps[:, 4 + j, :], k.ones[:, :], k.t2[:, chunk(j)], start=True, stop=True).then_inc(ln["var"], 1)
            if rms:
                pe.sem_inc(ln["mean"], 4)

        @block.scalar
        def _(act):
            for j in range(NCH):
                if not rms:
                    act.wait_ge(ln["centred"], base + j + 1)
                act.activation(k.t2[:, chunk(j)], cen[:, chunk(j)], ACT.Square).then_inc(ln["squared"], 1)
            for j in range(NCH):
                act.wait_ge(ln["var"], base + j + 1)
                act.activation(k.t3[:, chunk(j)], ps[:, 4 + j, :], ACT.Ln, bias=eps[:, 0:1]).then_inc(ln["log"], 1)
                act.wait_ge(ln["log"], base + j + 1)
                act.activation(k.t3[:, chunk(j)], k.t3[:, chunk(j)], ACT.Exp, scale=-0.5).then_inc(ln["rstd"], 1)

        @block.vector
        def _(dve):
            for j in range(NCH):
                if not rms:
                    dve.wait_ge(ln["mean"], base + j + 1)
                    dve.tensor_tensor(k.t1[:, chunk(j)], src[:, chunk(j)], ps[:, j, :], ALU.subtract).then_inc(ln["centred"], 1)
            for j in range(NCH):
                dve.wait_ge(ln["rstd"], base + j + 1)
                if gain is None:
                    dve.tensor_tensor(dst[:, chunk(j)], cen[:, chunk(j)], k.t3[:, chunk(j)], ALU.mult).then_inc(ln["out"], 1)
                else:
                    dve.scalar_tensor_tensor(out=dst[:, chunk(j)], in0=cen[:, chunk(j)], scalar=gain,
                                             in1=k.t3[:, chunk(j)], op0=ALU.mult, op1=ALU.mult).then_inc(ln["out"], 1)
            if bias is not None:
                dve.wait_ge(ln["out"], base + 4)
                dve.tensor_scalar(dst[:, :], dst[:, :], bias, None, ALU.add)
            if rms:
                dve.sem_inc(ln["centred"], 4)


def load(k, ctx, name):
    src, places = k.views[name]
    w = k.sb(ctx, "w_" + name, [P, src.shape[1]])
    loaded = k.sem(k.ctx, "loaded_" + name)
    with k.nc.Block() as block:

        @block.sync
        def _(sp):
            sp.dma_start(w[:, :], src).then_inc(loaded, 16)
            sp.wait_ge(loaded, 16)

    k.w3 = w

    def get(n):
        a, shape = places[n]
        cols = 1
        for d in shape[1:]:
            cols *= d
        v = w[0:shape[0], a:a + cols]
        if len(shape) == 3:
            v = v.rearrange("p (a b) -> p a b", b=shape[2])
        if len(shape) == 4:
            v = v.rearrange("p (a b c) -> p a b c", b=shape[2], c=shape[3])
        return v

    return get


def split_rows(k, ctx, bc3, name):
    s = k.sem(k.ctx, "split_" + name)
    mid = k.t2[0:96, :].bitcast(BF16)[:, 0:T]
    rest = k.t1[0:96, :]
    rows = k.ps[0:96, 0:4, :].rearrange("p a b -> p (a b)")
    return s, mid, rest, rows


def split_steps(dve, k, s, mid, rest, rows, bc3):
    dve.tensor_copy(bc3[:, :], rows).then_inc(s, 1)
    dve.wait_ge(s, 1)
    dve.tensor_tensor(rest, rows, bc3[:, :], ALU.subtract).then_inc(s, 1)
    dve.wait_ge(s, 2)
    dve.tensor_copy(mid, rest).then_inc(s, 1)
    dve.wait_ge(s, 3)
    dve.tensor_tensor(rest, rest, mid, ALU.subtract).then_inc(s, 1)
    dve.tensor_copy(bc3[32:64, :], mid[32:64, :])
    dve.wait_ge(s, 4)
    dve.tensor_copy(bc3[64:96, :], rest[64:96, :])


def softplus_steps(dve, k, dt, low, up, upped, soft, n, summed, m):
    dve.tensor_scalar(up[:, :], low[:, :], 1.0, None, ALU.add).then_inc(upped, 1)
    dve.wait_ge(upped, 2 * m + 1)
    dve.scalar_tensor_tensor(out=low[:, :], in0=up[:, :], scalar=-1.0, in1=low[:, :], op0=ALU.add,
                             op1=ALU.subtract).then_inc(upped, 1)
    dve.wait_ge(upped, 2 * m + 2)
    dve.wait_ge(soft, n)
    dve.scalar_tensor_tensor(out=k.t3[:, :], in0=up[:, :], scalar=1.0, in1=k.t3[:, :], op0=ALU.is_gt,
                             op1=ALU.mult).then_inc(summed, 1)
    dve.wait_ge(summed, 3 * m + 1)
    dve.tensor_tensor(low[:, :], k.t3[:, :], low[:, :], ALU.subtract).then_inc(summed, 1)
    dve.wait_ge(summed, 3 * m + 2)
    dve.tensor_tensor(dt, dt, low[:, :], ALU.add).then_inc(summed, 1)
    dve.wait_ge(summed, 3 * m + 3)


def scan_loop(k, ctx, name, halves, u, bc3, finish, decay=None, dt=None, rate=None):
    nc, ps = k.nc, k.ps
    w = k.sb(ctx, name + "_w", [P, 2, halves, SEQ])
    h = k.sb(ctx, name + "_h", [P, 2, halves, SEQ])
    hc = k.sb(ctx, name + "_hc", [P, 2, halves, SEQ])
    cs = k.sb(ctx, name + "_c", [P, 2, SEQ])
    a = k.sb(ctx, name + "_a", [P, 2, halves, SEQ]) if dt is not None else None
    b_ready, c_ready, w_done, scanned, cs_done, hc_done, summed, y_out, a_done = k.sems(
        ctx, name + "_", "b_ready c_ready w_done scanned cs_done hc_done summed y_out a_done")
    H = halves
    bank_b, bank_c, bank_y = 0, 2, 4

    def spread(bank):
        return ps[:, bank:bank + 2, :].rearrange("p a b -> p (a b)")

    with nc.Block() as block:

        @block.tensor
        def _(pe):
            pe.sem_inc(summed, 2 * H)

            def add_state(b, s):
                for hf in range(H):
                    k.hold(pe, hc_done, (b * NS + s) * H + hf + 1 + 2 * H)
                    if s == 0 and hf == 0:
                        k.hold(pe, y_out, b * H + 1)
                    for q in range(2):
                        mm = pe.matmul(ps[:, bank_y + 2 * hf + q, :], k.ident[:, :], hc[:, s % 2, hf, chunk(q)],
                                       start=(s == 0), stop=(s == NS - 1))
                    mm.then_inc(summed, 1)

            with pe.Fori(0, NB) as b:
                for s in range(NS + 1):
                    if s < NS:
                        g = b * NS + s
                        k.hold(pe, w_done, g * H + H)
                        for q in range(2):
                            mm = pe.matmul(ps[:, bank_b + q, :], k.sel[:, s, :], bc3[:, bass.ds(b * SEQ + CH * q, CH)],
                                           start=True, stop=True)
                        mm.then_inc(b_ready, 1)
                        k.hold(pe, cs_done, g + 1)
                        for q in range(2):
                            mm = pe.matmul(ps[:, bank_c + q, :], k.sel[:, NS + s, :],
                                           bc3[:, bass.ds(b * SEQ + CH * q, CH)], start=True, stop=True)
                        mm.then_inc(c_ready, 1)
                    if s >= 1:
                        add_state(b, s - 1)

        @block.scalar
        def _(act):
            act.sem_inc(cs_done, 1)
            with act.Fori(0, NB) as b:
                for s in range(NS):
                    g = b * NS + s
                    if dt is not None:
                        for hf in range(H):
                            k.hold(act, w_done, (g * H + hf) + 1)
                            k.hold(act, hc_done, g * H + hf + 1)
                            act.activation(a[:, s % 2, hf, :], dt[:, hf, bass.ds(b * SEQ, SEQ)], ACT.Exp,
                                           scale=rate[:, hf, s:s + 1]).then_inc(a_done, 1)
                    k.hold(act, c_ready, g + 1)
                    k.hold(act, hc_done, g * H + H)
                    act.activation(cs[:, s % 2, :], spread(bank_c), ACT.Copy).then_inc(cs_done, 1)

        @block.vector
        def _(dve):
            dve.sem_inc(w_done, H)
            dve.sem_inc(y_out, 1)
            with dve.Fori(0, NB) as b:
                for s in range(NS):
                    g = b * NS + s
                    k.hold(dve, b_ready, g + 1)
                    for hf in range(H):
                        dve.tensor_tensor(w[:, s % 2, hf, :], u[:, hf, bass.ds(b * SEQ, SEQ)], spread(bank_b),
                                          ALU.mult).then_inc(w_done, 1)
                    for hf in range(H):
                        k.hold(dve, w_done, g * H + hf + 1 + H)
                        if dt is not None:
                            k.hold(dve, a_done, g * H + hf + 1)
                        k.hold(dve, hc_done, g * H + hf + 1)
                        d0 = a[:, s % 2, hf, :] if dt is not None else decay[:, hf, bass.ds(b * SEQ, SEQ)]
                        dve.tensor_tensor_scan(h[:, s % 2, hf, :], d0, w[:, s % 2, hf, :], 0.0, ALU.mult,
                                               ALU.add).then_inc(scanned, 1)
                k.hold(dve, summed, (b + 1) * NS * H + 2 * H)
                for hf in range(H):
                    finish(dve, b, hf, spread(bank_y + 2 * hf)).then_inc(y_out, 1)

        @block.gpsimd
        def _(pool):
            pool.sem_inc(hc_done, 2 * H)
            with pool.Fori(0, NB) as b:
                for s in range(NS):
                    g = b * NS + s
                    k.hold(pool, cs_done, g + 2)
                    for hf in range(H):
                        k.hold(pool, scanned, g * H + hf + 1)
                        k.hold(pool, summed, g * H + hf + 1)
                        pool.tensor_tensor(hc[:, s % 2, hf, :], h[:, s % 2, hf, :], cs[:, s % 2, :],
                                           ALU.mult).then_inc(hc_done, 1)


def route_top2(k, ctx, name, gate, comb_t):
    nc, ps = k.nc, k.ps
    logits = ps[:, 0, 0:NT * NE].rearrange("p (t e) -> p t e", e=NE)
    top = k.sb(ctx, name + "_top", [P, NT, 8])
    shifted = k.sb(ctx, name + "_shifted", [P, NT, NE])
    mask = k.sb(ctx, name + "_mask", [P, NT, NE])
    ex = k.sb(ctx, name + "_ex", [P, NT, NE])
    total = k.sb(ctx, name + "_total", [P, NT])
    logit, topped, shift, masked, expd, kept, summed, inv, comb, turned = k.sems(
        ctx, name + "_", "logit topped shift masked expd kept summed inv comb turned")
    with nc.Block() as block:

        @block.tensor
        def _(pe):
            for t in range(NT):
                mm = pe.matmul(logits[:, t, :], k.xn[:, tile(t)], gate, start=True, stop=True)
            mm.then_inc(logit, 1)
            pe.wait_ge(comb, 1)
            for t in range(NT):
                mm = pe.transpose(ps[0:NE, 1 + t // 4, P * (t % 4):P * (t % 4) + P], mask[:, t, :], k.ident[:, :])
            mm.then_inc(turned, 1)

        @block.vector
        def _(dve):
            dve.wait_ge(logit, 1)
            for t in range(NT):
                dve.max(top[:, t, :], logits[:, t, :]).then_inc(topped, 1)
            dve.wait_ge(topped, NT)
            dve.tensor_tensor(shifted[:, :, :], logits, top[:, :, 0:1].to_broadcast([P, NT, NE]), ALU.subtract).then_inc(shift, 1)
            dve.tensor_tensor(mask[:, :, :], logits, top[:, :, 1:2].to_broadcast([P, NT, NE]), ALU.is_ge).then_inc(masked, 1)
            dve.wait_ge(expd, 1)
            dve.wait_ge(masked, 1)
            dve.tensor_tensor(ex[:, :, :], ex[:, :, :], mask[:, :, :], ALU.mult).then_inc(kept, 1)
            dve.wait_ge(kept, 1)
            dve.tensor_reduce(total[:, :], ex[:, :, :], AX.X, ALU.add).then_inc(summed, 1)
            dve.wait_ge(summed, 1)
            dve.reciprocal(total[:, :], total[:, :]).then_inc(inv, 1)
            dve.wait_ge(inv, 1)
            dve.tensor_tensor(mask[:, :, :], ex[:, :, :], total[:, :].unsqueeze(2).to_broadcast([P, NT, NE]),
                              ALU.mult).then_inc(comb, 1)

        @block.scalar
        def _(act):
            act.wait_ge(shift, 1)
            act.activation(ex[:, :, :], shifted[:, :, :], ACT.Exp).then_inc(expd, 1)
            act.wait_ge(turned, 1)
            act.activation(comb_t[:, :], ps[0:NE, 1:5, :].rearrange("p a b -> p (a b)"), ACT.Copy)


def project_out(k, ctx, name, weight, src, extra=None):
    ready, added = k.sems(ctx, name + "_", "ready added")
    with k.nc.Block() as block:

        @block.tensor
        def _(pe):
            for j in range(NCH):
                for hf in range(DI):
                    mm = pe.matmul(k.ps[:, j, :], weight[:, hf, :], src[:, hf, chunk(j)], start=(hf == 0), stop=(hf == DI - 1))
                mm.then_inc(ready, 1)

        @block.vector
        def _(dve):
            for j in range(NCH):
                dve.wait_ge(ready, j + 1)
                dve.tensor_tensor(k.x[:, chunk(j)], k.x[:, chunk(j)], k.ps[:, j, :], ALU.add).then_inc(added, 1)
            if extra is not None:
                dve.wait_ge(added, NCH)
                dve.tensor_tensor(k.x[:, :], k.x[:, :], extra[:, :], ALU.add)


def layer0_attn(k, W):
    nc, ps = k.nc, k.ps
    with ExitStack() as ctx:
        w = {n: W(n) for n in ("a0_norm_w", "a0_norm_b", "a0_in", "a0_conv", "a0_conv_b", "a0_bc", "a0_ds", "a0_dt_w",
                               "a0_dt_b", "a0_out")}
        xn2 = k.t2
        u = k.sb(ctx, "a0_u", [P, DI, T])
        decay = k.sb(ctx, "a0_decay", [P, DI, T])
        sz = k.sb(ctx, "a0_sz", [P, DI, T])
        bc3 = k.sb(ctx, "a0_bc3", [96, T], BF16)
        layer_norm(k, k.xn, xn2, k.eps5, w["a0_norm_w"][:, 0:1], w["a0_norm_b"][:, 0:1])
        with ExitStack() as sub:
            padded = k.sb(sub, "a0_padded", [P, DI, NB, SEQ + 3])
            proj, x_out, z_out = k.sems(ctx, "a0_", "proj x_out z_out")
            with nc.Block() as block:

                @block.tensor
                def _(pe):
                    for m in range(4):
                        for j in range(NCH):
                            n = 4 * m + j
                            if n >= 8:
                                pe.wait_ge(x_out, n - 7)
                            pe.matmul(ps[:, n % 8, :], w["a0_in"][:, tile(m)], xn2[:, chunk(j)], start=True,
                                      stop=True).then_inc(proj, 1)

                @block.vector
                def _(dve):
                    dve.memset(padded[:, :, :, 0:3], 0.0)
                    for n in range(8):
                        dve.wait_ge(proj, n + 1)
                        dve.tensor_copy(padded[:, n // 4, n % 4 // 2, 3 + CH * (n % 2):3 + CH * (n % 2) + CH],
                                        ps[:, n, :]).then_inc(x_out, 1)

                @block.scalar
                def _(act):
                    for n in range(8):
                        act.wait_ge(proj, n + 9)
                        act.activation(sz[:, n // 4, chunk(n % 4)], ps[:, n, :], ACT.Silu).then_inc(z_out, 1)

            conv, = k.sems(ctx, "a0_", "conv")
            with nc.Block() as block:

                @block.tensor
                def _(pe):
                    for m in range(DI):
                        for n in range(4):
                            for hf in range(DI):
                                for tap in range(4):
                                    lo = CH * (n % 2) + tap
                                    mm = pe.matmul(ps[:, 4 * m + n, :], w["a0_conv"][:, tap * DI + hf, tile(m)],
                                                   padded[:, hf, n // 2, lo:lo + CH],
                                                   start=(hf == 0 and tap == 0), stop=(hf == 1 and tap == 3))
                            mm.then_inc(conv, 1)

                @block.scalar
                def _(act):
                    for n in range(8):
                        act.wait_ge(conv, n + 1)
                        act.activation(u[:, n // 4, chunk(n % 4)], ps[:, n, :], ACT.Silu, bias=w["a0_conv_b"][:, n // 4:n // 4 + 1])
        rows, delta, neg = k.sems(ctx, "a0_", "rows delta neg")
        s, mid, rest, psrows = split_rows(k, ctx, bc3, "a0")
        nw = k.sb(ctx, "a0_negw", [P, DI])
        nb = k.sb(ctx, "a0_negb", [P, DI])
        with nc.Block() as block:

            @block.tensor
            def _(pe):
                for weight, bank, done, m in ((w["a0_bc"], 0, rows, 96), (w["a0_ds"], 4, delta, P)):
                    for j in range(NCH):
                        for hf in range(DI):
                            mm = pe.matmul(ps[0:m, bank + j, :], weight[:, hf, :], u[:, hf, chunk(j)], start=(hf == 0),
                                           stop=(hf == 1))
                        mm.then_inc(done, 1)

            @block.vector
            def _(dve):
                dve.tensor_scalar(nw[:, :], w["a0_dt_w"], -1.0, None, ALU.mult).then_inc(neg, 1)
                dve.tensor_scalar(nb[:, :], w["a0_dt_b"], -1.0, None, ALU.mult).then_inc(neg, 1)
                dve.wait_ge(rows, NCH)
                split_steps(dve, k, s, mid, rest, psrows, bc3)

            @block.scalar
            def _(act):
                act.wait_ge(neg, 2)
                act.wait_ge(delta, NCH)
                for hf in range(DI):
                    act.activation(decay[:, hf, :], ps[:, 4:8, :].rearrange("p a b -> p (a b)"), ACT.Sigmoid,
                                   scale=nw[:, hf:hf + 1], bias=nb[:, hf:hf + 1])
        with ExitStack() as sub:
            def finish(dve, b, hf, y):
                return dve.tensor_tensor(sz[:, hf, bass.ds(b * SEQ, SEQ)], sz[:, hf, bass.ds(b * SEQ, SEQ)], y, ALU.mult)

            scan_loop(k, sub, "a0s", DI, u, bc3, finish, decay=decay)
        project_out(k, ctx, "a0p", w["a0_out"], sz, extra=k.xn)


def layer0_ffn(k, W):
    nc, ps = k.nc, k.ps
    HID = 2
    with ExitStack() as ctx:
        w = {n: W(n) for n in ("f0_gate", "f0_w1", "f0_b1", "f0_g", "f0_b", "f0_w2", "f0_b2", "f0_ln_g", "f0_ln_b", "f0_sel")}
        comb_t = k.sb(ctx, "f0_comb_t", [NE, T])
        acc = k.sb(ctx, "f0_acc", [P, T])
        w1c = k.sb(ctx, "f0_w1c", [P, NE, HID * P])
        b1c = k.sb(ctx, "f0_b1c", [P, NE, HID])
        mean = k.sb(ctx, "f0_mean", [P, NE])
        mean2 = k.sb(ctx, "f0_mean2", [P, NE])
        route_top2(k, ctx, "f0r", w["f0_gate"], comb_t)
        wm, wh, wc, bm, bh, acc0 = k.sems(ctx, "f0_", "w_mean w_half w_centred b_mean b_half acc_init")
        with nc.Block() as block:

            @block.tensor
            def _(pe):
                pe.matmul(ps[:, 0, 0:NE * HID], k.ones[:, :], w["f0_b1"].rearrange("p e m -> p (e m)"), start=True,
                          stop=True).then_inc(bm, 1)

            @block.vector
            def _(dve):
                dve.tensor_reduce(mean[:, :], w["f0_w1"], AX.X, ALU.add).then_inc(wm, 1)
                dve.wait_ge(wm, 1)
                dve.tensor_scalar(mean[:, :], mean[:, :], 1.0 / (HID * P), None, ALU.mult).then_inc(wh, 1)
                dve.wait_ge(wh, 1)
                dve.tensor_tensor(w1c[:, :, :], w["f0_w1"], mean[:, :].unsqueeze(2).to_broadcast([P, NE, HID * P]), ALU.subtract)
                dve.wait_ge(bm, 1)
                dve.tensor_reduce(mean2[:, :], ps[:, 0, 0:NE * HID].rearrange("p (e m) -> p e m", m=HID), AX.X, ALU.add).then_inc(bh, 1)
                dve.wait_ge(bh, 1)
                dve.tensor_scalar(mean2[:, :], mean2[:, :], 1.0 / HID, None, ALU.mult).then_inc(bh, 1)
                dve.wait_ge(bh, 2)
                dve.tensor_tensor(b1c[:, :, :], w["f0_b1"], mean2[:, :].unsqueeze(2).to_broadcast([P, NE, HID]), ALU.subtract)

            @block.gpsimd
            def _(pool):
                pool.tensor_copy(acc[:, :], k.xn[:, :])

        hn = k.sb(ctx, "f0_hn", [P, NE, HID, CH])
        sq = k.sb(ctx, "f0_sq", [P, 2, HID, CH])
        rs = k.sb(ctx, "f0_rs", [P, 2, CH])
        gl = k.sb(ctx, "f0_gl", [P, 2, HID, CH])
        yb = k.sb(ctx, "f0_yb", [P, 2, CH])
        tmp = k.sb(ctx, "f0_tmp", [P, 2, CH])
        h_done, sq_done, var_done, log_done, rs_done, hn_done, gl_done, y_done, cb_done, yb_done, tmp_done, acc_done = k.sems(
            ctx, "f0l_", "h sq var log rs hn gl y cb yb tmp acc")
        with nc.Block() as block:

            @block.tensor
            def _(pe):
                pe.sem_inc(var_done, 2)
                pe.sem_inc(y_done, 2)
                with pe.Fori(0, NCH) as i:
                    def hidden(e):
                        for m in range(HID):
                            k.hold(pe, hn_done, (i * NE + e) * HID + m + 1)
                            pe.matmul(ps[:, 2 * (e % 2) + m, :], w1c[:, e, tile(m)], k.xn[:, bass.ds(i * CH, CH)], start=True,
                                      stop=True).then_inc(h_done, 1)

                    def variance(e):
                        k.hold(pe, sq_done, (i * NE + e) * HID + HID)
                        k.hold(pe, log_done, i * NE + e + 1)
                        for m in range(HID):
                            mm = pe.matmul(ps[:, 4 + e % 2, :], k.ones[:, :], sq[:, e % 2, m, :], start=(m == 0), stop=(m == HID - 1))
                        mm.then_inc(var_done, 1)

                    for e in range(NE + 1):
                        if e < NE:
                            hidden(e)
                        if e >= 1:
                            variance(e - 1)
                    for e in range(NE):
                        g = i * NE + e
                        k.hold(pe, tmp_done, g + 1)
                        if e < 2:
                            k.hold(pe, log_done, i * NE + NE + 2)
                        pe.matmul(ps[:, 6 + e % 2, :], w["f0_sel"][:, e, :], comb_t[:, bass.ds(i * CH, CH)], start=True,
                                  stop=True).then_inc(cb_done, 1)
                        k.hold(pe, gl_done, g * HID + HID + NE * HID)
                        k.hold(pe, yb_done, g + 1)
                        for m in range(HID):
                            mm = pe.matmul(ps[:, 4 + e % 2, :], w["f0_w2"][:, e * HID + m, :], gl[:, e % 2, m, :], start=(m == 0),
                                           stop=(m == HID - 1))
                        mm.then_inc(y_done, 1)

            @block.scalar
            def _(act):
                act.sem_inc(log_done, 2)
                act.sem_inc(gl_done, NE * HID)
                act.sem_inc(yb_done, 2)
                with act.Fori(0, NCH) as i:
                    def squares(e):
                        for m in range(HID):
                            k.hold(act, h_done, (i * NE + e) * HID + m + 1)
                            k.hold(act, var_done, i * NE + e + 1)
                            act.activation(sq[:, e % 2, m, :], ps[:, 2 * (e % 2) + m, :], ACT.Square,
                                           bias=b1c[:, e, m:m + 1]).then_inc(sq_done, 1)

                    def rstd(e):
                        g = i * NE + e
                        k.hold(act, var_done, g + 3)
                        k.hold(act, hn_done, g * HID + HID)
                        act.activation(rs[:, e % 2, :], ps[:, 4 + e % 2, :], ACT.Ln, scale=1.0 / HID,
                                       bias=k.eps5[:, 0:1]).then_inc(log_done, 1)
                        k.hold(act, log_done, g + 3)
                        act.activation(rs[:, e % 2, :], rs[:, e % 2, :], ACT.Exp, scale=-0.5).then_inc(rs_done, 1)

                    for e in range(NE + 1):
                        if e < NE:
                            squares(e)
                        if e >= 1:
                            rstd(e - 1)

                    def add_b2(e):
                        g = i * NE + e
                        k.hold(act, y_done, g + 3)
                        k.hold(act, tmp_done, g + 1)
                        act.activation(yb[:, e % 2, :], ps[:, 4 + e % 2, :], ACT.Identity,
                                       bias=w["f0_b2"][:, e:e + 1]).then_inc(yb_done, 1)

                    for e in range(NE + 1):
                        if e < NE:
                            for m in range(HID):
                                k.hold(act, hn_done, (i * NE + e) * HID + m + 1 + 2 * HID)
                                k.hold(act, y_done, i * NE + e + 1)
                                act.activation(gl[:, e % 2, m, :], hn[:, e, m, :], ACT.Gelu, scale=w["f0_g"][:, e, m:m + 1],
                                               bias=w["f0_b"][:, e, m:m + 1]).then_inc(gl_done, 1)
                        if e >= 1:
                            add_b2(e - 1)

            @block.vector
            def _(dve):
                dve.sem_inc(hn_done, 2 * HID)
                dve.sem_inc(tmp_done, 2)
                with dve.Fori(0, NCH) as i:
                    for e in range(NE):
                        g = i * NE + e
                        k.hold(dve, rs_done, g + 1)
                        for m in range(HID):
                            k.hold(dve, gl_done, g * HID + m + 1)
                            dve.scalar_tensor_tensor(out=hn[:, e, m, :], in0=ps[:, 2 * (e % 2) + m, :],
                                                     scalar=b1c[:, e, m:m + 1], in1=rs[:, e % 2, :], op0=ALU.add,
                                                     op1=ALU.mult).then_inc(hn_done, 1)
                    for e in range(NE):
                        g = i * NE + e
                        k.hold(dve, yb_done, g + 3)
                        k.hold(dve, cb_done, g + 1)
                        k.hold(dve, acc_done, g + 1)
                        dve.tensor_tensor(tmp[:, e % 2, :], yb[:, e % 2, :], ps[:, 6 + e % 2, :], ALU.mult).then_inc(tmp_done, 1)

            @block.gpsimd
            def _(pool):
                pool.sem_inc(acc_done, 2)
                with pool.Fori(0, NCH) as i:
                    for e in range(NE):
                        g = i * NE + e
                        k.hold(pool, tmp_done, g + 3)
                        k.hold(pool, acc_done, g + 2)
                        pool.tensor_tensor(acc[:, bass.ds(i * CH, CH)], acc[:, bass.ds(i * CH, CH)], tmp[:, e % 2, :],
                                           ALU.add).then_inc(acc_done, 1)

        layer_norm(k, acc, acc, k.eps5, w["f0_ln_g"][:, 0:1], w["f0_ln_b"][:, 0:1])
        with nc.Block() as block:

            @block.vector
            def _(dve):
                dve.tensor_tensor(k.x[:, :], k.x[:, :], acc[:, :], ALU.add)


def layer1_attn(k, W):
    nc, ps = k.nc, k.ps
    with ExitStack() as ctx:
        w = {n: W(n) for n in ("a1_norm_w", "a1_in", "a1_conv", "a1_dt_w", "a1_dt_b", "a1_alog", "a1_bc", "a1_D", "a1_out")}
        xc = k.sb(ctx, "a1_xc", [P, DI, T])
        dt = k.sb(ctx, "a1_dt", [P, DI, T])
        du = k.sb(ctx, "a1_du", [P, DI, T])
        bc3 = k.sb(ctx, "a1_bc3", [96, T], BF16)
        A = k.sb(ctx, "a1_A", [P, DI, NS])
        layer_norm(k, k.xn, k.t2, k.eps6, w["a1_norm_w"][:, 0:1], rms=True)
        with ExitStack() as sub:
            padded = k.sb(sub, "a1_padded", [P, DI, NB, SEQ + 3])
            gate = k.sb(sub, "a1_gate", [P, DI, T])
            proj, g_out, x_out, zero, conv = k.sems(ctx, "a1_", "proj g_out x_out zero conv")
            with nc.Block() as block:

                @block.tensor
                def _(pe):
                    for m in range(4):
                        for j in range(NCH):
                            n = 4 * m + j
                            if n >= 8:
                                pe.wait_ge(g_out, n - 7)
                            pe.matmul(ps[:, n % 8, :], w["a1_in"][:, tile((m + 2) % 4)], k.t2[:, chunk(j)], start=True,
                                      stop=True).then_inc(proj, 1)

                @block.scalar
                def _(act):
                    for n in range(8):
                        act.wait_ge(proj, n + 1)
                        act.activation(gate[:, n // 4, chunk(n % 4)], ps[:, n, :], ACT.Silu).then_inc(g_out, 1)

                @block.vector
                def _(dve):
                    dve.memset(padded[:, :, :, 0:3], 0.0).then_inc(zero, 1)
                    for n in range(8):
                        dve.wait_ge(proj, n + 9)
                        dve.wait_ge(g_out, n + 1)
                        dve.tensor_tensor(padded[:, n // 4, n % 4 // 2, 3 + CH * (n % 2):3 + CH * (n % 2) + CH],
                                          gate[:, n // 4, chunk(n % 4)], ps[:, n, :], ALU.mult).then_inc(x_out, 1)
                    dve.wait_ge(x_out, 8)
                    dve.wait_ge(zero, 1)
                    for tap in range(4):
                        for hf in range(DI):
                            dst = xc[:, hf, :].rearrange("p (b t) -> p b t", b=NB)
                            src = padded[:, hf, :, tap:tap + SEQ]
                            kern = w["a1_conv"][:, hf, tap:tap + 1]
                            if tap == 0:
                                dve.tensor_scalar(dst, src, kern, None, ALU.mult).then_inc(conv, 1)
                            else:
                                dve.wait_ge(conv, 2 * (tap - 1) + hf + 1)
                                dve.scalar_tensor_tensor(out=dst, in0=src, scalar=kern, in1=dst, op0=ALU.mult,
                                                         op1=ALU.add).then_inc(conv, 1)
        with ExitStack() as sub:
            low = k.sb(sub, "a1_low", [P, T])
            up = k.sb(sub, "a1_up", [P, T])
            upped, = k.sems(ctx, "a1_", "upped")
            pre, rows, soft, aexp, relu_done, logd, summed = k.sems(ctx, "a1_", "pre rows soft aexp relu logd summed")
            s, mid, rest, psrows = split_rows(k, ctx, bc3, "a1")
            with nc.Block() as block:

                @block.tensor
                def _(pe):
                    for j in range(NCH):
                        for hf in range(DI):
                            mm = pe.matmul(ps[0:96, j, :], w["a1_bc"][:, hf, :], xc[:, hf, chunk(j)], start=(hf == 0), stop=(hf == 1))
                        mm.then_inc(rows, 1)
                    for m in range(DI):
                        if m:
                            pe.wait_ge(relu_done, 1)
                            pe.wait_ge(soft, 1)
                        for j in range(NCH):
                            for hf in range(DI):
                                mm = pe.matmul(ps[:, 4 + j, :], w["a1_dt_w"][:, hf, tile(m)], xc[:, hf, chunk(j)], start=(hf == 0),
                                               stop=(hf == 1))
                            mm.then_inc(pre, 1)

                @block.scalar
                def _(act):
                    act.activation(A[:, :, :], w["a1_alog"], ACT.Exp).then_inc(aexp, 1)
                    for m in range(DI):
                        act.wait_ge(pre, NCH * (m + 1))
                        v = ps[:, 4:8, :].rearrange("p a b -> p (a b)")
                        bias = w["a1_dt_b"][:, m:m + 1]
                        if m:
                            act.wait_ge(summed, 3)
                        act.activation(dt[:, m, :], v, ACT.Relu, bias=bias).then_inc(relu_done, 1)
                        act.activation(low[:, :], v, ACT.Abs, bias=bias).then_inc(soft, 1)
                        act.wait_ge(soft, 3 * m + 1)
                        act.activation(low[:, :], low[:, :], ACT.Exp, scale=-1.0).then_inc(soft, 1)
                        act.wait_ge(upped, 2 * m + 1)
                        act.activation(k.t3[:, :], up[:, :], ACT.Ln).then_inc(soft, 1)

                @block.vector
                def _(dve):
                    dve.wait_ge(rows, NCH)
                    split_steps(dve, k, s, mid, rest, psrows, bc3)
                    for m in range(DI):
                        dve.wait_ge(soft, 3 * m + 2)
                        dve.wait_ge(relu_done, m + 1)
                        softplus_steps(dve, k, dt[:, m, :], low, up, upped, soft, 3 * m + 3, summed, m)
                        dve.tensor_tensor(du[:, m, :], dt[:, m, :], xc[:, m, :], ALU.mult)
                    dve.wait_ge(aexp, 1)
                    dve.tensor_scalar(A[:, :, :], A[:, :, :], -1.0, None, ALU.mult)
        with ExitStack() as sub:
            def finish(dve, b, hf, y):
                v = xc[:, hf, bass.ds(b * SEQ, SEQ)]
                return dve.scalar_tensor_tensor(out=v, in0=v, scalar=w["a1_D"][:, hf:hf + 1], in1=y, op0=ALU.mult, op1=ALU.add)

            scan_loop(k, sub, "a1s", DI, du, bc3, finish, dt=dt, rate=A)
        project_out(k, ctx, "a1p", w["a1_out"], xc)


def layer1_ffn(k, W):
    nc, ps = k.nc, k.ps
    HID = 4
    with ExitStack() as ctx:
        w = {n: W(n) for n in ("f1_gate", "f1_w1", "f1_b1", "f1_w2", "f1_b2", "f1_sw", "f1_sb", "f1_g", "f1_b", "f1_sel")}
        comb_t = k.sb(ctx, "f1_comb_t", [NE, T])
        acc = k.sb(ctx, "f1_acc", [P, T])
        route_top2(k, ctx, "f1r", w["f1_gate"], comb_t)
        shared, gelud = k.sems(ctx, "f1_", "shared gelud")
        with nc.Block() as block:

            @block.tensor
            def _(pe):
                for j in range(NCH):
                    pe.matmul(ps[:, j, :], w["f1_sw"], k.xn[:, chunk(j)], start=True, stop=True).then_inc(shared, 1)

            @block.scalar
            def _(act):
                for j in range(NCH):
                    act.wait_ge(shared, j + 1)
                    act.activation(acc[:, chunk(j)], ps[:, j, :], ACT.Gelu, bias=w["f1_sb"][:, 0:1]).then_inc(gelud, 1)

            @block.vector
            def _(dve):
                dve.wait_ge(gelud, NCH)
                dve.tensor_scalar(acc[:, :], acc[:, :], 0.5, None, ALU.mult)

        gl = k.sb(ctx, "f1_gl", [P, 2, HID, CH])
        yb = k.sb(ctx, "f1_yb", [P, 2, CH])
        tmp = k.sb(ctx, "f1_tmp", [P, 2, CH])
        h_done, gl_done, y_done, cb_done, yb_done, tmp_done, acc_done = k.sems(ctx, "f1l_", "h gl y cb yb tmp acc")
        with nc.Block() as block:

            @block.tensor
            def _(pe):
                pe.sem_inc(y_done, 2)
                with pe.Fori(0, NCH) as i:
                    for e in range(NE + 1):
                        if e < NE:
                            for m in range(HID):
                                k.hold(pe, gl_done, (i * NE + e) * HID + m + 1)
                                pe.matmul(ps[:, m, :], w["f1_w1"][:, e * HID + m, :], k.xn[:, bass.ds(i * CH, CH)], start=True,
                                          stop=True).then_inc(h_done, 1)
                        if e >= 1:
                            f, g = e - 1, i * NE + e - 1
                            k.hold(pe, tmp_done, g + 1)
                            pe.matmul(ps[:, 6 + f % 2, :], w["f1_sel"][:, f, :], comb_t[:, bass.ds(i * CH, CH)], start=True,
                                      stop=True).then_inc(cb_done, 1)
                            k.hold(pe, gl_done, g * HID + 2 * HID)
                            k.hold(pe, yb_done, g + 1)
                            for m in range(HID):
                                mm = pe.matmul(ps[:, 4 + f % 2, :], w["f1_w2"][:, f * HID + m, :], gl[:, f % 2, m, :],
                                               start=(m == 0), stop=(m == HID - 1))
                            mm.then_inc(y_done, 1)

            @block.scalar
            def _(act):
                act.sem_inc(gl_done, HID)
                act.sem_inc(yb_done, 2)
                with act.Fori(0, NCH) as i:
                    for e in range(NE + 1):
                        if e < NE:
                            for m in range(HID):
                                k.hold(act, h_done, (i * NE + e) * HID + m + 1)
                                k.hold(act, y_done, i * NE + e + 1)
                                act.activation(gl[:, e % 2, m, :], ps[:, m, :], ACT.Gelu,
                                               bias=w["f1_b1"][:, e, m:m + 1]).then_inc(gl_done, 1)
                        if e >= 1:
                            f, g = e - 1, i * NE + e - 1
                            k.hold(act, y_done, g + 3)
                            k.hold(act, tmp_done, g + 1)
                            act.activation(yb[:, f % 2, :], ps[:, 4 + f % 2, :], ACT.Identity,
                                           bias=w["f1_b2"][:, f:f + 1]).then_inc(yb_done, 1)

            @block.vector
            def _(dve):
                dve.sem_inc(tmp_done, 2)
                with dve.Fori(0, NCH) as i:
                    for e in range(NE):
                        g = i * NE + e
                        k.hold(dve, yb_done, g + 3)
                        k.hold(dve, cb_done, g + 1)
                        k.hold(dve, acc_done, g + 1)
                        dve.tensor_tensor(tmp[:, e % 2, :], yb[:, e % 2, :], ps[:, 6 + e % 2, :], ALU.mult).then_inc(tmp_done, 1)

            @block.gpsimd
            def _(pool):
                pool.sem_inc(acc_done, 2)
                with pool.Fori(0, NCH) as i:
                    for e in range(NE):
                        g = i * NE + e
                        k.hold(pool, tmp_done, g + 3)
                        k.hold(pool, acc_done, g + 2)
                        pool.tensor_tensor(acc[:, bass.ds(i * CH, CH)], acc[:, bass.ds(i * CH, CH)], tmp[:, e % 2, :],
                                           ALU.add).then_inc(acc_done, 1)

        layer_norm(k, acc, acc, k.eps5, w["f1_g"][:, 0:1], w["f1_b"][:, 0:1])
        with nc.Block() as block:

            @block.vector
            def _(dve):
                dve.tensor_tensor(k.x[:, :], k.x[:, :], acc[:, :], ALU.add)

LAYERS = (0, 1, 2, 3)


NH, HD = 16, 64
PAIRS = NH // 2
WQ_AT, WK_AT, WV_AT = 0, 2 * P, 6 * P
BQ_AT, BK_AT, BV_AT = 7 * P, 7 * P + 2, 7 * P + 6
PAIR_COLS = 7 * P + 7
F32R = mybir.dt.float32r


def layer2_attn(k, W):
    nc, ps = k.nc, k.ps
    pairs_dram, _ = k.views["a2w"]
    with ExitStack() as ctx:
        w = {n: W(n) for n in ("a2_wo", "a2_bo", "a2_g", "a2_b", "a2_lam")}
        ocat = k.sb(ctx, "a2_ocat", [P, PAIRS, T])
        wp = k.sb(ctx, "a2_wp", [P, PAIR_COLS])
        bq, bk, bv = wp[:, BQ_AT:BQ_AT + 2], wp[:, BK_AT:BK_AT + 4], wp[:, BV_AT:BV_AT + 1]
        qhl = k.sb(ctx, "a2_qhl", [P, 2, SEQ], F32R)
        kh = k.sb(ctx, "a2_kh", [P, 2, SEQ], F32R)
        kl = k.sb(ctx, "a2_kl", [P, 2, SEQ], F32R)
        v = k.sb(ctx, "a2_v", [P, NB, SEQ // P, P])
        prob = [t[:, :].rearrange("p (a c) -> p a c", a=2) for t in (k.t1, k.t2)]
        turned = k.sb(ctx, "a2_turned", [P, 2, SEQ // P, P])
        oq = k.sb(ctx, "a2_oq", [P, SEQ // P, P])
        negmax = k.sb(ctx, "a2_negmax", [P, 4, 2])
        total = k.sb(ctx, "a2_total", [P, 4, 2])
        inv = k.sb(ctx, "a2_inv", [P, 4, 2])
        ratio = k.sb(ctx, "a2_ratio", [P, 4])
        lam = k.sb(ctx, "a2_lam2", [P, 2])
        bvl = k.sb(ctx, "a2_bvl", [P, 1])
        (w_loaded, w_scaled, proj, high, low, s_ready, max_done, exp_done, inv_done, ratio_done, joined, t_ready,
         t_out, pv_done, o_done, init, bvl_done) = k.sems(
            ctx, "a2_", "w_loaded w_scaled proj high low s_ready max_done exp_done inv_done ratio_done joined t_ready "
            "t_out pv_done o_done init bvl")
        UNITS = [(b, hh) for b in range(NB) for hh in range(2)]
        TILES = 32
        TURNS = TILES + NB

        def banks_of(n):
            out = [("k", a, c, 2 * a + c) for a in range(2) for c in range(2)] + [("q", 0, c, c) for c in range(2)]
            if n % 2 == 0:
                out += [("v", 0, c, 2 + c) for c in range(2)]
            return out

        first = [0, 8, 14, 22, 28]
        BANKS, LOWS = first[4], 24
        OUT_TURN = (17, 33)

        def turn(j):
            return j + (1 if j >= OUT_TURN[0] else 0)

        with nc.Block() as block:

            @block.sync
            def _(sp):
                with sp.Fori(0, PAIRS + 1) as pr:
                    k.hold(sp, high, pr * BANKS + 1)
                    k.hold(sp, low, pr * LOWS + 1)
                    k.hold(sp, bvl_done, pr + 1)
                    sp.dma_start(wp[:, :], pairs_dram[:, bass.ds(pr * PAIR_COLS, PAIR_COLS)]).then_inc(w_loaded, 16)
                sp.wait_ge(w_loaded, 16 * (PAIRS + 1))

            @block.gpsimd
            def _(pool):
                with pool.Fori(0, PAIRS + 1) as pr:
                    k.hold(pool, w_loaded, 16 * (pr + 1))
                    pool.tensor_scalar(wp[:, WQ_AT:WQ_AT + 2 * P], wp[:, WQ_AT:WQ_AT + 2 * P], float(HD) ** -0.5, None, ALU.mult).then_inc(w_scaled, 1)
                    pool.tensor_scalar(bq, bq, float(HD) ** -0.5, None, ALU.mult).then_inc(w_scaled, 1)

            @block.tensor
            def _(pe):
                pe.sem_inc(t_ready, 3)
                pe.sem_inc(pv_done, 2)

                def project(pair, n, after_exp):
                    b, hh = UNITS[n]
                    for idx, (what, a, c, bank) in enumerate(banks_of(n)):
                        if idx >= 4:
                            k.hold(pe, low, pair * LOWS + 6 * n + idx - 4 + 2)
                        elif after_exp is not None:
                            k.hold(pe, exp_done, after_exp + a + 1)
                        at = SEQ * b + CH * c
                        if what == "q":
                            mm = pe.matmul(ps[:, bank, :], wp[:, WQ_AT + P * hh:WQ_AT + P * hh + P], k.xn[:, at:at + CH], start=True, stop=True)
                        elif what == "k":
                            wk = WK_AT + P * (2 * hh + a)
                            mm = pe.matmul(ps[:, bank, :], wp[:, wk:wk + P], k.xn[:, at:at + CH], start=True, stop=True)
                        else:
                            for t in range(4):
                                mm = pe.matmul(ps[:, bank, tile(t)], k.xn[:, at + P * t:at + P * t + P], wp[:, WV_AT:WV_AT + P],
                                               start=True, stop=True)
                        mm.then_inc(proj, 1)

                def scores(pr, j):
                    n, i = j // 8, j % 8
                    if i == 0:
                        k.hold(pe, low, pr * LOWS + 6 * n + 6 + 1)
                        k.hold(pe, high, pr * BANKS + first[n + 1] + 1)
                    for a in range(2):
                        k.hold(pe, exp_done, pr * 64 + 2 * j + a + 1)
                        for c in range(2):
                            pe.matmul(ps[:, 2 * a + c, :], qhl[:, a, tile(i)], kh[:, a, chunk(c)], start=True, stop=False)
                            mm = pe.matmul(ps[:, 2 * a + c, :], qhl[:, a, tile(i)], kl[:, a, chunk(c)], start=False, stop=True)
                        mm.then_inc(s_ready, 1)

                def turn_block(pr, e, block_at):
                    k.hold(pe, t_out, pr * TURNS + e + 1)
                    for c in range(8):
                        mm = pe.transpose(ps[:, 4 + c // 4, tile(c % 4)], block_at(c), k.ident[:, :])
                    mm.then_inc(t_ready, 1)

                def turn_out(pr, b):
                    k.hold(pe, o_done, pr * TILES + 16 * (b + 1) + 2)
                    turn_block(pr, OUT_TURN[b], lambda c: oq[:, c, :])

                def weigh(pr, j):
                    b, hh = UNITS[j // 8]
                    k.hold(pe, t_out, pr * TURNS + turn(j) + 2)
                    k.hold(pe, o_done, pr * TILES + j + 1)
                    for c in range(8):
                        mm = pe.matmul(ps[:, 6 + j % 2, 0:HD], turned[:, j % 2, c, :], v[:, b, c, HD * hh:HD * hh + HD],
                                       start=(c == 0), stop=(c == 7))
                    mm.then_inc(pv_done, 1)

                pe.wait_ge(w_scaled, 2)
                project(0, 0, None)
                with pe.Fori(0, PAIRS) as pr:
                    for j in range(TILES + 3):
                        if j < TILES:
                            scores(pr, j)
                        if j == OUT_TURN[0] + 1:
                            turn_out(pr, 0)
                        if j == TILES + 2:
                            turn_out(pr, 1)
                        if 2 <= j < TILES + 2:
                            weigh(pr, j - 2)
                        if j < TILES and j % 8 == 7:
                            n = j // 8 + 1
                            if n == 4:
                                k.hold(pe, w_scaled, 2 * pr + 4)
                            project(pr + n // 4, n % 4, pr * 64 + 2 * j + 2)
                        if 1 <= j < TILES + 1:
                            k.hold(pe, joined, pr * TILES + j)
                            turn_block(pr, turn(j - 1), lambda c: prob[(j - 1) % 2][:, 0, tile(c)])

            @block.scalar
            def _(act):
                act.sem_inc(exp_done, 2)
                act.sem_inc(t_out, 1)
                act.sem_inc(high, 1)

                def split_high(pair, n):
                    b, hh = UNITS[n]
                    for idx, (what, a, c, bank) in enumerate(banks_of(n)):
                        k.hold(act, proj, pair * BANKS + first[n] + idx + 1)
                        if what == "k":
                            ins = act.activation(kh[:, a, chunk(c)], ps[:, bank, :], ACT.Identity, bias=bk[:, 2 * hh + a:2 * hh + a + 1])
                        elif what == "q":
                            act.activation(qhl[0:HD, 0, chunk(c)], ps[0:HD, bank, :], ACT.Identity, bias=bq[0:HD, hh:hh + 1])
                            ins = act.activation(qhl[HD:P, 1, chunk(c)], ps[HD:P, bank, :], ACT.Identity, bias=bq[HD:P, hh:hh + 1])
                        else:
                            ins = act.activation(v[:, b, 4 * c:4 * c + 4, :], ps[:, bank, :].rearrange("p (t d) -> p t d", t=4), ACT.Copy)
                        ins.then_inc(high, 1)

                split_high(0, 0)
                with act.Fori(0, PAIRS) as pr:
                    for j in range(TILES + 3):
                        if j < TILES:
                            k.hold(act, t_ready, pr * TURNS + (turn(j - 2) + 4 if j >= 2 else j + 1))
                            for a in range(2):
                                k.hold(act, max_done, pr * 64 + 2 * j + a + 1)
                                act.activation(prob[j % 2][:, a, :], ps[:, 2 * a:2 * a + 2, :].rearrange("p a b -> p (a b)"), ACT.Exp,
                                               bias=negmax[:, j % 4, a:a + 1], accum_out=total[:, j % 4, a:a + 1]).then_inc(exp_done, 1)
                        for b in range(NB):
                            if j == (OUT_TURN[0] + 1, TILES + 2)[b]:
                                k.hold(act, t_ready, pr * TURNS + OUT_TURN[b] + 4)
                                k.hold(act, bvl_done, pr + 2)
                                act.activation(ocat[:, bass.ds(pr, 1), SEQ * b:SEQ * b + SEQ].rearrange("p a t -> p (a t)"),
                                               ps[:, 4:6, :].rearrange("p a b -> p (a b)"), ACT.Identity, bias=bvl[:, 0:1]).then_inc(t_out, 1)
                        if j < TILES and j % 8 == 7:
                            n = j // 8 + 1
                            split_high(pr + n // 4, n % 4)
                        if 1 <= j < TILES + 1:
                            k.hold(act, pv_done, pr * TILES + j)
                            k.hold(act, t_ready, pr * TURNS + turn(j - 1) + 4)
                            act.activation(turned[:, (j - 1) % 2, :, :], ps[:, 4:6, :].rearrange("p a (c q) -> p (a c) q", q=P),
                                           ACT.Copy).then_inc(t_out, 1)

            @block.vector
            def _(dve):
                dve.sem_inc(low, 1)
                dve.sem_inc(bvl_done, 1)
                dve.sem_inc(o_done, 2)
                dve.tensor_scalar(lam[:, 0:1], w["a2_lam"], -1.0, None, ALU.mult).then_inc(init, 1)
                dve.tensor_scalar(lam[:, 1:2], w["a2_lam"], -1.0, 1.0, ALU.mult, ALU.add).then_inc(init, 1)
                dve.wait_ge(init, 2)

                def split_low(pair, n):
                    b, hh = UNITS[n]
                    for idx, (what, a, c, bank) in enumerate(banks_of(n)[:6]):
                        k.hold(dve, high, pair * BANKS + first[n] + idx + 2)
                        if what == "k":
                            ins = dve.scalar_tensor_tensor(out=kl[:, a, chunk(c)], in0=ps[:, bank, :], scalar=bk[:, 2 * hh + a:2 * hh + a + 1],
                                                           in1=kh[:, a, chunk(c)].bitcast(F32), op0=ALU.add, op1=ALU.subtract)
                        else:
                            dve.scalar_tensor_tensor(out=qhl[HD:P, 0, chunk(c)], in0=ps[0:HD, bank, :], scalar=bq[0:HD, hh:hh + 1],
                                                     in1=qhl[0:HD, 0, chunk(c)].bitcast(F32), op0=ALU.add, op1=ALU.subtract)
                            ins = dve.scalar_tensor_tensor(out=qhl[0:HD, 1, chunk(c)], in0=ps[HD:P, bank, :], scalar=bq[HD:P, hh:hh + 1],
                                                           in1=qhl[HD:P, 1, chunk(c)].bitcast(F32), op0=ALU.add, op1=ALU.subtract)
                        ins.then_inc(low, 1)

                split_low(0, 0)
                with dve.Fori(0, PAIRS) as pr:
                    for j in range(TILES + 2):
                        if j < TILES:
                            for a in range(2):
                                k.hold(dve, s_ready, pr * 64 + 2 * j + a + 1)
                                dve.tensor_reduce(negmax[:, j % 4, a:a + 1], ps[:, 2 * a:2 * a + 2, :].rearrange("p a b -> p (a b)"),
                                                  AX.X, ALU.max, negate=True).then_inc(max_done, 1)
                        if j == 4:
                            k.hold(dve, w_scaled, 2 * pr + 2)
                            k.hold(dve, t_out, pr * TURNS + 1)
                            dve.tensor_scalar(bvl[:, :], bv, lam[:, 1:2], None, ALU.mult).then_inc(bvl_done, 1)
                        if j >= 2:
                            hh, o = (j - 2) // 8 % 2, j - 2
                            if o % 16 == 0:
                                k.hold(dve, t_ready, pr * TURNS + (OUT_TURN[0] + 4 if o else 3))
                            k.hold(dve, pv_done, pr * TILES + o + 3)
                            dve.tensor_scalar(oq[:, o % 8, HD * hh:HD * hh + HD], ps[:, 6 + o % 2, 0:HD], inv[:, o % 4, 0:1], None,
                                              ALU.mult).then_inc(o_done, 1)
                        if j < TILES:
                            k.hold(dve, exp_done, pr * 64 + 2 * j + 4)
                            dve.reciprocal(inv[:, j % 4, :], total[:, j % 4, :]).then_inc(inv_done, 1)
                            k.hold(dve, inv_done, pr * TILES + j + 1)
                            dve.scalar_tensor_tensor(out=ratio[:, j % 4:j % 4 + 1], in0=inv[:, j % 4, 1:2], scalar=total[:, j % 4, 0:1],
                                                     in1=lam[:, 0:1], op0=ALU.mult, op1=ALU.mult).then_inc(ratio_done, 1)
                            k.hold(dve, ratio_done, pr * TILES + j + 1)
                            dve.scalar_tensor_tensor(out=prob[j % 2][:, 0, :], in0=prob[j % 2][:, 1, :], scalar=ratio[:, j % 4:j % 4 + 1],
                                                     in1=prob[j % 2][:, 0, :], op0=ALU.mult, op1=ALU.add).then_inc(joined, 1)
                            if j % 8 == 7:
                                split_low(pr + (j // 8 + 1) // 4, (j // 8 + 1) % 4)

        y, y_out = k.sems(ctx, "a2_", "y y_out")
        with nc.Block() as block:

            @block.tensor
            def _(pe):
                for j in range(NCH):
                    for pr in range(PAIRS):
                        mm = pe.matmul(ps[:, j, :], w["a2_wo"][:, pr, :], ocat[:, pr, chunk(j)], start=(pr == 0), stop=(pr == PAIRS - 1))
                    mm.then_inc(y, 1)

            @block.scalar
            def _(act):
                for j in range(NCH):
                    act.wait_ge(y, j + 1)
                    act.activation(k.t1[:, chunk(j)], ps[:, j, :], ACT.Identity, bias=w["a2_bo"][:, 0:1])

        layer_norm(k, k.t1[:, :], k.t1[:, :], k.eps5, w["a2_g"][:, 0:1], w["a2_b"][:, 0:1])
        with nc.Block() as block:

            @block.vector
            def _(dve):
                dve.scalar_tensor_tensor(out=k.x[:, :], in0=k.t1[:, :], scalar=1.0 - 0.8, in1=k.x[:, :], op0=ALU.mult, op1=ALU.add)


def layer2_ffn(k, W):
    nc, ps = k.nc, k.ps
    E, GR, CAP, PR = 64, 8, 64, 32
    with ExitStack() as ctx:
        w = {n: W(n) for n in ("f2_router", "f2_gate", "f2_up", "f2_down", "f2_sg", "f2_su", "f2_sd", "f2_sel")}
        comb_t = k.sb(ctx, "f2_comb_t", [E, T])
        with ExitStack() as sub:
            sc = k.sb(sub, "f2_scores", [P, NT, E])
            rep = k.sb(sub, "f2_rep", [P, NT, E])
            mask = k.sb(sub, "f2_mask", [P, NT, E])
            gs = k.sb(sub, "f2_gs", [P, NT, GR])
            gtop = k.sb(sub, "f2_gtop", [P, NT, 8])
            top = k.sb(sub, "f2_top", [P, NT, 8])
            tot = k.sb(sub, "f2_tot", [P, NT])
            logit, scored, step, turned_w, turned_m, copied = k.sems(ctx, "f2r_", "logit scored step turned_w turned_m copied")
            flat = lambda v: v.rearrange("p t e -> p (t e)")
            with nc.Block() as block:

                @block.tensor
                def _(pe):
                    for t in range(NT):
                        mm = pe.matmul(ps[:, t // 8, E * (t % 8):E * (t % 8) + E], k.xn[:, tile(t)], w["f2_router"], start=True, stop=True)
                    mm.then_inc(logit, 1)
                    pe.wait_ge(step, 66)
                    for t in range(NT):
                        mm = pe.transpose(ps[0:E, t // 4, P * (t % 4):P * (t % 4) + P], sc[:, t, :], k.ident[:, :])
                    mm.then_inc(turned_w, 1)
                    for t in range(NT):
                        mm = pe.transpose(ps[0:E, 4 + t // 4, P * (t % 4):P * (t % 4) + P], mask[:, t, :], k.ident[:, :])
                    mm.then_inc(turned_m, 1)

                @block.scalar
                def _(act):
                    act.wait_ge(logit, 1)
                    act.activation(flat(sc[:, :, :]), ps[:, 0:2, :].rearrange("p a b -> p (a b)"), ACT.Sigmoid).then_inc(scored, 1)
                    act.wait_ge(turned_w, 1)
                    act.activation(comb_t[:, :], ps[0:E, 0:4, :].rearrange("p a b -> p (a b)"), ACT.Copy).then_inc(copied, 1)

                @block.vector
                def _(dve):
                    dve.wait_ge(scored, 1)
                    dve.tensor_reduce(flat(gs[:, :, :]), sc[:, :, :].rearrange("p t (g e) -> p (t g) e", g=GR), AX.X, ALU.max).then_inc(step, 1)
                    dve.wait_ge(step, 1)
                    for t in range(NT):
                        dve.max(gtop[:, t, :], gs[:, t, :]).then_inc(step, 1)
                    dve.wait_ge(step, 1 + NT)
                    dve.tensor_tensor(gs[:, :, :], gs[:, :, :], gtop[:, :, 3:4].to_broadcast([P, NT, GR]), ALU.is_ge).then_inc(step, 1)
                    dve.wait_ge(step, 2 + NT)
                    dve.tensor_tensor(sc[:, :, :].rearrange("p t (g e) -> p (t g) e", g=GR),
                                      sc[:, :, :].rearrange("p t (g e) -> p (t g) e", g=GR),
                                      flat(gs[:, :, :]).unsqueeze(2).to_broadcast([P, NT * GR, GR]), ALU.mult).then_inc(step, 1)
                    dve.wait_ge(step, 3 + NT)
                    for t in range(NT):
                        dve.max(top[:, t, :], sc[:, t, :]).then_inc(step, 1)
                    dve.wait_ge(step, 3 + 2 * NT)
                    for t in range(NT):
                        dve.match_replace(out=rep[:, t, :], in_to_replace=top[:, t, :], in_values=sc[:, t, :], imm_value=-1.0).then_inc(step, 1)
                    dve.tensor_reduce(tot[:, :], top[:, :, :], AX.X, ALU.add).then_inc(step, 1)
                    dve.wait_ge(step, 4 + 3 * NT)
                    dve.tensor_scalar(tot[:, :], tot[:, :], 1e-9, None, ALU.max).then_inc(step, 1)
                    dve.tensor_scalar(flat(mask[:, :, :]), flat(rep[:, :, :]), 0.0, None, ALU.is_lt).then_inc(step, 1)
                    dve.wait_ge(step, 6 + 3 * NT)
                    dve.reciprocal(tot[:, :], tot[:, :]).then_inc(step, 1)
                    dve.tensor_tensor(sc[:, :, :], sc[:, :, :], mask[:, :, :], ALU.mult).then_inc(step, 1)
                    dve.wait_ge(step, 8 + 3 * NT)
                    dve.tensor_scalar(tot[:, :], tot[:, :], 2.5, None, ALU.mult).then_inc(step, 1)
                    dve.wait_ge(step, 9 + 3 * NT)
                    dve.tensor_tensor(sc[:, :, :], sc[:, :, :], tot[:, :].unsqueeze(2).to_broadcast([P, NT, E]), ALU.mult).then_inc(step, 9)
                    dve.memset(k.t1[0:E, :], 1.0).then_inc(step, 1)
                    dve.wait_ge(step, 19 + 3 * NT)
                    dve.wait_ge(turned_m, 1)
                    dve.tensor_tensor_scan(k.t2[0:E, :], k.t1[0:E, :], ps[0:E, 4:8, :].rearrange("p a b -> p (a b)"), 0.0,
                                           ALU.mult, ALU.add).then_inc(step, 1)
                    dve.wait_ge(step, 20 + 3 * NT)
                    dve.wait_ge(copied, 1)
                    dve.scalar_tensor_tensor(out=comb_t[:, :], in0=k.t2[0:E, :], scalar=float(CAP), in1=comb_t[:, :],
                                             op0=ALU.is_le, op1=ALU.mult)

        sg = k.sb(ctx, "f2_sgb", [P, 2, CH])
        h1 = k.sb(ctx, "f2_h1", [P, 2, CH])
        hw = k.sb(ctx, "f2_hw", [P, 2, CH])
        g_s, silu_s, h_s, y_s = k.sems(ctx, "f2s_", "gated silu hidden y")
        hs = k.t2[0:HD, :]
        with nc.Block() as block:

            @block.tensor
            def _(pe):
                for j in range(NCH):
                    pe.matmul(ps[0:HD, j, :], w["f2_sg"], k.xn[:, chunk(j)], start=True, stop=True)
                    pe.matmul(ps[0:HD, 4 + j, :], w["f2_su"], k.xn[:, chunk(j)], start=True, stop=True).then_inc(g_s, 1)
                pe.wait_ge(h_s, 1)
                for j in range(NCH):
                    mm = pe.matmul(ps[:, j, :], w["f2_sd"], hs[:, chunk(j)], start=True, stop=True)
                mm.then_inc(y_s, 1)

            @block.scalar
            def _(act):
                act.wait_ge(g_s, NCH)
                act.activation(k.t1[0:HD, :], ps[0:HD, 0:4, :].rearrange("p a b -> p (a b)"), ACT.Silu).then_inc(silu_s, 1)

            @block.vector
            def _(dve):
                dve.wait_ge(silu_s, 1)
                dve.tensor_tensor(hs, k.t1[0:HD, :], ps[0:HD, 4:8, :].rearrange("p a b -> p (a b)"), ALU.mult).then_inc(h_s, 1)
                dve.wait_ge(y_s, 1)
                dve.tensor_tensor(k.x[:, :], k.x[:, :], ps[:, 0:4, :].rearrange("p a b -> p (a b)"), ALU.add)

        gu, cb, silu, mul1, mul2, y_done, y_out = k.sems(ctx, "f2l_", "gu cb silu mul1 mul2 y_done y_out")
        with nc.Block() as block:

            @block.tensor
            def _(pe):
                pe.sem_inc(y_done, 2)
                with pe.Fori(0, NCH) as i:
                    for p in range(PR + 1):
                        if p < PR:
                            g = i * PR + p
                            k.hold(pe, silu, g + 1)
                            k.hold(pe, mul1, g + 1)
                            pe.matmul(ps[:, p % 2, :], w["f2_gate"][:, p, :], k.xn[:, bass.ds(i * CH, CH)], start=True, stop=True)
                            pe.matmul(ps[:, 2 + p % 2, :], w["f2_up"][:, p, :], k.xn[:, bass.ds(i * CH, CH)], start=True,
                                      stop=True).then_inc(gu, 1)
                            k.hold(pe, mul2, g + 1)
                            pe.matmul(ps[:, 4 + p % 2, :], w["f2_sel"][:, p, :], comb_t[:, bass.ds(i * CH, CH)], start=True,
                                      stop=True).then_inc(cb, 1)
                        if p >= 1:
                            f, g = p - 1, i * PR + p - 1
                            k.hold(pe, mul2, g + 3)
                            if f == 0:
                                k.hold(pe, y_out, i + 1)
                            pe.matmul(ps[:, 6, :], w["f2_down"][:, f, :], hw[:, f % 2, :], start=(f == 0),
                                      stop=(f == PR - 1)).then_inc(y_done, 1)

            @block.scalar
            def _(act):
                act.sem_inc(silu, 2)
                with act.Fori(0, NCH) as i:
                    for p in range(PR):
                        g = i * PR + p
                        k.hold(act, gu, g + 1)
                        k.hold(act, mul1, g + 1)
                        act.activation(sg[:, p % 2, :], ps[:, p % 2, :], ACT.Silu).then_inc(silu, 1)

            @block.vector
            def _(dve):
                dve.sem_inc(mul1, 2)
                dve.sem_inc(mul2, 2)
                dve.sem_inc(y_out, 1)
                with dve.Fori(0, NCH) as i:
                    for p in range(PR):
                        g = i * PR + p
                        k.hold(dve, silu, g + 3)
                        k.hold(dve, mul2, g + 1)
                        dve.tensor_tensor(h1[:, p % 2, :], sg[:, p % 2, :], ps[:, 2 + p % 2, :], ALU.mult).then_inc(mul1, 1)
                        k.hold(dve, mul1, g + 3)
                        k.hold(dve, cb, g + 1)
                        k.hold(dve, y_done, g + 1)
                        dve.tensor_tensor(hw[:, p % 2, :], h1[:, p % 2, :], ps[:, 4 + p % 2, :], ALU.mult).then_inc(mul2, 1)
                    k.hold(dve, y_done, (i + 1) * PR + 2)
                    dve.tensor_tensor(k.x[:, bass.ds(i * CH, CH)], k.x[:, bass.ds(i * CH, CH)], ps[:, 6, :], ALU.add).then_inc(y_out, 1)


def layer3_attn(k, W):
    nc, ps = k.nc, k.ps
    with ExitStack() as ctx:
        w = {n: W(n) for n in ("a3_in", "a3_conv", "a3_bc", "a3_dtr", "a3_dt_w", "a3_dt_b", "a3_alog", "a3_D", "a3_out", "a3_bout")}
        xz = k.sb(ctx, "a3_xz", [P, 2, T])
        dt = k.sb(ctx, "a3_dt", [P, 1, T])
        du = k.sb(ctx, "a3_du", [P, 1, T])
        bc3 = k.sb(ctx, "a3_bc3", [96, T], BF16)
        A = k.sb(ctx, "a3_A", [P, 1, NS])
        with ExitStack() as sub:
            padded = k.sb(sub, "a3_padded", [P, 2, NB, SEQ + 3])
            proj, x_out, zero, conv = k.sems(ctx, "a3_", "proj x_out zero conv")
            with nc.Block() as block:

                @block.tensor
                def _(pe):
                    for n in range(8):
                        pe.matmul(ps[:, n, :], w["a3_in"][:, tile(n // 4)], k.xn[:, chunk(n % 4)], start=True, stop=True).then_inc(proj, 1)

                @block.scalar
                def _(act):
                    for n in range(8):
                        act.wait_ge(proj, n + 1)
                        act.activation(padded[:, n // 4, n % 4 // 2, 1 + CH * (n % 2):1 + CH * (n % 2) + CH], ps[:, n, :],
                                       ACT.Copy).then_inc(x_out, 1)
                    for m in range(2):
                        act.wait_ge(conv, 7 + m)
                        act.activation(xz[:, m, :], xz[:, m, :], ACT.Silu)

                @block.vector
                def _(dve):
                    dve.memset(padded[:, :, :, 0:1], 0.0).then_inc(zero, 1)
                    dve.memset(padded[:, :, :, SEQ + 1:SEQ + 3], 0.0).then_inc(zero, 1)
                    dve.wait_ge(zero, 2)
                    dve.wait_ge(x_out, 8)
                    for tap in range(4):
                        for m in range(2):
                            dst = xz[:, m, :].rearrange("p (b t) -> p b t", b=NB)
                            src = padded[:, m, :, tap:tap + SEQ]
                            kern = w["a3_conv"][:, m, tap:tap + 1]
                            if tap == 0:
                                dve.tensor_scalar(dst, src, kern, None, ALU.mult).then_inc(conv, 1)
                            else:
                                dve.wait_ge(conv, 2 * (tap - 1) + m + 1)
                                dve.scalar_tensor_tensor(out=dst, in0=src, scalar=kern, in1=dst, op0=ALU.mult,
                                                         op1=ALU.add).then_inc(conv, 1)
        with ExitStack() as sub:
            low = k.sb(sub, "a3_low", [P, T])
            up = k.sb(sub, "a3_up", [P, T])
            upped, = k.sems(ctx, "a3_", "upped")
            dtr = k.sb(sub, "a3_dtrows", [8, T])
            b2 = k.sb(sub, "a3_b2", [P, 1])
            rows, drows, dcopy, pre, soft, aexp, summed, biased = k.sems(ctx, "a3_", "rows drows dcopy pre soft aexp summed biased")
            s, mid, rest, psrows = split_rows(k, ctx, bc3, "a3")
            with nc.Block() as block:

                @block.tensor
                def _(pe):
                    for j in range(NCH):
                        pe.matmul(ps[0:8, 4 + j, :], w["a3_dtr"], xz[:, 0, chunk(j)], start=True, stop=True).then_inc(drows, 1)
                    for j in range(NCH):
                        pe.matmul(ps[0:96, j, :], w["a3_bc"][:, 0, :], xz[:, 0, chunk(j)], start=True, stop=True).then_inc(rows, 1)
                    pe.wait_ge(dcopy, 1)
                    for j in range(NCH):
                        pe.matmul(ps[:, 4 + j, :], w["a3_dt_w"], dtr[:, chunk(j)], start=True, stop=True).then_inc(pre, 1)

                @block.scalar
                def _(act):
                    act.activation(A[:, 0, :], w["a3_alog"], ACT.Exp).then_inc(aexp, 1)
                    act.wait_ge(drows, NCH)
                    act.activation(dtr[:, :], ps[0:8, 4:8, :].rearrange("p a b -> p (a b)"), ACT.Copy).then_inc(dcopy, 1)
                    act.wait_ge(pre, NCH)
                    act.wait_ge(biased, 1)
                    v = ps[:, 4:8, :].rearrange("p a b -> p (a b)")
                    act.activation(dt[:, 0, :], v, ACT.Relu, bias=b2[:, 0:1]).then_inc(soft, 1)
                    act.activation(low[:, :], v, ACT.Abs, bias=b2[:, 0:1]).then_inc(soft, 1)
                    act.wait_ge(soft, 2)
                    act.activation(low[:, :], low[:, :], ACT.Exp, scale=-1.0).then_inc(soft, 1)
                    act.wait_ge(upped, 1)
                    act.activation(k.t3[:, :], up[:, :], ACT.Ln).then_inc(soft, 1)

                @block.vector
                def _(dve):
                    dve.tensor_scalar(b2[:, :], w["a3_dt_b"], 2.0, None, ALU.mult).then_inc(biased, 1)
                    dve.wait_ge(rows, NCH)
                    split_steps(dve, k, s, mid, rest, psrows, bc3)
                    dve.wait_ge(soft, 3)
                    softplus_steps(dve, k, dt[:, 0, :], low, up, upped, soft, 4, summed, 0)
                    dve.tensor_tensor(du[:, 0, :], dt[:, 0, :], xz[:, 0, :], ALU.mult)
                    dve.wait_ge(aexp, 1)
                    dve.tensor_scalar(A[:, 0, :], A[:, 0, :], -1.0, None, ALU.mult)
        with ExitStack() as sub:
            def finish(dve, b, hf, y):
                v = xz[:, 0, bass.ds(b * SEQ, SEQ)]
                return dve.scalar_tensor_tensor(out=v, in0=v, scalar=w["a3_D"][:, 0:1], in1=y, op0=ALU.mult, op1=ALU.add)

            scan_loop(k, sub, "a3s", 1, du, bc3, finish, dt=dt, rate=A)
        with nc.Block() as block:

            @block.scalar
            def _(act):
                act.activation(k.x[:, :], k.x[:, :], ACT.Identity, bias=w["a3_bout"][:, 0:1])
        project_out(k, ctx, "a3p", w["a3_out"], xz)


MIDS = (5.0, 3.5, 2.5, 1.75, 1.25, 0.75, 0.25)


class Fp4:

    STEPS, PARTS = 14, 2

    def __init__(self, k, ctx, name, nblk):
        self.k, self.n = k, nblk
        self.step, self.parts = k.sems(ctx, name + "_", "step parts")
        self.amax = k.sb(ctx, name + "_amax", [P, nblk])
        self.rec = k.sb(ctx, name + "_rec", [P, nblk])
        self.ab = k.sb(ctx, name + "_ab", [P, nblk * 16])
        self.sg = k.sb(ctx, name + "_sg", [P, nblk * 16])
        self.xs = k.sb(ctx, name + "_xs", [P, nblk * 16])

    def blocks(self, v):
        return v.rearrange("p (n c) -> p n c", c=16)

    def scalar(self, act, wait, n0):
        wait(act, self.step, n0 * self.STEPS + 4)
        act.activation(self.ab[:, :], self.xs[:, :], ACT.Abs).then_inc(self.parts, 1)
        act.activation(self.sg[:, :], self.xs[:, :], ACT.Sign).then_inc(self.parts, 1)

    def vector(self, dve, wait, n0, src, dst):
        base = n0 * self.STEPS
        bc = lambda v: v.unsqueeze(2).to_broadcast([P, self.n, 16])
        count = [0]

        def done(ins):
            ins.then_inc(self.step, 1)
            count[0] += 1
            wait(dve, self.step, base + count[0])

        done(dve.tensor_reduce(self.amax[:, :], self.blocks(src), AX.X, ALU.max, apply_absolute_value=True))
        done(dve.tensor_scalar(self.amax[:, :], self.amax[:, :], 1.0 / 6.0, 1e-12, ALU.mult, ALU.max))
        done(dve.reciprocal(self.rec[:, :], self.amax[:, :]))
        done(dve.tensor_tensor(self.blocks(self.xs[:, :]), self.blocks(src), bc(self.rec[:, :]), ALU.mult))
        wait(dve, self.parts, n0 * self.PARTS + 2)
        ab, q = self.ab[:, :], self.xs[:, :]
        done(dve.tensor_scalar(q, ab, MIDS[0], 2.0, ALU.is_gt, ALU.mult))
        for m in MIDS[1:3]:
            done(dve.scalar_tensor_tensor(out=q, in0=ab, scalar=m, in1=q, op0=ALU.is_gt, op1=ALU.add))
        done(dve.tensor_scalar(q, q, 2.0, None, ALU.mult))
        for m in MIDS[3:]:
            done(dve.scalar_tensor_tensor(out=q, in0=ab, scalar=m, in1=q, op0=ALU.is_gt, op1=ALU.add))
        done(dve.scalar_tensor_tensor(out=q, in0=q, scalar=0.5, in1=self.sg[:, :], op0=ALU.mult, op1=ALU.mult))
        done(dve.tensor_tensor(self.blocks(dst), self.blocks(q), bc(self.amax[:, :]), ALU.mult))
        assert count[0] == self.STEPS


def static_wait(eng, sem, n):
    eng.wait_ge(sem, n)


def layer3_ffn(k, W):
    nc, ps = k.nc, k.ps
    I = 352
    PARTS = [(0, P), (P, P), (2 * P, I - 2 * P)]
    with ExitStack() as ctx:
        wgu, wd = W("f3_gu"), W("f3_down")
        wt = k.sb(ctx, "f3_wt", [P, 6, P])
        wdt = k.sb(ctx, "f3_wdt", [P, 3, P])
        xq = k.sb(ctx, "f3_xq", [P, T])
        NW = 6 * P + I
        allw = k.sb(ctx, "f3_wq", [P, NW])
        with ExitStack() as sub:
            fq = Fp4(k, sub, "f3w", NW // 16)
            turned, out = k.sems(ctx, "f3w_", "turned out")
            with nc.Block() as block:

                @block.vector
                def _(dve):
                    fq.vector(dve, static_wait, 0, k.w3[:, 0:NW], allw[:, :])

                @block.scalar
                def _(act):
                    fq.scalar(act, static_wait, 0)
                    act.wait_ge(turned, 1)
                    act.activation(wt[:, :, :].rearrange("p m c -> p (m c)"), ps[:, 0:2, 0:3 * P], ACT.Copy)
                    act.activation(wdt[:, 0:2, :], ps[:, 2, 0:2 * P].rearrange("p (m c) -> p m c", m=2), ACT.Copy)
                    act.activation(wdt[0:96, 2, :], ps[0:96, 3, 0:P], ACT.Copy)

                @block.tensor
                def _(pe):
                    pe.wait_ge(fq.step, fq.STEPS)
                    for m in range(6):
                        pe.transpose(ps[:, m // 3, tile(m % 3)], allw[:, tile(m)], k.ident[:, :])
                    for m, (a, n) in enumerate(PARTS):
                        mm = pe.transpose(ps[0:n, 2 if m < 2 else 3, tile(m if m < 2 else 0)], allw[:, 6 * P + a:6 * P + a + n], k.ident[:, :])
                    mm.then_inc(turned, 1)
        with ExitStack() as sub:
            fq = Fp4(k, sub, "f3x", T // 16)
            turned, copied, back = k.sems(ctx, "f3x_", "turned copied back")
            with nc.Block() as block:

                @block.tensor
                def _(pe):
                    for t in range(NT):
                        mm = pe.transpose(ps[:, t // 4, tile(t % 4)], k.xn[:, tile(t)], k.ident[:, :])
                    mm.then_inc(turned, 1)
                    pe.wait_ge(fq.step, fq.STEPS)
                    for t in range(NT):
                        mm = pe.transpose(ps[:, 4 + t // 4, tile(t % 4)], k.t1[:, tile(t)], k.ident[:, :])
                    mm.then_inc(back, 1)

                @block.vector
                def _(dve):
                    dve.wait_ge(turned, 1)
                    fq.vector(dve, static_wait, 0, ps[:, 0:4, :].rearrange("p a b -> p (a b)"), k.t1[:, :])

                @block.scalar
                def _(act):
                    fq.scalar(act, static_wait, 0)
                    act.wait_ge(back, 1)
                    act.activation(xq[:, :], ps[:, 4:8, :].rearrange("p a b -> p (a b)"), ACT.Copy)
        xs = k.sb(ctx, "f3_xs", [P, CH])
        sg = k.sb(ctx, "f3_sg", [P, 4, I])
        h = k.sb(ctx, "f3_h", [P, 4 * I])
        ht = k.sb(ctx, "f3_ht", [P, 3, CH])
        fq = Fp4(k, ctx, "f3h", 4 * I // 16)
        x_in, prod, silu, hid, turned, ht_done, y, added = k.sems(ctx, "f3l_", "x_in prod silu hid turned ht y added")
        h4 = h[:, :].rearrange("p (t i) -> p t i", t=4)
        with nc.Block() as block:

            @block.scalar
            def _(act):
                with act.Fori(0, NCH) as i:
                    k.hold(act, added, i + 1)
                    act.activation(xs[:, :], xq[:, bass.ds(i * CH, CH)], ACT.Copy).then_inc(x_in, 1)
                    k.hold(act, prod, i + 1)
                    act.activation(sg[:, :, :], ps[:, 0:4, 0:I], ACT.Silu).then_inc(silu, 1)
                    fq.scalar(act, k.hold, i)
                    k.hold(act, turned, i + 1)
                    act.activation(ht[:, 0:2, :], ps[:, 0:2, :], ACT.Copy).then_inc(ht_done, 1)
                    act.activation(ht[0:96, 2, :], ps[0:96, 2, :], ACT.Copy).then_inc(ht_done, 1)

            @block.tensor
            def _(pe):
                with pe.Fori(0, NCH) as i:
                    k.hold(pe, x_in, i + 1)
                    for t in range(4):
                        pe.matmul(ps[:, t, 0:I], xs[:, tile(t)], wt[:, 0:3, :].rearrange("p m c -> p (m c)")[:, 0:I], start=True, stop=True)
                        mm = pe.matmul(ps[:, 4 + t, 0:I], xs[:, tile(t)], wt[:, 3:6, :].rearrange("p m c -> p (m c)")[:, 0:I], start=True, stop=True)
                    mm.then_inc(prod, 1)
                    k.hold(pe, fq.step, (i + 1) * fq.STEPS)
                    for m, (a, n) in enumerate(PARTS):
                        for t in range(4):
                            mm = pe.transpose(ps[0:n, m, tile(t)], h4[:, t, a:a + n], k.ident[:, :])
                    mm.then_inc(turned, 1)
                    k.hold(pe, ht_done, 2 * i + 2)
                    for m, (a, n) in enumerate(PARTS):
                        mm = pe.matmul(ps[:, 3, :], wdt[0:n, m, :], ht[0:n, m, :], start=(m == 0), stop=(m == 2))
                    mm.then_inc(y, 1)

            @block.vector
            def _(dve):
                dve.sem_inc(added, 1)
                with dve.Fori(0, NCH) as i:
                    k.hold(dve, silu, i + 1)
                    dve.tensor_tensor(h4, sg[:, :, :], ps[:, 4:8, 0:I], ALU.mult).then_inc(hid, 1)
                    k.hold(dve, hid, i + 1)
                    fq.vector(dve, k.hold, i, h[:, :], h[:, :])
                    k.hold(dve, y, i + 1)
                    dve.tensor_tensor(k.x[:, bass.ds(i * CH, CH)], k.x[:, bass.ds(i * CH, CH)], ps[:, 3, :], ALU.add).then_inc(added, 1)


def more_layouts(np, a, L, f, col, kt, three, choose, eh):
    g = lambda n: f(a["L2_attn_" + n])
    L["a2"] = dict(a2_wo=kt(g("Wo")), a2_bo=col(g("bo")), a2_g=col(g("gamma")), a2_b=col(g("beta")),
                   a2_lam=np.full((128, 1), g("lam"), np.float32))
    wq, wk, wv, bq, bk, bv = (g(n) for n in ("Wq", "Wk", "Wv", "bq", "bk", "bv"))
    pairs = {}
    for p in list(range(8)) + [7]:
        cols = []
        for h in (2 * p, 2 * p + 1):
            cols.append(wq[h])
        for h in (2 * p, 2 * p + 1):
            for m in range(2):
                cols += [wk[h][:, 64 * m:64 * m + 64]] * 2
        cols += [wv[2 * p], wv[2 * p + 1], bq[2 * p][:, None], bq[2 * p + 1][:, None]]
        for h in (2 * p, 2 * p + 1):
            for m in range(2):
                cols.append(np.tile(bk[h][64 * m:64 * m + 64], 2)[:, None])
        cols.append(np.concatenate([bv[2 * p], bv[2 * p + 1]])[:, None])
        pairs[f"pair{len(pairs)}"] = np.concatenate(cols, axis=1)
    L["a2w"] = pairs
    g = lambda n: f(a["L2_ffn_" + n])
    two = lambda v: v.reshape(32, 2, 128, 64).transpose(2, 0, 1, 3).reshape(128, 32, 128)
    sel = np.zeros((64, 32, 128), np.float32)
    for e in range(64):
        sel[e, e // 2, 64 * (e % 2):64 * (e % 2) + 64] = 1
    L["f2"] = dict(f2_router=g("router_w"), f2_gate=two(g("gate_w")), f2_up=two(g("up_w")),
                   f2_down=g("down_w").reshape(32, 128, 128).transpose(1, 0, 2), f2_sg=g("shared_gate_w"),
                   f2_su=g("shared_up_w"), f2_sd=g("shared_down_w"), f2_sel=sel)
    g = lambda n: f(a["L3_attn_" + n])
    L["a3"] = dict(a3_in=g("W_in"), a3_conv=np.stack([g("conv_x_k")[:, 0, :].T, g("conv_z_k")[:, 0, :].T], axis=1),
                   a3_bc=three(g("W_xproj")[:, 8:40]), a3_dtr=g("W_xproj")[:, 0:8], a3_dt_w=g("W_dt"), a3_dt_b=col(g("b_dt")),
                   a3_alog=g("A_log"), a3_D=col(g("D")), a3_out=kt(g("W_out")), a3_bout=col(g("b_out")))
    g = lambda n: f(a["L3_ffn_" + n])

    def rows(v):
        out = np.zeros((384, 128), np.float32)
        out[:352] = v
        return out.reshape(3, 128, 128).transpose(1, 0, 2)

    L["f3"] = dict(f3_gu=np.concatenate([rows(g("w_gate")), rows(g("w_up"))], axis=1), f3_down=g("w_down"))


def program(nc, views, x_dram, sel_dram, out_dram):
    with ExitStack() as ctx:
        k = Kit(nc, ctx, views)
        x_loaded, consts, turned, stored = k.sems(ctx, "main_", "x_loaded consts turned stored")
        with nc.Block() as block:

            @block.sync
            def _(sp):
                sp.dma_start(k.x[:, :], x_dram).then_inc(x_loaded, 16)
                sp.dma_start(k.sel[:, :, :], sel_dram).then_inc(x_loaded, 16)
                sp.wait_ge(x_loaded, 32)

            @block.gpsimd
            def _(pool):
                pool.memset(k.ones[:, :], 1.0 / P)
                pool.memset(k.eps5[:, :], 1e-5)
                pool.memset(k.eps6[:, :], 1e-6)
                pool.memset(k.ident[:, :], 0.0).then_inc(consts, 1)
                pool.wait_ge(consts, 1)
                pool.affine_select(out=k.ident[:, :], in_=k.ident[:, :], compare_op=ALU.not_equal, fill=1.0, base=0,
                                   pattern=[[-1, P]], channel_multiplier=1)

        for n, (attn, ffn) in enumerate(((layer0_attn, layer0_ffn), (layer1_attn, layer1_ffn), (layer2_attn, layer2_ffn),
                                         (layer3_attn, layer3_ffn))):
            if n not in LAYERS:
                continue
            layer_norm(k, k.x, k.xn, k.eps5)
            for part, half in ((attn, "a"), (ffn, "f")):
                with ExitStack() as sub:
                    k.ctx, k.counted = sub, []
                    part(k, load(k, sub, f"{half}{n}"))
                    k.clear_counts()
        with nc.Block() as block:

            @block.sync
            def _(sp):
                sp.dma_start(out_dram, k.x[:, :]).then_inc(stored, 16)
                sp.wait_ge(stored, 16)


def layouts(np, a):
    f = lambda v: np.asarray(v)
    col = lambda v: f(v).reshape(-1, 128).T
    kt = lambda v: f(v).reshape(-1, 128, f(v).shape[-1]).transpose(1, 0, 2)

    def three(v):
        return np.concatenate([kt(v)] * 3, axis=2)

    def choose(n, m):
        out = np.zeros((n, m, 128), np.float32)
        for r in range(n):
            out[r, r * m // n, :] = 1.0
        return out

    L = {}
    g = lambda n: f(a["L0_attn_" + n])
    xp = g("x_proj_w").T
    L["a0"] = dict(a0_norm_w=col(g("norm_w")), a0_norm_b=col(g("norm_b")), a0_in=g("in_proj_w").T,
                   a0_conv=g("conv_w").transpose(1, 2, 0).reshape(2, 128, 4, 256).transpose(1, 2, 0, 3).reshape(128, 8, 256),
                   a0_conv_b=col(g("conv_b")), a0_bc=three(xp[:, 1:33]), a0_ds=kt(np.repeat(xp[:, 0:1], 128, axis=1)),
                   a0_dt_w=col(g("dt_w")), a0_dt_b=col(g("dt_b")), a0_out=kt(g("out_proj_w").T))
    g = lambda n: f(a["L0_ffn_" + n])
    eh = lambda v, m: v.reshape(v.shape[0], m, 128).transpose(2, 0, 1)
    L["f0"] = dict(f0_gate=g("gate_w"), f0_w1=g("w1").transpose(1, 0, 2), f0_b1=eh(g("b1"), 2), f0_g=eh(g("ln1_g"), 2),
                   f0_b=eh(g("ln1_b"), 2), f0_w2=g("w2").reshape(16, 128, 128).transpose(1, 0, 2), f0_b2=g("b2").T,
                   f0_ln_g=col(g("ln_g")), f0_ln_b=col(g("ln_b")), f0_sel=choose(8, 8))
    g = lambda n: f(a["L1_attn_" + n])
    L["a1"] = dict(a1_norm_w=col(g("norm_w")), a1_in=g("in_proj_w"), a1_conv=g("conv_w")[:, 0, :].reshape(2, 128, 4).transpose(1, 0, 2),
                   a1_dt_w=kt(g("dt_w")), a1_dt_b=col(g("dt_b")), a1_alog=kt(g("A_log")),
                   a1_bc=three(np.concatenate([g("B_w"), g("C_w")], axis=1)), a1_D=col(g("D_skip")), a1_out=kt(g("out_proj_w")))
    g = lambda n: f(a["L1_ffn_" + n])
    L["f1"] = dict(f1_gate=g("gate_W"), f1_w1=g("W1").reshape(8, 128, 4, 128).transpose(1, 0, 2, 3).reshape(128, 32, 128),
                   f1_b1=eh(g("b1"), 4), f1_w2=g("W2").reshape(32, 128, 128).transpose(1, 0, 2), f1_b2=g("b2").T,
                   f1_sw=g("shared_W"), f1_sb=col(g("shared_b")), f1_g=col(g("gamma")), f1_b=col(g("beta")), f1_sel=choose(8, 8))
    more_layouts(np, a, L, f, col, kt, three, choose, eh)
    return L


def kernel(**inputs):
    import numpy as _np
    import concourse.bacc as _bacc
    from concourse import mybir as _mybir
    from concourse.bass_utils import run_bass_kernel_spmd as _run

    nc = _bacc.Bacc("TRN2", target_bir_lowering=False, num_devices=1)
    arrays, views = {}, {}
    for name, parts in layouts(_np, inputs).items():
        cols, places, blocks = 0, {}, []
        for part, v in parts.items():
            places[part] = (cols, v.shape)
            v = v.reshape(v.shape[0], -1)
            full = _np.zeros((128, v.shape[1]), _np.float32)
            full[:v.shape[0]] = v
            blocks.append(full)
            cols += v.shape[1]
        packed = _np.ascontiguousarray(_np.concatenate(blocks, axis=1))
        arrays[f"in_{name}_dram"] = packed
        views[name] = (nc.dram_tensor(f"in_{name}_dram", packed.shape, _mybir.dt.float32, kind="ExternalInput").ap(), places)
    x = _np.ascontiguousarray(_np.asarray(inputs["L0_attn_x"]).reshape(2048, 128).T)
    arrays["in_x_dram"] = x
    x_dram = nc.dram_tensor("in_x_dram", x.shape, _mybir.dt.float32, kind="ExternalInput").ap()
    sel = _np.zeros((96, 32, 128), _mybir.dt.np(_mybir.dt.bfloat16))
    for r in range(96):
        sel[r, r % 32, :] = 1
    arrays["in_sel_dram"] = sel
    sel_dram = nc.dram_tensor("in_sel_dram", sel.shape, _mybir.dt.bfloat16, kind="ExternalInput").ap()
    out_dram = nc.dram_tensor("out_0_dram", (128, 2048), _mybir.dt.float32, kind="ExternalOutput").ap()
    program(nc, views, x_dram, sel_dram, out_dram)
    r = _run(nc, [arrays], core_ids=[0])
    return _np.ascontiguousarray(r.results[0]["out_0_dram"].T).reshape(2, 1024, 128)
```

```python
from contextlib import ExitStack

import concourse.bass as bass
from concourse import mybir

ALU = mybir.AluOpType
ACT = mybir.ActivationFunctionType
AX = mybir.AxisListType
F32 = mybir.dt.float32
F32R = mybir.dt.float32r
BF16 = mybir.dt.bfloat16
I32 = mybir.dt.int32

P = 128
NB, SEQ = 2, 1024
T = NB * SEQ
CH = 512
NCH = T // CH
NT = T // P
NS = 16
DI = 2
LN_EXP = "natural_log_exp_and_others"
NE = 8


LOAD_FIRST = 64


def chunk(j):
    return slice(CH * j, CH * j + CH)


def tile(t):
    return slice(P * t, P * t + P)


class Kit:

    def __init__(self, nc, ctx, views):
        self.nc, self.ctx, self.views, self.norms = nc, ctx, views, 0
        self.counted = []
        self.x = self.sb(ctx, "x", [P, T])
        self.xn = self.sb(ctx, "xn", [P, T])
        self.t1 = self.sb(ctx, "t1", [P, T])
        self.t2 = self.sb(ctx, "t2", [P, T])
        self.t3 = self.sb(ctx, "t3", [P, T])
        self.ones = self.sb(ctx, "ones", [P, P])
        self.ident = self.sb(ctx, "ident", [P, P])
        self.eps5 = self.sb(ctx, "eps5", [P, 1])
        self.eps6 = self.sb(ctx, "eps6", [P, 1])
        self.ps = ctx.enter_context(nc.psum_tensor("ps", [P, 8, CH], F32))
        self.loaded = {n: (self.sem(ctx, "loaded_" + n), self.sem(ctx, "rest_loaded_" + n)) for n in views if n != "a2w"}
        self.pad = self.sem(ctx, "loop_wait_carrier")
        self.ln = {n: self.sem(ctx, "ln_" + n) for n in ("mean", "centred", "squared", "var", "log", "rstd", "out")}

    def sb(self, ctx, name, shape, dt=F32):
        return ctx.enter_context(self.nc.sbuf_tensor(name, shape, dt))

    def sem(self, ctx, name):
        s = ctx.enter_context(self.nc.semaphore(name))
        if ctx is self.ctx:
            self.counted.append(s)
        return s

    def clear_counts(self):
        with self.nc.Block() as block:

            @block.gpsimd
            def _(pool):
                for s in self.counted:
                    pool.sem_clear(s)

    def sems(self, ctx, prefix, names):
        return [self.sem(self.ctx, prefix + n) for n in names.split()]

    def hold(self, eng, sem, count):
        eng.wait_ge(sem, count)
        eng.sem_inc(self.pad, 1)


def layer_norm(k, src, dst, eps, gain=None, bias=None, rms=False):
    base = 4 * k.norms
    k.norms += 1
    ln, ps = k.ln, k.ps
    cen = src if rms else k.t1
    with k.nc.Block() as block:

        @block.tensor
        def _(pe):
            for j in range(NCH):
                if not rms:
                    pe.matmul(ps[:, j, :], k.ones[:, :], src[:, chunk(j)], start=True, stop=True).then_inc(ln["mean"], 1)
            for j in range(NCH):
                pe.wait_ge(ln["squared"], base + j + 1)
                pe.matmul(ps[:, 4 + j, :], k.ones[:, :], k.t2[:, chunk(j)], start=True, stop=True).then_inc(ln["var"], 1)
            if rms:
                pe.sem_inc(ln["mean"], 4)

        @block.scalar
        def _(act):
            act.preload_act_table_set(LN_EXP)
            for j in range(NCH):
                if not rms:
                    act.wait_ge(ln["centred"], base + j + 1)
                act.activation(k.t2[:, chunk(j)], cen[:, chunk(j)], ACT.Square).then_inc(ln["squared"], 1)
            for j in range(NCH):
                act.wait_ge(ln["var"], base + j + 1)
                act.activation(k.t3[:, chunk(j)], ps[:, 4 + j, :], ACT.Ln, bias=eps[:, 0:1]).then_inc(ln["log"], 1)
                act.wait_ge(ln["log"], base + j + 1)
                act.activation(k.t3[:, chunk(j)], k.t3[:, chunk(j)], ACT.Exp, scale=-0.5).then_inc(ln["rstd"], 1)

        @block.vector
        def _(dve):
            for j in range(NCH):
                if not rms:
                    dve.wait_ge(ln["mean"], base + j + 1)
                    dve.tensor_tensor(k.t1[:, chunk(j)], src[:, chunk(j)], ps[:, j, :], ALU.subtract).then_inc(ln["centred"], 1)
            for j in range(NCH):
                dve.wait_ge(ln["rstd"], base + j + 1)
                if gain is None:
                    dve.tensor_tensor(dst[:, chunk(j)], cen[:, chunk(j)], k.t3[:, chunk(j)], ALU.mult).then_inc(ln["out"], 1)
                else:
                    dve.scalar_tensor_tensor(out=dst[:, chunk(j)], in0=cen[:, chunk(j)], scalar=gain,
                                             in1=k.t3[:, chunk(j)], op0=ALU.mult, op1=ALU.mult).then_inc(ln["out"], 1)
            if bias is not None:
                dve.wait_ge(ln["out"], base + 4)
                dve.tensor_scalar(dst[:, :], dst[:, :], bias, None, ALU.add)
            if rms:
                dve.sem_inc(ln["centred"], 4)


def load(k, ctx, name):
    src, places = k.views[name]
    cols = src.shape[1]
    first = min(cols, LOAD_FIRST)
    w = k.sb(ctx, "w_" + name, [P, cols])
    loaded, rest_loaded = k.loaded[name]
    scans = name in ("a0", "a1", "a3")
    if scans:
        k.sel = k.sb(ctx, "sel_" + name, [P, 2 * NS, P], BF16)
    with k.nc.Block() as block:

        @block.sync
        def _(sp):
            sp.dma_start(w[:, 0:first], src[:, 0:first]).then_inc(loaded, 16)
            if first < cols:
                sp.dma_start(w[:, first:cols], src[:, first:cols]).then_inc(rest_loaded, 16)
            if scans:
                sp.dma_start(k.sel[:, :, :], k.sel_dram).then_inc(loaded, 16)

    k.w3 = w

    def get(n):
        a, shape = places[n]
        cols = 1
        for d in shape[1:]:
            cols *= d
        v = w[0:shape[0], a:a + cols]
        if len(shape) == 3:
            v = v.rearrange("p (a b) -> p a b", b=shape[2])
        if len(shape) == 4:
            v = v.rearrange("p (a b c) -> p a b c", b=shape[2], c=shape[3])
        return v

    k.pending = ((loaded, 32 if scans else 16), (rest_loaded, 16) if first < cols else None)
    return get


def wait_loaded(k, which):
    if k.pending[which] is not None:
        with k.nc.Block() as block:

            @block.sync
            def _(sp):
                sp.wait_ge(*k.pending[which])


def split_rows(k, ctx, bc3, name):
    s = k.sem(k.ctx, "split_" + name)
    mid = k.t2[0:96, :].bitcast(BF16)[:, 0:T]
    rest = k.t1[0:96, :]
    rows = k.ps[0:96, 0:4, :].rearrange("p a b -> p (a b)")
    return s, mid, rest, rows


def split_steps(dve, k, s, mid, rest, rows, bc3):
    dve.memset(bc3[96:P, :], 0.0)
    dve.tensor_copy(bc3[0:96, :], rows).then_inc(s, 1)
    dve.wait_ge(s, 1)
    dve.tensor_tensor(rest, rows, bc3[0:96, :], ALU.subtract).then_inc(s, 1)
    dve.wait_ge(s, 2)
    dve.tensor_copy(mid, rest).then_inc(s, 1)
    dve.wait_ge(s, 3)
    dve.tensor_tensor(rest, rest, mid, ALU.subtract).then_inc(s, 1)
    dve.tensor_copy(bc3[32:64, :], mid[32:64, :])
    dve.wait_ge(s, 4)
    dve.tensor_copy(bc3[64:96, :], rest[64:96, :])


def softplus_steps(dve, k, dt, low, up, upped, soft, n, summed, m):
    dve.tensor_scalar(up[:, :], low[:, :], 1.0, None, ALU.add).then_inc(upped, 1)
    dve.wait_ge(upped, 2 * m + 1)
    dve.scalar_tensor_tensor(out=low[:, :], in0=up[:, :], scalar=-1.0, in1=low[:, :], op0=ALU.add,
                             op1=ALU.subtract).then_inc(upped, 1)
    dve.wait_ge(upped, 2 * m + 2)
    dve.wait_ge(soft, n)
    dve.scalar_tensor_tensor(out=k.t3[:, :], in0=up[:, :], scalar=1.0, in1=k.t3[:, :], op0=ALU.is_gt,
                             op1=ALU.mult).then_inc(summed, 1)
    dve.wait_ge(summed, 3 * m + 1)
    dve.tensor_tensor(low[:, :], k.t3[:, :], low[:, :], ALU.subtract).then_inc(summed, 1)
    dve.wait_ge(summed, 3 * m + 2)
    dve.tensor_tensor(dt, dt, low[:, :], ALU.add).then_inc(summed, 1)
    dve.wait_ge(summed, 3 * m + 3)


def scan_loop(k, ctx, name, halves, u, bc3, finish, decay=None, dt=None, rate=None):
    nc, ps = k.nc, k.ps
    w = k.sb(ctx, name + "_w", [P, 2, halves, SEQ])
    h = k.sb(ctx, name + "_h", [P, 2, halves, SEQ])
    hc = k.sb(ctx, name + "_hc", [P, 2, halves, SEQ])
    cs = k.sb(ctx, name + "_c", [P, 2, SEQ])
    a = k.sb(ctx, name + "_a", [P, 2, halves, SEQ]) if dt is not None else None
    b_ready, c_ready, w_done, scanned, cs_done, hc_done, summed, y_out, a_done = k.sems(
        ctx, name + "_", "b_ready c_ready w_done scanned cs_done hc_done summed y_out a_done")
    H = halves
    bank_c, bank_y = 2, 4
    banks_b = (0, 0) if H == 2 else (0, 6)

    def spread(bank):
        return ps[:, bank:bank + 2, :].rearrange("p a b -> p (a b)")

    with nc.Block() as block:

        @block.tensor
        def _(pe):
            pe.sem_inc(summed, 2 * H)

            def add_state(b, s):
                for hf in range(H):
                    k.hold(pe, hc_done, (b * NS + s) * H + hf + 1 + 2 * H)
                    if s == 0 and hf == 0:
                        k.hold(pe, y_out, b * H + 1)
                    for q in range(2):
                        mm = pe.matmul(ps[:, bank_y + 2 * hf + q, :], k.ident[:, :], hc[:, s % 2, hf, chunk(q)],
                                       start=(s == 0), stop=(s == NS - 1))
                    mm.then_inc(summed, 1)

            with pe.Fori(0, NB) as b:
                for s in range(NS + 2):
                    if s < NS:
                        g = b * NS + s
                        k.hold(pe, w_done, g * H + H)
                        for q in range(2):
                            mm = pe.matmul(ps[:, banks_b[s % 2] + q, :], k.sel[:, s, :], bc3[:, bass.ds(b * SEQ + CH * q, CH)],
                                           start=True, stop=True)
                        mm.then_inc(b_ready, 1)
                        k.hold(pe, cs_done, g + 1)
                        for q in range(2):
                            mm = pe.matmul(ps[:, bank_c + q, :], k.sel[:, NS + s, :],
                                           bc3[:, bass.ds(b * SEQ + CH * q, CH)], start=True, stop=True)
                        mm.then_inc(c_ready, 1)
                    if s >= 2:
                        add_state(b, s - 2)

        @block.scalar
        def _(act):
            act.sem_inc(cs_done, 1)
            with act.Fori(0, NB) as b:
                for s in range(NS):
                    g = b * NS + s
                    if dt is not None:
                        for hf in range(H):
                            k.hold(act, w_done, (g * H + hf) + 1)
                            k.hold(act, hc_done, g * H + hf + 1)
                            act.activation(a[:, s % 2, hf, :], dt[:, hf, bass.ds(b * SEQ, SEQ)], ACT.Exp,
                                           scale=rate[:, hf, s:s + 1]).then_inc(a_done, 1)
                    k.hold(act, c_ready, g + 1)
                    k.hold(act, hc_done, g * H + H)
                    act.activation(cs[:, s % 2, :], spread(bank_c), ACT.Copy).then_inc(cs_done, 1)

        @block.vector
        def _(dve):
            dve.sem_inc(w_done, 2)
            dve.sem_inc(y_out, 1)
            with dve.Fori(0, NB) as b:
                for s in range(NS):
                    g = b * NS + s
                    k.hold(dve, b_ready, g + 1)
                    for hf in range(H):
                        dve.tensor_tensor(w[:, s % 2, hf, :], u[:, hf, bass.ds(b * SEQ, SEQ)], spread(banks_b[s % 2]),
                                          ALU.mult).then_inc(w_done, 1)
                    for hf in range(H):
                        k.hold(dve, w_done, g * H + hf + 1 + 2)
                        if dt is not None:
                            k.hold(dve, a_done, g * H + hf + 1)
                        k.hold(dve, hc_done, g * H + hf + 1)
                        d0 = a[:, s % 2, hf, :] if dt is not None else decay[:, hf, bass.ds(b * SEQ, SEQ)]
                        dve.tensor_tensor_scan(h[:, s % 2, hf, :], d0, w[:, s % 2, hf, :], 0.0, ALU.mult,
                                               ALU.add).then_inc(scanned, 1)
                k.hold(dve, summed, (b + 1) * NS * H + 2 * H)
                for hf in range(H):
                    finish(dve, b, hf, spread(bank_y + 2 * hf)).then_inc(y_out, 1)

        @block.gpsimd
        def _(pool):
            pool.sem_inc(hc_done, 2 * H)
            with pool.Fori(0, NB) as b:
                for s in range(NS):
                    g = b * NS + s
                    k.hold(pool, cs_done, g + 2)
                    for hf in range(H):
                        k.hold(pool, scanned, g * H + hf + 1)
                        k.hold(pool, summed, g * H + hf + 1)
                        pool.tensor_tensor(hc[:, s % 2, hf, :], h[:, s % 2, hf, :], cs[:, s % 2, :],
                                           ALU.mult).then_inc(hc_done, 1)


def route_top2(k, ctx, name, gate, comb_t):
    nc, ps = k.nc, k.ps
    logits = ps[:, 0, 0:NT * NE].rearrange("p (t e) -> p t e", e=NE)
    top = k.sb(ctx, name + "_top", [P, NT, 8])
    shifted = k.sb(ctx, name + "_shifted", [P, NT, NE])
    mask = k.sb(ctx, name + "_mask", [P, NT, NE])
    ex = k.sb(ctx, name + "_ex", [P, NT, NE])
    total = k.sb(ctx, name + "_total", [P, NT])
    logit, topped, shift, masked, expd, kept, summed, inv, comb, turned, zeroed, high = k.sems(
        ctx, name + "_", "logit topped shift masked expd kept summed inv comb turned zeroed high")
    with nc.Block() as block:

        @block.tensor
        def _(pe):
            for t in range(NT):
                mm = pe.matmul(logits[:, t, :], k.xn[:, tile(t)], gate, start=True, stop=True)
            mm.then_inc(logit, 1)
            pe.wait_ge(comb, 1)
            for t in range(NT):
                mm = pe.transpose(ps[0:NE, 1 + t // 4, P * (t % 4):P * (t % 4) + P], mask[:, t, :], k.ident[:, :])
            mm.then_inc(turned, 1)

        @block.vector
        def _(dve):
            dve.wait_ge(logit, 1)
            for t in range(NT):
                dve.max(top[:, t, :], logits[:, t, :]).then_inc(topped, 1)
            dve.wait_ge(topped, NT)
            dve.tensor_tensor(shifted[:, :, :], logits, top[:, :, 0:1].to_broadcast([P, NT, NE]), ALU.subtract).then_inc(shift, 1)
            dve.tensor_tensor(mask[:, :, :], logits, top[:, :, 1:2].to_broadcast([P, NT, NE]), ALU.is_ge).then_inc(masked, 1)
            dve.wait_ge(expd, 1)
            dve.wait_ge(masked, 1)
            dve.tensor_tensor(ex[:, :, :], ex[:, :, :], mask[:, :, :], ALU.mult).then_inc(kept, 1)
            dve.wait_ge(kept, 1)
            dve.tensor_reduce(total[:, :], ex[:, :, :], AX.X, ALU.add).then_inc(summed, 1)
            dve.wait_ge(summed, 1)
            dve.reciprocal(total[:, :], total[:, :]).then_inc(inv, 1)
            dve.wait_ge(inv, 1)
            dve.tensor_tensor(mask[:, :, :], ex[:, :, :], total[:, :].unsqueeze(2).to_broadcast([P, NT, NE]),
                              ALU.mult).then_inc(comb, 1)
            dve.wait_ge(high, 1)
            dve.tensor_tensor(comb_t[32:32 + NE, :], ps[0:NE, 1:5, :].rearrange("p a b -> p (a b)"),
                              comb_t[0:NE, :].bitcast(F32), ALU.subtract)

        @block.gpsimd
        def _(pool):
            pool.memset(k.t3[:, :], 0.0).then_inc(zeroed, 1)
            pool.wait_ge(zeroed, 1)
            pool.tensor_copy(comb_t[:, :], k.t3[:, :]).then_inc(zeroed, 1)

        @block.scalar
        def _(act):
            act.wait_ge(shift, 1)
            act.activation(ex[:, :, :], shifted[:, :, :], ACT.Exp).then_inc(expd, 1)
            act.wait_ge(turned, 1)
            act.wait_ge(zeroed, 2)
            act.activation(comb_t[0:NE, :], ps[0:NE, 1:5, :].rearrange("p a b -> p (a b)"), ACT.Copy).then_inc(high, 1)


def project_out(k, ctx, name, weight, src, extra=None):
    ready, added = k.sems(ctx, name + "_", "ready added")
    with k.nc.Block() as block:

        @block.tensor
        def _(pe):
            for j in range(NCH):
                for hf in range(DI):
                    mm = pe.matmul(k.ps[:, j, :], weight[:, hf, :], src[:, hf, chunk(j)], start=(hf == 0), stop=(hf == DI - 1))
                mm.then_inc(ready, 1)

        @block.vector
        def _(dve):
            for j in range(NCH):
                dve.wait_ge(ready, j + 1)
                dve.tensor_tensor(k.x[:, chunk(j)], k.x[:, chunk(j)], k.ps[:, j, :], ALU.add).then_inc(added, 1)
            if extra is not None:
                dve.wait_ge(added, NCH)
                dve.tensor_tensor(k.x[:, :], k.x[:, :], extra[:, :], ALU.add)


def layer0_attn(k, W):
    nc, ps = k.nc, k.ps
    with ExitStack() as ctx:
        w = {n: W(n) for n in ("a0_norm_w", "a0_norm_b", "a0_in", "a0_conv", "a0_conv_b", "a0_bc", "a0_ds", "a0_dt_w",
                               "a0_dt_b", "a0_out")}
        xn2 = k.t2
        u = k.sb(ctx, "a0_u", [P, DI, T])
        decay = k.sb(ctx, "a0_decay", [P, DI, T])
        sz = k.sb(ctx, "a0_sz", [P, DI, T])
        bc3 = k.sb(ctx, "a0_bc3", [P, T], BF16)
        layer_norm(k, k.xn, xn2, k.eps5, w["a0_norm_w"][:, 0:1], w["a0_norm_b"][:, 0:1])
        with ExitStack() as sub:
            padded = k.sb(sub, "a0_padded", [P, DI, NB, SEQ + 3])
            proj, x_out, z_out = k.sems(ctx, "a0_", "proj x_out z_out")
            with nc.Block() as block:

                @block.tensor
                def _(pe):
                    for m in range(4):
                        for j in range(NCH):
                            n = 4 * m + j
                            if n >= 8:
                                pe.wait_ge(x_out, n - 7)
                            pe.matmul(ps[:, n % 8, :], w["a0_in"][:, tile(m)], xn2[:, chunk(j)], start=True,
                                      stop=True).then_inc(proj, 1)

                @block.vector
                def _(dve):
                    dve.memset(padded[:, :, :, 0:3], 0.0)
                    for n in range(8):
                        dve.wait_ge(proj, n + 1)
                        dve.tensor_copy(padded[:, n // 4, n % 4 // 2, 3 + CH * (n % 2):3 + CH * (n % 2) + CH],
                                        ps[:, n, :]).then_inc(x_out, 1)

                @block.scalar
                def _(act):
                    for n in range(8):
                        act.wait_ge(proj, n + 9)
                        act.activation(sz[:, n // 4, chunk(n % 4)], ps[:, n, :], ACT.Silu).then_inc(z_out, 1)

            conv, = k.sems(ctx, "a0_", "conv")
            with nc.Block() as block:

                @block.tensor
                def _(pe):
                    for m in range(DI):
                        for n in range(4):
                            for hf in range(DI):
                                for tap in range(4):
                                    lo = CH * (n % 2) + tap
                                    mm = pe.matmul(ps[:, 4 * m + n, :], w["a0_conv"][:, tap * DI + hf, tile(m)],
                                                   padded[:, hf, n // 2, lo:lo + CH],
                                                   start=(hf == 0 and tap == 0), stop=(hf == 1 and tap == 3))
                            mm.then_inc(conv, 1)

                @block.scalar
                def _(act):
                    for n in range(8):
                        act.wait_ge(conv, n + 1)
                        act.activation(u[:, n // 4, chunk(n % 4)], ps[:, n, :], ACT.Silu, bias=w["a0_conv_b"][:, n // 4:n // 4 + 1])
        rows, delta, neg = k.sems(ctx, "a0_", "rows delta neg")
        s, mid, rest, psrows = split_rows(k, ctx, bc3, "a0")
        nw = k.sb(ctx, "a0_negw", [P, DI])
        nb = k.sb(ctx, "a0_negb", [P, DI])
        with nc.Block() as block:

            @block.tensor
            def _(pe):
                for weight, bank, done, m in ((w["a0_bc"], 0, rows, 96), (w["a0_ds"], 4, delta, P)):
                    for j in range(NCH):
                        for hf in range(DI):
                            mm = pe.matmul(ps[0:m, bank + j, :], weight[:, hf, :], u[:, hf, chunk(j)], start=(hf == 0),
                                           stop=(hf == 1))
                        mm.then_inc(done, 1)

            @block.vector
            def _(dve):
                dve.tensor_scalar(nw[:, :], w["a0_dt_w"], -1.0, None, ALU.mult).then_inc(neg, 1)
                dve.tensor_scalar(nb[:, :], w["a0_dt_b"], -1.0, None, ALU.mult).then_inc(neg, 1)
                dve.wait_ge(rows, NCH)
                split_steps(dve, k, s, mid, rest, psrows, bc3)

            @block.scalar
            def _(act):
                act.wait_ge(neg, 2)
                act.wait_ge(delta, NCH)
                for hf in range(DI):
                    act.activation(decay[:, hf, :], ps[:, 4:8, :].rearrange("p a b -> p (a b)"), ACT.Sigmoid,
                                   scale=nw[:, hf:hf + 1], bias=nb[:, hf:hf + 1])
        with ExitStack() as sub:
            def finish(dve, b, hf, y):
                return dve.tensor_tensor(sz[:, hf, bass.ds(b * SEQ, SEQ)], sz[:, hf, bass.ds(b * SEQ, SEQ)], y, ALU.mult)

            scan_loop(k, sub, "a0s", DI, u, bc3, finish, decay=decay)
        project_out(k, ctx, "a0p", w["a0_out"], sz, extra=k.xn)


def layer0_ffn(k, W):
    nc, ps = k.nc, k.ps
    HID = 2
    H_BANKS = (0, 2, 6)
    with ExitStack() as ctx:
        w = {n: W(n) for n in ("f0_gate", "f0_w1", "f0_b1", "f0_g", "f0_b", "f0_w2", "f0_b2", "f0_ln_g", "f0_ln_b", "f0_sel")}
        comb_t = k.sb(ctx, "f0_comb_t", [P, T], F32R)
        sel = k.sb(ctx, "f0_sel_r", [P, NE, P], F32R)
        acc = k.sb(ctx, "f0_acc", [P, T])
        w1c = k.sb(ctx, "f0_w1c", [P, NE, HID * P])
        b1c = k.sb(ctx, "f0_b1c", [P, NE, HID])
        mean = k.sb(ctx, "f0_mean", [P, NE])
        mean2 = k.sb(ctx, "f0_mean2", [P, NE])
        route_top2(k, ctx, "f0r", w["f0_gate"], comb_t)
        wait_loaded(k, 1)
        wm, wh, wc, bm, bh, acc0 = k.sems(ctx, "f0_", "w_mean w_half w_centred b_mean b_half acc_init")
        with nc.Block() as block:

            @block.tensor
            def _(pe):
                pe.matmul(ps[:, 0, 0:NE * HID], k.ones[:, :], w["f0_b1"].rearrange("p e m -> p (e m)"), start=True,
                          stop=True).then_inc(bm, 1)

            @block.vector
            def _(dve):
                dve.tensor_reduce(mean[:, :], w["f0_w1"], AX.X, ALU.add).then_inc(wm, 1)
                dve.wait_ge(wm, 1)
                dve.tensor_scalar(mean[:, :], mean[:, :], 1.0 / (HID * P), None, ALU.mult).then_inc(wh, 1)
                dve.wait_ge(wh, 1)
                dve.tensor_tensor(w1c[:, :, :], w["f0_w1"], mean[:, :].unsqueeze(2).to_broadcast([P, NE, HID * P]), ALU.subtract)
                dve.wait_ge(bm, 1)
                dve.tensor_reduce(mean2[:, :], ps[:, 0, 0:NE * HID].rearrange("p (e m) -> p e m", m=HID), AX.X, ALU.add).then_inc(bh, 1)
                dve.wait_ge(bh, 1)
                dve.tensor_scalar(mean2[:, :], mean2[:, :], 1.0 / HID, None, ALU.mult).then_inc(bh, 1)
                dve.wait_ge(bh, 2)
                dve.tensor_tensor(b1c[:, :, :], w["f0_b1"], mean2[:, :].unsqueeze(2).to_broadcast([P, NE, HID]), ALU.subtract)

            @block.gpsimd
            def _(pool):
                pool.tensor_copy(acc[:, :], k.xn[:, :])

            @block.scalar
            def _(act):
                act.activation(sel[:, :, :], w["f0_sel"], ACT.Copy)

        hn = k.sb(ctx, "f0_hn", [P, NE, HID, CH])
        sq = k.sb(ctx, "f0_sq", [P, 2, HID, CH])
        rs = k.sb(ctx, "f0_rs", [P, 2, CH])
        gl = k.sb(ctx, "f0_gl", [P, 2, HID, CH])
        yb = k.sb(ctx, "f0_yb", [P, 2, CH])
        tmp = k.sb(ctx, "f0_tmp", [P, 2, CH])
        h_done, sq_done, sq_sum, var_done, log_done, rs_done, hn_done, gl_done, y_done, cb_done, yb_done, tmp_done, acc_done = k.sems(
            ctx, "f0l_", "h sq sq_sum var log rs hn gl y cb yb tmp acc")
        with nc.Block() as block:

            @block.tensor
            def _(pe):
                pe.sem_inc(var_done, 2)
                pe.sem_inc(y_done, 2)
                with pe.Fori(0, NCH) as i:
                    def hidden(e):
                        if e == 2:
                            k.hold(pe, tmp_done, i * NE + 2)
                        for m in range(HID):
                            k.hold(pe, hn_done, (i * NE + e) * HID + m + 1 + (HID if e < 2 else 0))
                            pe.matmul(ps[:, H_BANKS[e % 3] + m, :], w1c[:, e, tile(m)], k.xn[:, bass.ds(i * CH, CH)], start=True,
                                      stop=True).then_inc(h_done, 1)

                    def variance(e):
                        k.hold(pe, sq_sum, i * NE + e + 1)
                        k.hold(pe, log_done, i * NE + e + 1)
                        pe.matmul(ps[:, 4 + e % 2, :], k.ones[:, :], sq[:, e % 2, 0, :], start=True, stop=True).then_inc(var_done, 1)

                    for e in range(NE + 1):
                        if e < NE:
                            hidden(e)
                        if e >= 1:
                            variance(e - 1)
                    for e in range(NE):
                        g = i * NE + e
                        k.hold(pe, tmp_done, g + 1)
                        if e < 2:
                            k.hold(pe, log_done, i * NE + NE + 2)
                            k.hold(pe, hn_done, (i * NE + 6) * HID + 3 * HID)
                        pe.matmul(ps[:, 6 + e % 2, :], sel[:, e, :], comb_t[:, bass.ds(i * CH, CH)], start=True,
                                  stop=True).then_inc(cb_done, 1)
                        k.hold(pe, gl_done, g * HID + HID + NE * HID)
                        k.hold(pe, yb_done, g + 1)
                        for m in range(HID):
                            mm = pe.matmul(ps[:, 4 + e % 2, :], w["f0_w2"][:, e * HID + m, :], gl[:, e % 2, m, :], start=(m == 0),
                                           stop=(m == HID - 1))
                        mm.then_inc(y_done, 1)

            @block.scalar
            def _(act):
                act.sem_inc(log_done, 2)
                act.sem_inc(gl_done, NE * HID)
                act.sem_inc(yb_done, 2)
                with act.Fori(0, NCH) as i:
                    def squares(e):
                        for m in range(HID):
                            k.hold(act, h_done, (i * NE + e) * HID + m + 1)
                            k.hold(act, var_done, i * NE + e + 1)
                            act.activation(sq[:, e % 2, m, :], ps[:, H_BANKS[e % 3] + m, :], ACT.Square,
                                           bias=b1c[:, e, m:m + 1]).then_inc(sq_done, 1)

                    def rstd(e):
                        g = i * NE + e
                        k.hold(act, var_done, g + 3)
                        k.hold(act, hn_done, g * HID + 2 * HID)
                        act.activation(rs[:, e % 2, :], ps[:, 4 + e % 2, :], ACT.Ln, scale=1.0 / HID,
                                       bias=k.eps5[:, 0:1]).then_inc(log_done, 1)
                        k.hold(act, log_done, g + 3)
                        act.activation(rs[:, e % 2, :], rs[:, e % 2, :], ACT.Exp, scale=-0.5).then_inc(rs_done, 1)

                    act.preload_act_table_set(LN_EXP)
                    for e in range(NE + 1):
                        if e < NE:
                            squares(e)
                        if e >= 1:
                            rstd(e - 1)

                    def add_b2(e):
                        g = i * NE + e
                        k.hold(act, y_done, g + 3)
                        k.hold(act, tmp_done, g + 1)
                        act.activation(yb[:, e % 2, :], ps[:, 4 + e % 2, :], ACT.Identity,
                                       bias=w["f0_b2"][:, e:e + 1]).then_inc(yb_done, 1)

                    for e in range(NE + 1):
                        if e < NE:
                            for m in range(HID):
                                k.hold(act, hn_done, (i * NE + e) * HID + m + 1 + 3 * HID)
                                k.hold(act, y_done, i * NE + e + 1)
                                act.activation(gl[:, e % 2, m, :], hn[:, e, m, :], ACT.Gelu, scale=w["f0_g"][:, e, m:m + 1],
                                               bias=w["f0_b"][:, e, m:m + 1]).then_inc(gl_done, 1)
                        if e >= 1:
                            add_b2(e - 1)

            @block.vector
            def _(dve):
                dve.sem_inc(hn_done, 3 * HID)
                dve.sem_inc(tmp_done, 2)
                with dve.Fori(0, NCH) as i:
                    def add_squares(e):
                        k.hold(dve, sq_done, (i * NE + e) * HID + HID)
                        dve.tensor_tensor(sq[:, e % 2, 0, :], sq[:, e % 2, 0, :], sq[:, e % 2, 1, :], ALU.add).then_inc(sq_sum, 1)

                    add_squares(0)
                    for e in range(NE):
                        if e + 1 < NE:
                            add_squares(e + 1)
                        g = i * NE + e
                        k.hold(dve, rs_done, g + 1)
                        for m in range(HID):
                            k.hold(dve, gl_done, g * HID + m + 1)
                            dve.scalar_tensor_tensor(out=hn[:, e, m, :], in0=ps[:, H_BANKS[e % 3] + m, :],
                                                     scalar=b1c[:, e, m:m + 1], in1=rs[:, e % 2, :], op0=ALU.add,
                                                     op1=ALU.mult).then_inc(hn_done, 1)
                    for e in range(NE):
                        g = i * NE + e
                        k.hold(dve, yb_done, g + 3)
                        k.hold(dve, cb_done, g + 1)
                        k.hold(dve, acc_done, g + 1)
                        dve.tensor_tensor(tmp[:, e % 2, :], yb[:, e % 2, :], ps[:, 6 + e % 2, :], ALU.mult).then_inc(tmp_done, 1)

            @block.gpsimd
            def _(pool):
                pool.sem_inc(acc_done, 2)
                with pool.Fori(0, NCH) as i:
                    for e in range(NE):
                        g = i * NE + e
                        k.hold(pool, tmp_done, g + 3)
                        k.hold(pool, acc_done, g + 2)
                        pool.tensor_tensor(acc[:, bass.ds(i * CH, CH)], acc[:, bass.ds(i * CH, CH)], tmp[:, e % 2, :],
                                           ALU.add).then_inc(acc_done, 1)

        layer_norm(k, acc, acc, k.eps5, w["f0_ln_g"][:, 0:1], w["f0_ln_b"][:, 0:1])
        with nc.Block() as block:

            @block.vector
            def _(dve):
                dve.tensor_tensor(k.x[:, :], k.x[:, :], acc[:, :], ALU.add)


def layer1_attn(k, W):
    nc, ps = k.nc, k.ps
    with ExitStack() as ctx:
        w = {n: W(n) for n in ("a1_norm_w", "a1_in", "a1_conv", "a1_dt_w", "a1_dt_b", "a1_alog", "a1_bc", "a1_D", "a1_out")}
        xc = k.sb(ctx, "a1_xc", [P, DI, T])
        dt = k.sb(ctx, "a1_dt", [P, DI, T])
        du = k.sb(ctx, "a1_du", [P, DI, T])
        bc3 = k.sb(ctx, "a1_bc3", [P, T], BF16)
        A = k.sb(ctx, "a1_A", [P, DI, NS])
        layer_norm(k, k.xn, k.t2, k.eps6, w["a1_norm_w"][:, 0:1], rms=True)
        with ExitStack() as sub:
            padded = k.sb(sub, "a1_padded", [P, DI, NB, SEQ + 3])
            gate = k.sb(sub, "a1_gate", [P, DI, T])
            proj, g_out, x_out, zero, conv = k.sems(ctx, "a1_", "proj g_out x_out zero conv")
            with nc.Block() as block:

                @block.tensor
                def _(pe):
                    for m in range(4):
                        for j in range(NCH):
                            n = 4 * m + j
                            if n >= 8:
                                pe.wait_ge(g_out, n - 7)
                            pe.matmul(ps[:, n % 8, :], w["a1_in"][:, tile((m + 2) % 4)], k.t2[:, chunk(j)], start=True,
                                      stop=True).then_inc(proj, 1)

                @block.scalar
                def _(act):
                    for n in range(8):
                        act.wait_ge(proj, n + 1)
                        act.activation(gate[:, n // 4, chunk(n % 4)], ps[:, n, :], ACT.Silu).then_inc(g_out, 1)

                @block.vector
                def _(dve):
                    dve.memset(padded[:, :, :, 0:3], 0.0).then_inc(zero, 1)
                    for n in range(8):
                        dve.wait_ge(proj, n + 9)
                        dve.wait_ge(g_out, n + 1)
                        dve.tensor_tensor(padded[:, n // 4, n % 4 // 2, 3 + CH * (n % 2):3 + CH * (n % 2) + CH],
                                          gate[:, n // 4, chunk(n % 4)], ps[:, n, :], ALU.mult).then_inc(x_out, 1)
                    dve.wait_ge(x_out, 8)
                    dve.wait_ge(zero, 1)
                    for tap in range(4):
                        for hf in range(DI):
                            dst = xc[:, hf, :].rearrange("p (b t) -> p b t", b=NB)
                            src = padded[:, hf, :, tap:tap + SEQ]
                            kern = w["a1_conv"][:, hf, tap:tap + 1]
                            if tap == 0:
                                dve.tensor_scalar(dst, src, kern, None, ALU.mult).then_inc(conv, 1)
                            else:
                                dve.wait_ge(conv, 2 * (tap - 1) + hf + 1)
                                dve.scalar_tensor_tensor(out=dst, in0=src, scalar=kern, in1=dst, op0=ALU.mult,
                                                         op1=ALU.add).then_inc(conv, 1)
        with ExitStack() as sub:
            low = k.sb(sub, "a1_low", [P, T])
            up = k.sb(sub, "a1_up", [P, T])
            upped, = k.sems(ctx, "a1_", "upped")
            pre, rows, soft, aexp, relu_done, logd, summed = k.sems(ctx, "a1_", "pre rows soft aexp relu logd summed")
            s, mid, rest, psrows = split_rows(k, ctx, bc3, "a1")
            with nc.Block() as block:

                @block.tensor
                def _(pe):
                    for j in range(NCH):
                        for hf in range(DI):
                            mm = pe.matmul(ps[0:96, j, :], w["a1_bc"][:, hf, :], xc[:, hf, chunk(j)], start=(hf == 0), stop=(hf == 1))
                        mm.then_inc(rows, 1)
                    for m in range(DI):
                        if m:
                            pe.wait_ge(relu_done, 1)
                            pe.wait_ge(soft, 1)
                        for j in range(NCH):
                            for hf in range(DI):
                                mm = pe.matmul(ps[:, 4 + j, :], w["a1_dt_w"][:, hf, tile(m)], xc[:, hf, chunk(j)], start=(hf == 0),
                                               stop=(hf == 1))
                            mm.then_inc(pre, 1)

                @block.scalar
                def _(act):
                    act.activation(A[:, :, :], w["a1_alog"], ACT.Exp).then_inc(aexp, 1)
                    act.preload_act_table_set(LN_EXP)
                    for m in range(DI):
                        act.wait_ge(pre, NCH * (m + 1))
                        v = ps[:, 4:8, :].rearrange("p a b -> p (a b)")
                        bias = w["a1_dt_b"][:, m:m + 1]
                        if m:
                            act.wait_ge(summed, 3)
                        act.activation(dt[:, m, :], v, ACT.Relu, bias=bias).then_inc(relu_done, 1)
                        act.activation(low[:, :], v, ACT.Abs, bias=bias).then_inc(soft, 1)
                        act.wait_ge(soft, 3 * m + 1)
                        act.activation(low[:, :], low[:, :], ACT.Exp, scale=-1.0).then_inc(soft, 1)
                        act.wait_ge(upped, 2 * m + 1)
                        act.activation(k.t3[:, :], up[:, :], ACT.Ln).then_inc(soft, 1)

                @block.vector
                def _(dve):
                    dve.wait_ge(rows, NCH)
                    split_steps(dve, k, s, mid, rest, psrows, bc3)
                    for m in range(DI):
                        dve.wait_ge(soft, 3 * m + 2)
                        dve.wait_ge(relu_done, m + 1)
                        softplus_steps(dve, k, dt[:, m, :], low, up, upped, soft, 3 * m + 3, summed, m)
                        dve.tensor_tensor(du[:, m, :], dt[:, m, :], xc[:, m, :], ALU.mult)
                    dve.wait_ge(aexp, 1)
                    dve.tensor_scalar(A[:, :, :], A[:, :, :], -1.0, None, ALU.mult)
        with ExitStack() as sub:
            def finish(dve, b, hf, y):
                v = xc[:, hf, bass.ds(b * SEQ, SEQ)]
                return dve.scalar_tensor_tensor(out=v, in0=v, scalar=w["a1_D"][:, hf:hf + 1], in1=y, op0=ALU.mult, op1=ALU.add)

            scan_loop(k, sub, "a1s", DI, du, bc3, finish, dt=dt, rate=A)
        project_out(k, ctx, "a1p", w["a1_out"], xc)


def layer1_ffn(k, W):
    nc, ps = k.nc, k.ps
    HID = 4
    with ExitStack() as ctx:
        w = {n: W(n) for n in ("f1_gate", "f1_w1", "f1_b1", "f1_w2", "f1_b2", "f1_sw", "f1_sb", "f1_g", "f1_b", "f1_sel")}
        comb_t = k.sb(ctx, "f1_comb_t", [P, T], F32R)
        sel = k.sb(ctx, "f1_sel_r", [P, NE, P], F32R)
        acc = k.sb(ctx, "f1_acc", [P, T])
        route_top2(k, ctx, "f1r", w["f1_gate"], comb_t)
        wait_loaded(k, 1)
        shared, gelud = k.sems(ctx, "f1_", "shared gelud")
        with nc.Block() as block:

            @block.tensor
            def _(pe):
                for j in range(NCH):
                    pe.matmul(ps[:, j, :], w["f1_sw"], k.xn[:, chunk(j)], start=True, stop=True).then_inc(shared, 1)

            @block.scalar
            def _(act):
                for j in range(NCH):
                    act.wait_ge(shared, j + 1)
                    act.activation(acc[:, chunk(j)], ps[:, j, :], ACT.Gelu, bias=w["f1_sb"][:, 0:1]).then_inc(gelud, 1)
                act.activation(sel[:, :, :], w["f1_sel"], ACT.Copy)

            @block.vector
            def _(dve):
                dve.wait_ge(gelud, NCH)
                dve.tensor_scalar(acc[:, :], acc[:, :], 0.5, None, ALU.mult)

        gl = k.sb(ctx, "f1_gl", [P, 2, HID, CH])
        yb = k.sb(ctx, "f1_yb", [P, 2, CH])
        tmp = k.sb(ctx, "f1_tmp", [P, 2, CH])
        h_done, gl_done, y_done, cb_done, yb_done, tmp_done, acc_done = k.sems(ctx, "f1l_", "h gl y cb yb tmp acc")
        with nc.Block() as block:

            @block.tensor
            def _(pe):
                pe.sem_inc(y_done, 2)
                with pe.Fori(0, NCH) as i:
                    for e in range(NE + 1):
                        if e < NE:
                            for m in range(HID):
                                k.hold(pe, gl_done, (i * NE + e) * HID + m + 1)
                                pe.matmul(ps[:, m, :], w["f1_w1"][:, e * HID + m, :], k.xn[:, bass.ds(i * CH, CH)], start=True,
                                          stop=True).then_inc(h_done, 1)
                        if e >= 1:
                            f, g = e - 1, i * NE + e - 1
                            k.hold(pe, tmp_done, g + 1)
                            pe.matmul(ps[:, 6 + f % 2, :], sel[:, f, :], comb_t[:, bass.ds(i * CH, CH)], start=True,
                                      stop=True).then_inc(cb_done, 1)
                            k.hold(pe, gl_done, g * HID + 2 * HID)
                            k.hold(pe, yb_done, g + 1)
                            for m in range(HID):
                                mm = pe.matmul(ps[:, 4 + f % 2, :], w["f1_w2"][:, f * HID + m, :], gl[:, f % 2, m, :],
                                               start=(m == 0), stop=(m == HID - 1))
                            mm.then_inc(y_done, 1)

            @block.scalar
            def _(act):
                act.sem_inc(gl_done, HID)
                act.sem_inc(yb_done, 2)
                with act.Fori(0, NCH) as i:
                    for e in range(NE + 1):
                        if e < NE:
                            for m in range(HID):
                                k.hold(act, h_done, (i * NE + e) * HID + m + 1)
                                k.hold(act, y_done, i * NE + e + 1)
                                act.activation(gl[:, e % 2, m, :], ps[:, m, :], ACT.Gelu,
                                               bias=w["f1_b1"][:, e, m:m + 1]).then_inc(gl_done, 1)
                        if e >= 1:
                            f, g = e - 1, i * NE + e - 1
                            k.hold(act, y_done, g + 3)
                            k.hold(act, tmp_done, g + 1)
                            act.activation(yb[:, f % 2, :], ps[:, 4 + f % 2, :], ACT.Identity,
                                           bias=w["f1_b2"][:, f:f + 1]).then_inc(yb_done, 1)

            @block.vector
            def _(dve):
                dve.sem_inc(tmp_done, 2)
                with dve.Fori(0, NCH) as i:
                    for e in range(NE):
                        g = i * NE + e
                        k.hold(dve, yb_done, g + 3)
                        k.hold(dve, cb_done, g + 1)
                        k.hold(dve, acc_done, g + 1)
                        dve.tensor_tensor(tmp[:, e % 2, :], yb[:, e % 2, :], ps[:, 6 + e % 2, :], ALU.mult).then_inc(tmp_done, 1)

            @block.gpsimd
            def _(pool):
                pool.sem_inc(acc_done, 2)
                with pool.Fori(0, NCH) as i:
                    for e in range(NE):
                        g = i * NE + e
                        k.hold(pool, tmp_done, g + 3)
                        k.hold(pool, acc_done, g + 2)
                        pool.tensor_tensor(acc[:, bass.ds(i * CH, CH)], acc[:, bass.ds(i * CH, CH)], tmp[:, e % 2, :],
                                           ALU.add).then_inc(acc_done, 1)

        layer_norm(k, acc, acc, k.eps5, w["f1_g"][:, 0:1], w["f1_b"][:, 0:1])
        with nc.Block() as block:

            @block.vector
            def _(dve):
                dve.tensor_tensor(k.x[:, :], k.x[:, :], acc[:, :], ALU.add)

LAYERS = (0, 1, 2, 3)


NH, HD = 16, 64
PAIRS = NH // 2
WQ_AT, WK_AT, WV_AT = 0, 2 * P, 6 * P
BQ_AT, BK_AT, BV_AT = 7 * P, 7 * P + 2, 7 * P + 6
PAIR_COLS = 7 * P + 7


def layer2_attn(k, W):
    nc, ps = k.nc, k.ps
    pairs_dram, _ = k.views["a2w"]
    with ExitStack() as ctx:
        w = {n: W(n) for n in ("a2_wo", "a2_bo", "a2_g", "a2_b", "a2_lam")}
        ocat = k.sb(ctx, "a2_ocat", [P, PAIRS, T])
        wp = k.sb(ctx, "a2_wp", [P, PAIR_COLS])
        bq, bk, bv = wp[:, BQ_AT:BQ_AT + 2], wp[:, BK_AT:BK_AT + 4], wp[:, BV_AT:BV_AT + 1]
        qhl2 = k.sb(ctx, "a2_qhl", [P, 2, 2, SEQ], F32R)
        kh2 = k.sb(ctx, "a2_kh", [P, 2, 2, SEQ], F32R)
        kl2 = k.sb(ctx, "a2_kl", [P, 2, 2, SEQ], F32R)
        v = k.sb(ctx, "a2_v", [P, NB, SEQ // P, P])
        prob4 = k.sb(ctx, "a2_prob4", [P, T])
        prob = [t[:, :].rearrange("p (a c) -> p a c", a=2) for t in (k.t1, k.t2, k.t3, prob4)]
        turned = k.sb(ctx, "a2_turned", [P, 2, SEQ // P, P])
        oq = k.sb(ctx, "a2_oq", [P, SEQ // P, P])
        negmax = k.sb(ctx, "a2_negmax", [P, 4, 2])
        total = k.sb(ctx, "a2_total", [P, 4, 2])
        inv = k.sb(ctx, "a2_inv", [P, 4, 2])
        ratio = k.sb(ctx, "a2_ratio", [P, 4])
        lam = k.sb(ctx, "a2_lam2", [P, 2])
        bvl = k.sb(ctx, "a2_bvl", [P, 1])
        (w_loaded, w_scaled, proj, high, low, s_ready, max_done, exp_done, inv_done, ratio_done, joined, t_ready,
         t_out, pv_done, o_done, init, bvl_done) = k.sems(
            ctx, "a2_", "w_loaded w_scaled proj high low s_ready max_done exp_done inv_done ratio_done joined t_ready "
            "t_out pv_done o_done init bvl")
        UNITS = [(b, hh) for b in range(NB) for hh in range(2)]
        TILES = 32
        TURNS = TILES + NB

        def projections(n):
            return [("k", a, c) for a in range(2) for c in range(2)] + [("q", 0, 0), ("q", 0, 1)] + ([] if n % 2 else [("v", 0, 0), ("v", 0, 1)])

        def made_in(j):
            n, idx = j % TILES // 8 + 1, j % 8
            return (n, idx) if idx < len(projections(n)) else None

        PROJ_BANK = 7
        first = [0, 8, 14, 22, 28]
        BANKS, LOWS = first[4], 24
        OUT_TURN = (18, TURNS + 1)
        OUT_STEP = (16 + 3, TILES + 3)

        def turn(j):
            return j + (1 if j >= 1 else 0) + (1 if j >= 17 else 0)

        def at(pr, j):
            return (pr, j) if j < TILES else (pr + 1, j - TILES)

        FREE = 5

        with nc.Block() as block:

            @block.sync
            def _(sp):
                with sp.Fori(0, PAIRS + 1) as pr:
                    k.hold(sp, high, pr * BANKS + 1)
                    k.hold(sp, low, pr * LOWS + 1)
                    k.hold(sp, bvl_done, pr + 1)
                    sp.dma_start(wp[:, :], pairs_dram[:, bass.ds(pr * PAIR_COLS, PAIR_COLS)]).then_inc(w_loaded, 16)
                sp.wait_ge(w_loaded, 16 * (PAIRS + 1))

            @block.gpsimd
            def _(pool):
                with pool.Fori(0, PAIRS + 1) as pr:
                    k.hold(pool, w_loaded, 16 * (pr + 1))
                    pool.tensor_scalar(wp[:, WQ_AT:WQ_AT + 2 * P], wp[:, WQ_AT:WQ_AT + 2 * P], float(HD) ** -0.5, None, ALU.mult).then_inc(w_scaled, 1)
                    pool.tensor_scalar(bq, bq, float(HD) ** -0.5, None, ALU.mult).then_inc(w_scaled, 1)

            @block.tensor
            def _(pe):
                pe.sem_inc(t_ready, FREE)
                pe.sem_inc(pv_done, 2)

                def project(n, idx, bank):
                    what, a, c = projections(n)[idx]
                    b, hh = UNITS[n % 4]
                    toks = SEQ * b + CH * c
                    if what == "q":
                        mm = pe.matmul(ps[:, bank, :], wp[:, WQ_AT + P * hh:WQ_AT + P * hh + P], k.xn[:, toks:toks + CH], start=True, stop=True)
                    elif what == "k":
                        wk = WK_AT + P * (2 * hh + a)
                        mm = pe.matmul(ps[:, bank, :], wp[:, wk:wk + P], k.xn[:, toks:toks + CH], start=True, stop=True)
                    else:
                        for t in range(4):
                            mm = pe.matmul(ps[:, bank, tile(t)], k.xn[:, toks + P * t:toks + P * t + P], wp[:, WV_AT:WV_AT + P],
                                           start=True, stop=True)
                    mm.then_inc(proj, 1)

                def project_next(pr, j):
                    pr, j = at(pr, j)
                    n, idx = made_in(j)
                    if j == 24:
                        k.hold(pe, w_scaled, 2 * pr + 4)
                    e = first[n] + idx
                    k.hold(pe, high, pr * BANKS + e + 1)
                    lows = 6 * n + min(idx, 6)
                    k.hold(pe, low, pr * LOWS + lows + 1)
                    project(n, idx, PROJ_BANK)

                def scores(pr, j):
                    pr, j = at(pr, j)
                    n, i = j // 8, j % 8
                    qhl, kh, kl = qhl2[:, n % 2, :, :], kh2[:, n % 2, :, :], kl2[:, n % 2, :, :]
                    for a in range(2):
                        if i == 0 and a == 0:
                            k.hold(pe, low, pr * LOWS + 6 * n + 6 + 1)
                            k.hold(pe, high, pr * BANKS + first[n] + 6 + 1)
                        k.hold(pe, exp_done, pr * 64 + 2 * j + a + 1)
                        for c in range(2):
                            pe.matmul(ps[:, 2 * a + c, :], qhl[:, a, tile(i)], kh[:, a, chunk(c)], start=True, stop=False)
                            mm = pe.matmul(ps[:, 2 * a + c, :], qhl[:, a, tile(i)], kl[:, a, chunk(c)], start=False, stop=True)
                        mm.then_inc(s_ready, 1)

                def turn_block(pr, e, block_at):
                    k.hold(pe, t_out, pr * TURNS + e + 1)
                    for c in range(8):
                        mm = pe.transpose(ps[:, 4 + c // 4, tile(c % 4)], block_at(c), k.ident[:, :])
                    mm.then_inc(t_ready, 1)

                def turn_out(pr, b):
                    k.hold(pe, o_done, pr * TILES + 16 * (b + 1) + 2)
                    turn_block(pr, OUT_TURN[b], lambda c: oq[:, c, :])

                def weigh(pr, j):
                    pr, j = at(pr, j)
                    b, hh = UNITS[j // 8]
                    if j % 16 == 0:
                        k.hold(pe, high, pr * BANKS + first[j // 8 + 1] + 1)
                    k.hold(pe, t_out, pr * TURNS + turn(j) + 2)
                    k.hold(pe, o_done, pr * TILES + j + 2)
                    for c in range(8):
                        mm = pe.matmul(ps[:, 6, 0:HD], turned[:, j % 2, c, :], v[:, b, c, HD * hh:HD * hh + HD],
                                       start=(c == 0), stop=(c == 7))
                    mm.then_inc(pv_done, 1)

                pe.wait_ge(w_scaled, 2)
                for idx in range(8):
                    project(0, idx, idx)

                def step(pr, j):
                    scores(pr, j)
                    for b in range(NB):
                        if j == OUT_STEP[b]:
                            turn_out(pr, b)
                    if j >= 3:
                        weigh(pr, j - 3)
                    if j >= 2:
                        q, i = at(pr, j - 2)
                        k.hold(pe, joined, q * TILES + i + 1)
                        turn_block(q, turn(i), lambda c: prob[i % 4][:, 0, tile(c)])
                    if made_in(j):
                        project_next(pr, j)

                for j in range(3):
                    step(0, j)
                scores(0, 3)
                weigh(0, 0)
                pe.sem_inc(t_ready, 1)
                k.hold(pe, joined, 2)
                turn_block(0, turn(1), lambda c: prob[1][:, 0, tile(c)])
                project_next(0, 3)
                with pe.Fori(0, PAIRS) as pr:
                    for j in range(4, TILES + 4):
                        step(pr, j)

            @block.scalar
            def _(act):
                act.sem_inc(exp_done, 2)
                act.sem_inc(t_out, 1)
                act.sem_inc(high, 1)

                def split_high(pair, n, idx, bank):
                    what, a, c = projections(n)[idx]
                    b, hh = UNITS[n % 4]
                    qhl, kh = qhl2[:, n % 2, :, :], kh2[:, n % 2, :, :]
                    k.hold(act, proj, pair * BANKS + first[n] + idx + 1)
                    if what == "k":
                        ins = act.activation(kh[:, a, chunk(c)], ps[:, bank, :], ACT.Identity, bias=bk[:, 2 * hh + a:2 * hh + a + 1])
                    elif what == "q":
                        act.activation(qhl[0:HD, 0, chunk(c)], ps[0:HD, bank, :], ACT.Identity, bias=bq[0:HD, hh:hh + 1])
                        ins = act.activation(qhl[HD:P, 1, chunk(c)], ps[HD:P, bank, :], ACT.Identity, bias=bq[HD:P, hh:hh + 1])
                    else:
                        ins = act.activation(v[:, b, 4 * c:4 * c + 4, :], ps[:, bank, :].rearrange("p (t d) -> p t d", t=4), ACT.Copy)
                    ins.then_inc(high, 1)

                for idx in range(8):
                    split_high(0, 0, idx, idx)

                def step(pr, j):
                    q, i = at(pr, j)
                    k.hold(act, t_ready, q * TURNS + (turn(i - 4) + 1 + FREE if i >= 4 else i + 1))
                    for a in range(2):
                        k.hold(act, max_done, q * 64 + 2 * i + a + 1)
                        act.activation(prob[i % 4][:, a, :], ps[:, 2 * a:2 * a + 2, :].rearrange("p a b -> p (a b)"), ACT.Exp,
                                       bias=negmax[:, i % 4, a:a + 1], accum_out=total[:, i % 4, a:a + 1]).then_inc(exp_done, 1)
                    for b in range(NB):
                        if j == OUT_STEP[b]:
                            k.hold(act, t_ready, pr * TURNS + OUT_TURN[b] + 1 + FREE)
                            k.hold(act, bvl_done, pr + 2)
                            act.activation(ocat[:, bass.ds(pr, 1), SEQ * b:SEQ * b + SEQ].rearrange("p a t -> p (a t)"),
                                           ps[:, 4:6, :].rearrange("p a b -> p (a b)"), ACT.Identity, bias=bvl[:, 0:1]).then_inc(t_out, 1)
                    if j == 3:
                        act.wait_ge(t_ready, 2 + FREE)
                        act.sem_inc(t_out, 1)
                    if j >= 2:
                        q, i = at(pr, j - 2)
                        k.hold(act, pv_done, q * TILES + i + 1)
                        k.hold(act, t_ready, q * TURNS + turn(i) + 1 + FREE)
                        act.activation(turned[:, i % 2, :, :], ps[:, 4:6, :].rearrange("p a (c q) -> p (a c) q", q=P),
                                       ACT.Copy).then_inc(t_out, 1)
                    if made_in(j):
                        split_high(at(pr, j)[0], *made_in(j), PROJ_BANK)

                for j in range(4):
                    step(0, j)
                with act.Fori(0, PAIRS) as pr:
                    for j in range(4, TILES + 4):
                        step(pr, j)

            @block.vector
            def _(dve):
                dve.sem_inc(low, 1)
                dve.sem_inc(bvl_done, 1)
                dve.sem_inc(o_done, 2)
                dve.tensor_scalar(lam[:, 0:1], w["a2_lam"], -1.0, None, ALU.mult).then_inc(init, 1)
                dve.tensor_scalar(lam[:, 1:2], w["a2_lam"], -1.0, 1.0, ALU.mult, ALU.add).then_inc(init, 1)
                dve.wait_ge(init, 2)

                def split_low(pair, n, idx, bank):
                    what, a, c = projections(n)[idx]
                    if what == "v":
                        return
                    hh = UNITS[n % 4][1]
                    qhl, kh, kl = qhl2[:, n % 2, :, :], kh2[:, n % 2, :, :], kl2[:, n % 2, :, :]
                    k.hold(dve, high, pair * BANKS + first[n] + idx + 2)
                    if what == "k":
                        ins = dve.scalar_tensor_tensor(out=kl[:, a, chunk(c)], in0=ps[:, bank, :], scalar=bk[:, 2 * hh + a:2 * hh + a + 1],
                                                       in1=kh[:, a, chunk(c)].bitcast(F32), op0=ALU.add, op1=ALU.subtract)
                    else:
                        dve.scalar_tensor_tensor(out=qhl[HD:P, 0, chunk(c)], in0=ps[0:HD, bank, :], scalar=bq[0:HD, hh:hh + 1],
                                                 in1=qhl[0:HD, 0, chunk(c)].bitcast(F32), op0=ALU.add, op1=ALU.subtract)
                        ins = dve.scalar_tensor_tensor(out=qhl[0:HD, 1, chunk(c)], in0=ps[HD:P, bank, :], scalar=bq[HD:P, hh:hh + 1],
                                                       in1=qhl[HD:P, 1, chunk(c)].bitcast(F32), op0=ALU.add, op1=ALU.subtract)
                    ins.then_inc(low, 1)

                for idx in range(8):
                    split_low(0, 0, idx, idx)

                def step(pr, j):
                    q, i = at(pr, j)
                    for a in range(2):
                        k.hold(dve, s_ready, q * 64 + 2 * i + a + 1)
                        dve.tensor_reduce(negmax[:, i % 4, a:a + 1], ps[:, 2 * a:2 * a + 2, :].rearrange("p a b -> p (a b)"),
                                          AX.X, ALU.max, negate=True).then_inc(max_done, 1)
                    if j >= 1 and made_in(j - 1):
                        split_low(at(pr, j - 1)[0], *made_in(j - 1), PROJ_BANK)
                    if j == 6:
                        k.hold(dve, w_scaled, 2 * pr + 2)
                        k.hold(dve, t_out, pr * TURNS + 3)
                        dve.tensor_scalar(bvl[:, :], bv, lam[:, 1:2], None, ALU.mult).then_inc(bvl_done, 1)
                    if j >= 1:
                        q, i = at(pr, j - 1)
                        k.hold(dve, exp_done, q * 64 + 2 * i + 4)
                        dve.reciprocal(inv[:, i % 4, :], total[:, i % 4, :]).then_inc(inv_done, 1)
                        k.hold(dve, inv_done, q * TILES + i + 1)
                        dve.scalar_tensor_tensor(out=ratio[:, i % 4:i % 4 + 1], in0=inv[:, i % 4, 1:2], scalar=total[:, i % 4, 0:1],
                                                 in1=lam[:, 0:1], op0=ALU.mult, op1=ALU.mult).then_inc(ratio_done, 1)
                        k.hold(dve, ratio_done, q * TILES + i + 1)
                        dve.scalar_tensor_tensor(out=prob[i % 4][:, 0, :], in0=prob[i % 4][:, 1, :], scalar=ratio[:, i % 4:i % 4 + 1],
                                                 in1=prob[i % 4][:, 0, :], op0=ALU.mult, op1=ALU.add).then_inc(joined, 1)
                    if j >= 3:
                        q, i = at(pr, j - 3)
                        hh = i // 8 % 2
                        for b in range(NB):
                            if j == OUT_STEP[b]:
                                k.hold(dve, t_ready, pr * TURNS + OUT_TURN[b] + 1 + FREE)
                        k.hold(dve, pv_done, q * TILES + i + 3)
                        dve.tensor_scalar(oq[:, i % 8, HD * hh:HD * hh + HD], ps[:, 6, 0:HD], inv[:, i % 4, 0:1], None,
                                          ALU.mult).then_inc(o_done, 1)

                for j in range(4):
                    step(0, j)
                with dve.Fori(0, PAIRS) as pr:
                    for j in range(4, TILES + 4):
                        step(pr, j)

        y, y_out = k.sems(ctx, "a2_", "y y_out")
        with nc.Block() as block:

            @block.tensor
            def _(pe):
                for j in range(NCH):
                    for pr in range(PAIRS):
                        mm = pe.matmul(ps[:, j, :], w["a2_wo"][:, pr, :], ocat[:, pr, chunk(j)], start=(pr == 0), stop=(pr == PAIRS - 1))
                    mm.then_inc(y, 1)

            @block.scalar
            def _(act):
                for j in range(NCH):
                    act.wait_ge(y, j + 1)
                    act.activation(k.t1[:, chunk(j)], ps[:, j, :], ACT.Identity, bias=w["a2_bo"][:, 0:1])

        layer_norm(k, k.t1[:, :], k.t1[:, :], k.eps5, w["a2_g"][:, 0:1], w["a2_b"][:, 0:1])
        with nc.Block() as block:

            @block.vector
            def _(dve):
                dve.scalar_tensor_tensor(out=k.x[:, :], in0=k.t1[:, :], scalar=1.0 - 0.8, in1=k.x[:, :], op0=ALU.mult, op1=ALU.add)


def layer2_ffn(k, W):
    nc, ps = k.nc, k.ps
    E, GR, CAP, PR = 64, 8, 64, 32
    with ExitStack() as ctx:
        w = {n: W(n) for n in ("f2_router", "f2_gate", "f2_up", "f2_down", "f2_sg", "f2_su", "f2_sd", "f2_sel")}
        comb_t = k.sb(ctx, "f2_comb_t", [P, T], F32R)
        sel = k.sb(ctx, "f2_sel_r", [P, PR, P], F32R)
        comb_f = k.t3[0:E, :]
        with ExitStack() as sub:
            sc = k.sb(sub, "f2_scores", [P, NT, E])
            rep = k.sb(sub, "f2_rep", [P, NT, E])
            mask = k.sb(sub, "f2_mask", [P, NT, E])
            gs = k.sb(sub, "f2_gs", [P, NT, GR])
            gtop = k.sb(sub, "f2_gtop", [P, NT, 8])
            top = k.sb(sub, "f2_top", [P, NT, 8])
            tot = k.sb(sub, "f2_tot", [P, NT])
            logit, scored, step, turned_w, turned_m, copied = k.sems(ctx, "f2r_", "logit scored step turned_w turned_m copied")
            flat = lambda v: v.rearrange("p t e -> p (t e)")
            with nc.Block() as block:

                @block.tensor
                def _(pe):
                    for t in range(NT):
                        mm = pe.matmul(ps[:, t // 8, E * (t % 8):E * (t % 8) + E], k.xn[:, tile(t)], w["f2_router"], start=True, stop=True)
                    mm.then_inc(logit, 1)
                    pe.wait_ge(step, 66)
                    for t in range(NT):
                        mm = pe.transpose(ps[0:E, t // 4, P * (t % 4):P * (t % 4) + P], sc[:, t, :], k.ident[:, :])
                    mm.then_inc(turned_w, 1)
                    for t in range(NT):
                        mm = pe.transpose(ps[0:E, 4 + t // 4, P * (t % 4):P * (t % 4) + P], mask[:, t, :], k.ident[:, :])
                    mm.then_inc(turned_m, 1)

                @block.scalar
                def _(act):
                    act.wait_ge(logit, 1)
                    act.activation(flat(sc[:, :, :]), ps[:, 0:2, :].rearrange("p a b -> p (a b)"), ACT.Sigmoid).then_inc(scored, 1)
                    act.wait_ge(turned_w, 1)
                    act.activation(comb_f, ps[0:E, 0:4, :].rearrange("p a b -> p (a b)"), ACT.Copy).then_inc(copied, 1)

                @block.vector
                def _(dve):
                    dve.wait_ge(scored, 1)
                    dve.tensor_reduce(flat(gs[:, :, :]), sc[:, :, :].rearrange("p t (g e) -> p (t g) e", g=GR), AX.X, ALU.max).then_inc(step, 1)
                    dve.wait_ge(step, 1)
                    for t in range(NT):
                        dve.max(gtop[:, t, :], gs[:, t, :]).then_inc(step, 1)
                    dve.wait_ge(step, 1 + NT)
                    dve.tensor_tensor(gs[:, :, :], gs[:, :, :], gtop[:, :, 3:4].to_broadcast([P, NT, GR]), ALU.is_ge).then_inc(step, 1)
                    dve.wait_ge(step, 2 + NT)
                    dve.tensor_tensor(sc[:, :, :].rearrange("p t (g e) -> p (t g) e", g=GR),
                                      sc[:, :, :].rearrange("p t (g e) -> p (t g) e", g=GR),
                                      flat(gs[:, :, :]).unsqueeze(2).to_broadcast([P, NT * GR, GR]), ALU.mult).then_inc(step, 1)
                    dve.wait_ge(step, 3 + NT)
                    for t in range(NT):
                        dve.max(top[:, t, :], sc[:, t, :]).then_inc(step, 1)
                    dve.wait_ge(step, 3 + 2 * NT)
                    for t in range(NT):
                        dve.match_replace(out=rep[:, t, :], in_to_replace=top[:, t, :], in_values=sc[:, t, :], imm_value=-1.0).then_inc(step, 1)
                    dve.tensor_reduce(tot[:, :], top[:, :, :], AX.X, ALU.add).then_inc(step, 1)
                    dve.wait_ge(step, 4 + 3 * NT)
                    dve.tensor_scalar(tot[:, :], tot[:, :], 1e-9, None, ALU.max).then_inc(step, 1)
                    dve.tensor_scalar(flat(mask[:, :, :]), flat(rep[:, :, :]), 0.0, None, ALU.is_lt).then_inc(step, 1)
                    dve.wait_ge(step, 6 + 3 * NT)
                    dve.reciprocal(tot[:, :], tot[:, :]).then_inc(step, 1)
                    dve.tensor_tensor(sc[:, :, :], sc[:, :, :], mask[:, :, :], ALU.mult).then_inc(step, 1)
                    dve.wait_ge(step, 8 + 3 * NT)
                    dve.tensor_scalar(tot[:, :], tot[:, :], 2.5, None, ALU.mult).then_inc(step, 1)
                    dve.wait_ge(step, 9 + 3 * NT)
                    dve.tensor_tensor(sc[:, :, :], sc[:, :, :], tot[:, :].unsqueeze(2).to_broadcast([P, NT, E]), ALU.mult).then_inc(step, 9)
                    dve.memset(k.t1[0:E, :], 1.0).then_inc(step, 1)
                    dve.wait_ge(step, 19 + 3 * NT)
                    dve.wait_ge(turned_m, 1)
                    dve.tensor_tensor_scan(k.t2[0:E, :], k.t1[0:E, :], ps[0:E, 4:8, :].rearrange("p a b -> p (a b)"), 0.0,
                                           ALU.mult, ALU.add).then_inc(step, 1)
                    dve.wait_ge(step, 20 + 3 * NT)
                    dve.wait_ge(copied, 1)
                    dve.scalar_tensor_tensor(out=comb_f, in0=k.t2[0:E, :], scalar=float(CAP), in1=comb_f,
                                             op0=ALU.is_le, op1=ALU.mult).then_inc(step, 1)
                    dve.wait_ge(step, 21 + 3 * NT)
                    dve.tensor_copy(comb_t[0:E, :], comb_f).then_inc(step, 1)
                    dve.wait_ge(step, 22 + 3 * NT)
                    dve.tensor_tensor(comb_t[E:P, :], comb_f, comb_t[0:E, :].bitcast(F32), ALU.subtract)

        sg = k.sb(ctx, "f2_sgb", [P, 2, CH])
        h1 = k.sb(ctx, "f2_h1", [P, 2, CH])
        hw = k.sb(ctx, "f2_hw", [P, 2, CH])
        g_s, silu_s, h_s, y_s = k.sems(ctx, "f2s_", "gated silu hidden y")
        hs = k.t2[0:HD, :]
        wait_loaded(k, 1)
        with nc.Block() as block:

            @block.tensor
            def _(pe):
                for j in range(NCH):
                    pe.matmul(ps[0:HD, j, :], w["f2_sg"], k.xn[:, chunk(j)], start=True, stop=True)
                    pe.matmul(ps[0:HD, 4 + j, :], w["f2_su"], k.xn[:, chunk(j)], start=True, stop=True).then_inc(g_s, 1)
                pe.wait_ge(h_s, 1)
                for j in range(NCH):
                    mm = pe.matmul(ps[:, j, :], w["f2_sd"], hs[:, chunk(j)], start=True, stop=True)
                mm.then_inc(y_s, 1)

            @block.scalar
            def _(act):
                act.wait_ge(g_s, NCH)
                act.activation(k.t1[0:HD, :], ps[0:HD, 0:4, :].rearrange("p a b -> p (a b)"), ACT.Silu).then_inc(silu_s, 1)
                act.activation(sel[:, :, :], w["f2_sel"], ACT.Copy)

            @block.vector
            def _(dve):
                dve.wait_ge(silu_s, 1)
                dve.tensor_tensor(hs, k.t1[0:HD, :], ps[0:HD, 4:8, :].rearrange("p a b -> p (a b)"), ALU.mult).then_inc(h_s, 1)
                dve.wait_ge(y_s, 1)
                dve.tensor_tensor(k.x[:, :], k.x[:, :], ps[:, 0:4, :].rearrange("p a b -> p (a b)"), ALU.add)

        gu, cb, silu, mul1, mul2, y_done, y_out = k.sems(ctx, "f2l_", "gu cb silu mul1 mul2 y_done y_out")
        with nc.Block() as block:

            @block.tensor
            def _(pe):
                pe.sem_inc(y_done, 2)
                with pe.Fori(0, NCH) as i:
                    for p in range(PR + 1):
                        if p < PR:
                            g = i * PR + p
                            k.hold(pe, silu, g + 1)
                            k.hold(pe, mul1, g + 1)
                            pe.matmul(ps[:, p % 2, :], w["f2_gate"][:, p, :], k.xn[:, bass.ds(i * CH, CH)], start=True, stop=True)
                            pe.matmul(ps[:, 2 + p % 2, :], w["f2_up"][:, p, :], k.xn[:, bass.ds(i * CH, CH)], start=True,
                                      stop=True).then_inc(gu, 1)
                            k.hold(pe, mul2, g + 1)
                            pe.matmul(ps[:, 4 + p % 2, :], sel[:, p, :], comb_t[:, bass.ds(i * CH, CH)], start=True,
                                      stop=True).then_inc(cb, 1)
                        if p >= 1:
                            f, g = p - 1, i * PR + p - 1
                            k.hold(pe, mul2, g + 3)
                            if f == 0:
                                k.hold(pe, y_out, i + 1)
                            pe.matmul(ps[:, 6, :], w["f2_down"][:, f, :], hw[:, f % 2, :], start=(f == 0),
                                      stop=(f == PR - 1)).then_inc(y_done, 1)

            @block.scalar
            def _(act):
                act.sem_inc(silu, 2)
                with act.Fori(0, NCH) as i:
                    for p in range(PR):
                        g = i * PR + p
                        k.hold(act, gu, g + 1)
                        k.hold(act, mul1, g + 1)
                        act.activation(sg[:, p % 2, :], ps[:, p % 2, :], ACT.Silu).then_inc(silu, 1)

            @block.vector
            def _(dve):
                dve.sem_inc(mul1, 2)
                dve.sem_inc(mul2, 2)
                dve.sem_inc(y_out, 1)
                with dve.Fori(0, NCH) as i:
                    for p in range(PR):
                        g = i * PR + p
                        k.hold(dve, silu, g + 3)
                        k.hold(dve, mul2, g + 1)
                        dve.tensor_tensor(h1[:, p % 2, :], sg[:, p % 2, :], ps[:, 2 + p % 2, :], ALU.mult).then_inc(mul1, 1)
                        k.hold(dve, mul1, g + 3)
                        k.hold(dve, cb, g + 1)
                        k.hold(dve, y_done, g + 1)
                        dve.tensor_tensor(hw[:, p % 2, :], h1[:, p % 2, :], ps[:, 4 + p % 2, :], ALU.mult).then_inc(mul2, 1)
                    k.hold(dve, y_done, (i + 1) * PR + 2)
                    dve.tensor_tensor(k.x[:, bass.ds(i * CH, CH)], k.x[:, bass.ds(i * CH, CH)], ps[:, 6, :], ALU.add).then_inc(y_out, 1)


def layer3_attn(k, W):
    nc, ps = k.nc, k.ps
    with ExitStack() as ctx:
        w = {n: W(n) for n in ("a3_in", "a3_conv", "a3_bc", "a3_dtr", "a3_dt_w", "a3_dt_b", "a3_alog", "a3_D", "a3_out", "a3_bout")}
        xz = k.sb(ctx, "a3_xz", [P, 2, T])
        dt = k.sb(ctx, "a3_dt", [P, 1, T])
        du = k.sb(ctx, "a3_du", [P, 1, T])
        bc3 = k.sb(ctx, "a3_bc3", [P, T], BF16)
        A = k.sb(ctx, "a3_A", [P, 1, NS])
        with ExitStack() as sub:
            padded = k.sb(sub, "a3_padded", [P, 2, NB, SEQ + 3])
            proj, x_out, zero, conv = k.sems(ctx, "a3_", "proj x_out zero conv")
            with nc.Block() as block:

                @block.tensor
                def _(pe):
                    for n in range(8):
                        pe.matmul(ps[:, n, :], w["a3_in"][:, tile(n // 4)], k.xn[:, chunk(n % 4)], start=True, stop=True).then_inc(proj, 1)

                @block.scalar
                def _(act):
                    for n in range(8):
                        act.wait_ge(proj, n + 1)
                        act.activation(padded[:, n // 4, n % 4 // 2, 1 + CH * (n % 2):1 + CH * (n % 2) + CH], ps[:, n, :],
                                       ACT.Copy).then_inc(x_out, 1)
                    for m in range(2):
                        act.wait_ge(conv, 7 + m)
                        act.activation(xz[:, m, :], xz[:, m, :], ACT.Silu)

                @block.vector
                def _(dve):
                    dve.memset(padded[:, :, :, 0:1], 0.0).then_inc(zero, 1)
                    dve.memset(padded[:, :, :, SEQ + 1:SEQ + 3], 0.0).then_inc(zero, 1)
                    dve.wait_ge(zero, 2)
                    dve.wait_ge(x_out, 8)
                    for tap in range(4):
                        for m in range(2):
                            dst = xz[:, m, :].rearrange("p (b t) -> p b t", b=NB)
                            src = padded[:, m, :, tap:tap + SEQ]
                            kern = w["a3_conv"][:, m, tap:tap + 1]
                            if tap == 0:
                                dve.tensor_scalar(dst, src, kern, None, ALU.mult).then_inc(conv, 1)
                            else:
                                dve.wait_ge(conv, 2 * (tap - 1) + m + 1)
                                dve.scalar_tensor_tensor(out=dst, in0=src, scalar=kern, in1=dst, op0=ALU.mult,
                                                         op1=ALU.add).then_inc(conv, 1)
        with ExitStack() as sub:
            low = k.sb(sub, "a3_low", [P, T])
            up = k.sb(sub, "a3_up", [P, T])
            upped, = k.sems(ctx, "a3_", "upped")
            dtr = k.sb(sub, "a3_dtrows", [8, T])
            b2 = k.sb(sub, "a3_b2", [P, 1])
            rows, drows, dcopy, pre, soft, aexp, summed, biased = k.sems(ctx, "a3_", "rows drows dcopy pre soft aexp summed biased")
            s, mid, rest, psrows = split_rows(k, ctx, bc3, "a3")
            with nc.Block() as block:

                @block.tensor
                def _(pe):
                    for j in range(NCH):
                        pe.matmul(ps[0:8, 4 + j, :], w["a3_dtr"], xz[:, 0, chunk(j)], start=True, stop=True).then_inc(drows, 1)
                    for j in range(NCH):
                        pe.matmul(ps[0:96, j, :], w["a3_bc"][:, 0, :], xz[:, 0, chunk(j)], start=True, stop=True).then_inc(rows, 1)
                    pe.wait_ge(dcopy, 1)
                    for j in range(NCH):
                        pe.matmul(ps[:, 4 + j, :], w["a3_dt_w"], dtr[:, chunk(j)], start=True, stop=True).then_inc(pre, 1)

                @block.scalar
                def _(act):
                    act.activation(A[:, 0, :], w["a3_alog"], ACT.Exp).then_inc(aexp, 1)
                    act.wait_ge(drows, NCH)
                    act.activation(dtr[:, :], ps[0:8, 4:8, :].rearrange("p a b -> p (a b)"), ACT.Copy).then_inc(dcopy, 1)
                    act.wait_ge(pre, NCH)
                    act.wait_ge(biased, 1)
                    v = ps[:, 4:8, :].rearrange("p a b -> p (a b)")
                    act.activation(dt[:, 0, :], v, ACT.Relu, bias=b2[:, 0:1]).then_inc(soft, 1)
                    act.activation(low[:, :], v, ACT.Abs, bias=b2[:, 0:1]).then_inc(soft, 1)
                    act.wait_ge(soft, 2)
                    act.activation(low[:, :], low[:, :], ACT.Exp, scale=-1.0).then_inc(soft, 1)
                    act.wait_ge(upped, 1)
                    act.activation(k.t3[:, :], up[:, :], ACT.Ln).then_inc(soft, 1)

                @block.vector
                def _(dve):
                    dve.tensor_scalar(b2[:, :], w["a3_dt_b"], 2.0, None, ALU.mult).then_inc(biased, 1)
                    dve.wait_ge(rows, NCH)
                    split_steps(dve, k, s, mid, rest, psrows, bc3)
                    dve.wait_ge(soft, 3)
                    softplus_steps(dve, k, dt[:, 0, :], low, up, upped, soft, 4, summed, 0)
                    dve.tensor_tensor(du[:, 0, :], dt[:, 0, :], xz[:, 0, :], ALU.mult)
                    dve.wait_ge(aexp, 1)
                    dve.tensor_scalar(A[:, 0, :], A[:, 0, :], -1.0, None, ALU.mult)
        with ExitStack() as sub:
            def finish(dve, b, hf, y):
                v = xz[:, 0, bass.ds(b * SEQ, SEQ)]
                return dve.scalar_tensor_tensor(out=v, in0=v, scalar=w["a3_D"][:, 0:1], in1=y, op0=ALU.mult, op1=ALU.add)

            scan_loop(k, sub, "a3s", 1, du, bc3, finish, dt=dt, rate=A)
        with nc.Block() as block:

            @block.scalar
            def _(act):
                act.activation(k.x[:, :], k.x[:, :], ACT.Identity, bias=w["a3_bout"][:, 0:1])
        project_out(k, ctx, "a3p", w["a3_out"], xz)


MIDS = (5.0, 3.5, 2.5, 1.75, 1.25, 0.75, 0.25)


class Fp4:

    STEPS, PARTS = 14, 2

    def __init__(self, k, ctx, name, nblk):
        self.k, self.n = k, nblk
        self.step, self.parts = k.sems(ctx, name + "_", "step parts")
        self.amax = k.sb(ctx, name + "_amax", [P, nblk])
        self.rec = k.sb(ctx, name + "_rec", [P, nblk])
        self.ab = k.sb(ctx, name + "_ab", [P, nblk * 16])
        self.sg = k.sb(ctx, name + "_sg", [P, nblk * 16])
        self.xs = k.sb(ctx, name + "_xs", [P, nblk * 16])

    def blocks(self, v):
        return v.rearrange("p (n c) -> p n c", c=16)

    def scalar(self, act, wait, n0):
        wait(act, self.step, n0 * self.STEPS + 4)
        act.activation(self.ab[:, :], self.xs[:, :], ACT.Abs).then_inc(self.parts, 1)
        act.activation(self.sg[:, :], self.xs[:, :], ACT.Sign).then_inc(self.parts, 1)

    def vector(self, dve, wait, n0, src, dst):
        base = n0 * self.STEPS
        bc = lambda v: v.unsqueeze(2).to_broadcast([P, self.n, 16])
        count = [0]

        def done(ins):
            ins.then_inc(self.step, 1)
            count[0] += 1
            wait(dve, self.step, base + count[0])

        done(dve.tensor_reduce(self.amax[:, :], self.blocks(src), AX.X, ALU.max, apply_absolute_value=True))
        done(dve.tensor_scalar(self.amax[:, :], self.amax[:, :], 1.0 / 6.0, 1e-12, ALU.mult, ALU.max))
        done(dve.reciprocal(self.rec[:, :], self.amax[:, :]))
        done(dve.tensor_tensor(self.blocks(self.xs[:, :]), self.blocks(src), bc(self.rec[:, :]), ALU.mult))
        wait(dve, self.parts, n0 * self.PARTS + 2)
        ab, q = self.ab[:, :], self.xs[:, :]
        done(dve.tensor_scalar(q, ab, MIDS[0], 2.0, ALU.is_gt, ALU.mult))
        for m in MIDS[1:3]:
            done(dve.scalar_tensor_tensor(out=q, in0=ab, scalar=m, in1=q, op0=ALU.is_gt, op1=ALU.add))
        done(dve.tensor_scalar(q, q, 2.0, None, ALU.mult))
        for m in MIDS[3:]:
            done(dve.scalar_tensor_tensor(out=q, in0=ab, scalar=m, in1=q, op0=ALU.is_gt, op1=ALU.add))
        done(dve.scalar_tensor_tensor(out=q, in0=q, scalar=0.5, in1=self.sg[:, :], op0=ALU.mult, op1=ALU.mult))
        done(dve.tensor_tensor(self.blocks(dst), self.blocks(q), bc(self.amax[:, :]), ALU.mult))
        assert count[0] == self.STEPS


def static_wait(eng, sem, n):
    eng.wait_ge(sem, n)


def layer3_ffn(k, W):
    nc, ps = k.nc, k.ps
    I = 352
    PARTS = [(0, P), (P, P), (2 * P, I - 2 * P)]
    with ExitStack() as ctx:
        wgu, wd = W("f3_gu"), W("f3_down")
        wt = k.sb(ctx, "f3_wt", [P, 6, P])
        wdt = k.sb(ctx, "f3_wdt", [P, 3, P])
        xq = k.sb(ctx, "f3_xq", [P, T])
        NW = 6 * P + I
        allw = k.sb(ctx, "f3_wq", [P, NW])
        with ExitStack() as sub:
            fq = Fp4(k, sub, "f3w", NW // 16)
            turned, out = k.sems(ctx, "f3w_", "turned out")
            with nc.Block() as block:

                @block.vector
                def _(dve):
                    fq.vector(dve, static_wait, 0, k.w3[:, 0:NW], allw[:, :])

                @block.scalar
                def _(act):
                    fq.scalar(act, static_wait, 0)
                    act.wait_ge(turned, 1)
                    act.activation(wt[:, :, :].rearrange("p m c -> p (m c)"), ps[:, 0:2, 0:3 * P], ACT.Copy)
                    act.activation(wdt[:, 0:2, :], ps[:, 2, 0:2 * P].rearrange("p (m c) -> p m c", m=2), ACT.Copy)
                    act.activation(wdt[0:96, 2, :], ps[0:96, 3, 0:P], ACT.Copy)

                @block.tensor
                def _(pe):
                    pe.wait_ge(fq.step, fq.STEPS)
                    for m in range(6):
                        pe.transpose(ps[:, m // 3, tile(m % 3)], allw[:, tile(m)], k.ident[:, :])
                    for m, (a, n) in enumerate(PARTS):
                        mm = pe.transpose(ps[0:n, 2 if m < 2 else 3, tile(m if m < 2 else 0)], allw[:, 6 * P + a:6 * P + a + n], k.ident[:, :])
                    mm.then_inc(turned, 1)
        with ExitStack() as sub:
            fq = Fp4(k, sub, "f3x", T // 16)
            turned, copied, back = k.sems(ctx, "f3x_", "turned copied back")
            with nc.Block() as block:

                @block.tensor
                def _(pe):
                    for t in range(NT):
                        mm = pe.transpose(ps[:, t // 4, tile(t % 4)], k.xn[:, tile(t)], k.ident[:, :])
                    mm.then_inc(turned, 1)
                    pe.wait_ge(fq.step, fq.STEPS)
                    for t in range(NT):
                        mm = pe.transpose(ps[:, 4 + t // 4, tile(t % 4)], k.t1[:, tile(t)], k.ident[:, :])
                    mm.then_inc(back, 1)

                @block.vector
                def _(dve):
                    dve.wait_ge(turned, 1)
                    fq.vector(dve, static_wait, 0, ps[:, 0:4, :].rearrange("p a b -> p (a b)"), k.t1[:, :])

                @block.scalar
                def _(act):
                    fq.scalar(act, static_wait, 0)
                    act.wait_ge(back, 1)
                    act.activation(xq[:, :], ps[:, 4:8, :].rearrange("p a b -> p (a b)"), ACT.Copy)
        sg = k.sb(ctx, "f3_sg", [P, 4, I])
        h = k.sb(ctx, "f3_h", [P, 2, 4 * I])
        ht = k.sb(ctx, "f3_ht", [P, 3, CH])
        yb = k.sb(ctx, "f3_y", [P, 2, CH])
        fq = Fp4(k, ctx, "f3h", 4 * I // 16)
        prod, silu, hid, turned, ht_done, y, y_copied, added = k.sems(ctx, "f3l_", "prod silu hid turned ht y y_copied added")
        tiles_of = lambda v: v.rearrange("p (t i) -> p t i", t=4)
        with nc.Block() as block:

            @block.scalar
            def _(act):
                def gates(c):
                    act.wait_ge(prod, c + 1)
                    act.activation(sg[:, :, :], ps[:, 0:4, 0:I], ACT.Silu).then_inc(silu, 1)

                gates(0)
                for c in range(NCH):
                    fq.scalar(act, static_wait, c)
                    if c + 1 < NCH:
                        gates(c + 1)
                    act.wait_ge(turned, c + 1)
                    act.activation(ht[:, 0:2, :], ps[:, 0:2, :], ACT.Copy).then_inc(ht_done, 1)
                    act.activation(ht[0:96, 2, :], ps[0:96, 2, :], ACT.Copy).then_inc(ht_done, 1)
                    act.wait_ge(y, c + 1)
                    if c >= 2:
                        act.wait_ge(added, c - 1)
                    act.activation(yb[:, c % 2, :], ps[:, 3, :], ACT.Copy).then_inc(y_copied, 1)

            @block.tensor
            def _(pe):
                def products(c):
                    if c >= 1:
                        pe.wait_ge(hid, c)
                        pe.wait_ge(silu, c)
                    if c >= 2:
                        pe.wait_ge(y_copied, c - 1)
                    for t in range(4):
                        at = CH * c + P * t
                        pe.matmul(ps[:, t, 0:I], xq[:, at:at + P], wt[:, 0:3, :].rearrange("p m c -> p (m c)")[:, 0:I], start=True, stop=True)
                        mm = pe.matmul(ps[:, 4 + t, 0:I], xq[:, at:at + P], wt[:, 3:6, :].rearrange("p m c -> p (m c)")[:, 0:I], start=True, stop=True)
                    mm.then_inc(prod, 1)

                products(0)
                products(1)
                for c in range(NCH):
                    pe.wait_ge(fq.step, (c + 1) * fq.STEPS)
                    pe.wait_ge(silu, min(c + 2, NCH))
                    for m, (a, n) in enumerate(PARTS):
                        for t in range(4):
                            mm = pe.transpose(ps[0:n, m, tile(t)], tiles_of(h[:, c % 2, :])[:, t, a:a + n], k.ident[:, :])
                    mm.then_inc(turned, 1)
                    pe.wait_ge(ht_done, 2 * c + 2)
                    for m, (a, n) in enumerate(PARTS):
                        mm = pe.matmul(ps[:, 3, :], wdt[0:n, m, :], ht[0:n, m, :], start=(m == 0), stop=(m == 2))
                    mm.then_inc(y, 1)
                    if c + 2 < NCH:
                        products(c + 2)

            @block.vector
            def _(dve):
                def add(c):
                    dve.wait_ge(y_copied, c + 1)
                    dve.tensor_tensor(k.x[:, chunk(c)], k.x[:, chunk(c)], yb[:, c % 2, :], ALU.add).then_inc(added, 1)

                for c in range(NCH):
                    dve.wait_ge(silu, c + 1)
                    if c >= 2:
                        dve.wait_ge(turned, c - 1)
                    hc = h[:, c % 2, :]
                    dve.tensor_tensor(tiles_of(hc), sg[:, :, :], ps[:, 4:8, 0:I], ALU.mult).then_inc(hid, 1)
                    dve.wait_ge(hid, c + 1)
                    fq.vector(dve, static_wait, c, hc, hc)
                    if c >= 1:
                        add(c - 1)
                add(NCH - 1)


def more_layouts(np, a, L, f, col, kt, three, choose, eh):
    g = lambda n: f(a["L2_attn_" + n])
    L["a2"] = dict(a2_wo=kt(g("Wo")), a2_bo=col(g("bo")), a2_g=col(g("gamma")), a2_b=col(g("beta")),
                   a2_lam=np.full((128, 1), g("lam"), np.float32))
    wq, wk, wv, bq, bk, bv = (g(n) for n in ("Wq", "Wk", "Wv", "bq", "bk", "bv"))
    pairs = {}
    for p in list(range(8)) + [7]:
        cols = []
        for h in (2 * p, 2 * p + 1):
            cols.append(wq[h])
        for h in (2 * p, 2 * p + 1):
            for m in range(2):
                cols += [wk[h][:, 64 * m:64 * m + 64]] * 2
        cols += [wv[2 * p], wv[2 * p + 1], bq[2 * p][:, None], bq[2 * p + 1][:, None]]
        for h in (2 * p, 2 * p + 1):
            for m in range(2):
                cols.append(np.tile(bk[h][64 * m:64 * m + 64], 2)[:, None])
        cols.append(np.concatenate([bv[2 * p], bv[2 * p + 1]])[:, None])
        pairs[f"pair{len(pairs)}"] = np.concatenate(cols, axis=1)
    L["a2w"] = pairs
    g = lambda n: f(a["L2_ffn_" + n])
    two = lambda v: v.reshape(32, 2, 128, 64).transpose(2, 0, 1, 3).reshape(128, 32, 128)
    sel = np.zeros((64, 32, 128), np.float32)
    for e in range(64):
        sel[e, e // 2, 64 * (e % 2):64 * (e % 2) + 64] = 1
    L["f2"] = dict(f2_router=g("router_w"), f2_gate=two(g("gate_w")), f2_up=two(g("up_w")),
                   f2_down=g("down_w").reshape(32, 128, 128).transpose(1, 0, 2), f2_sg=g("shared_gate_w"),
                   f2_su=g("shared_up_w"), f2_sd=g("shared_down_w"), f2_sel=np.concatenate([sel, sel]))
    g = lambda n: f(a["L3_attn_" + n])
    L["a3"] = dict(a3_in=g("W_in"), a3_conv=np.stack([g("conv_x_k")[:, 0, :].T, g("conv_z_k")[:, 0, :].T], axis=1),
                   a3_bc=three(g("W_xproj")[:, 8:40]), a3_dtr=g("W_xproj")[:, 0:8], a3_dt_w=g("W_dt"), a3_dt_b=col(g("b_dt")),
                   a3_alog=g("A_log"), a3_D=col(g("D")), a3_out=kt(g("W_out")), a3_bout=col(g("b_out")))
    g = lambda n: f(a["L3_ffn_" + n])

    def rows(v):
        out = np.zeros((384, 128), np.float32)
        out[:352] = v
        return out.reshape(3, 128, 128).transpose(1, 0, 2)

    L["f3"] = dict(f3_gu=np.concatenate([rows(g("w_gate")), rows(g("w_up"))], axis=1), f3_down=g("w_down"))


def program(nc, views, x_dram, sel_dram, out_dram):
    with ExitStack() as ctx:
        k = Kit(nc, ctx, views)
        k.sel_dram = sel_dram
        x_loaded, consts, turned, stored = k.sems(ctx, "main_", "x_loaded consts turned stored")
        with nc.Block() as block:

            @block.sync
            def _(sp):
                sp.dma_start(k.x[:, :], x_dram).then_inc(x_loaded, 16)
                sp.wait_ge(x_loaded, 16)

            @block.gpsimd
            def _(pool):
                pool.memset(k.ones[:, :], 1.0 / P)
                pool.memset(k.eps5[:, :], 1e-5)
                pool.memset(k.eps6[:, :], 1e-6)
                pool.memset(k.ident[:, :], 0.0).then_inc(consts, 1)
                pool.wait_ge(consts, 1)
                pool.affine_select(out=k.ident[:, :], in_=k.ident[:, :], compare_op=ALU.not_equal, fill=1.0, base=0,
                                   pattern=[[-1, P]], channel_multiplier=1)

        for n, (attn, ffn) in enumerate(((layer0_attn, layer0_ffn), (layer1_attn, layer1_ffn), (layer2_attn, layer2_ffn),
                                         (layer3_attn, layer3_ffn))):
            if n not in LAYERS:
                continue
            for part, half in ((attn, "a"), (ffn, "f")):
                with ExitStack() as sub:
                    k.ctx, k.counted = sub, []
                    get = load(k, sub, f"{half}{n}")
                    if half == "a":
                        layer_norm(k, k.x, k.xn, k.eps5)
                    wait_loaded(k, 0)
                    if f"{half}{n}" not in ("f0", "f1", "f2"):
                        wait_loaded(k, 1)
                    part(k, get)
                    k.clear_counts()
        with nc.Block() as block:

            @block.sync
            def _(sp):
                sp.dma_start(out_dram, k.x[:, :]).then_inc(stored, 16)
                sp.wait_ge(stored, 16)


def layouts(np, a):
    f = lambda v: np.asarray(v)
    col = lambda v: f(v).reshape(-1, 128).T
    kt = lambda v: f(v).reshape(-1, 128, f(v).shape[-1]).transpose(1, 0, 2)

    def three(v):
        return np.concatenate([kt(v)] * 3, axis=2)

    def choose(n):
        out = np.zeros((128, n, 128), np.float32)
        for r in range(n):
            out[r, r, :] = out[32 + r, r, :] = 1.0
        return out

    L = {}
    g = lambda n: f(a["L0_attn_" + n])
    xp = g("x_proj_w").T
    L["a0"] = dict(a0_norm_w=col(g("norm_w")), a0_norm_b=col(g("norm_b")), a0_in=g("in_proj_w").T,
                   a0_conv=g("conv_w").transpose(1, 2, 0).reshape(2, 128, 4, 256).transpose(1, 2, 0, 3).reshape(128, 8, 256),
                   a0_conv_b=col(g("conv_b")), a0_bc=three(xp[:, 1:33]), a0_ds=kt(np.repeat(xp[:, 0:1], 128, axis=1)),
                   a0_dt_w=col(g("dt_w")), a0_dt_b=col(g("dt_b")), a0_out=kt(g("out_proj_w").T))
    g = lambda n: f(a["L0_ffn_" + n])
    eh = lambda v, m: v.reshape(v.shape[0], m, 128).transpose(2, 0, 1)
    L["f0"] = dict(f0_gate=g("gate_w"), f0_w1=g("w1").transpose(1, 0, 2), f0_b1=eh(g("b1"), 2), f0_g=eh(g("ln1_g"), 2),
                   f0_b=eh(g("ln1_b"), 2), f0_w2=g("w2").reshape(16, 128, 128).transpose(1, 0, 2), f0_b2=g("b2").T,
                   f0_ln_g=col(g("ln_g")), f0_ln_b=col(g("ln_b")), f0_sel=choose(8))
    g = lambda n: f(a["L1_attn_" + n])
    L["a1"] = dict(a1_norm_w=col(g("norm_w")), a1_in=g("in_proj_w"), a1_conv=g("conv_w")[:, 0, :].reshape(2, 128, 4).transpose(1, 0, 2),
                   a1_dt_w=kt(g("dt_w")), a1_dt_b=col(g("dt_b")), a1_alog=kt(g("A_log")),
                   a1_bc=three(np.concatenate([g("B_w"), g("C_w")], axis=1)), a1_D=col(g("D_skip")), a1_out=kt(g("out_proj_w")))
    g = lambda n: f(a["L1_ffn_" + n])
    L["f1"] = dict(f1_gate=g("gate_W"), f1_w1=g("W1").reshape(8, 128, 4, 128).transpose(1, 0, 2, 3).reshape(128, 32, 128),
                   f1_b1=eh(g("b1"), 4), f1_w2=g("W2").reshape(32, 128, 128).transpose(1, 0, 2), f1_b2=g("b2").T,
                   f1_sw=g("shared_W"), f1_sb=col(g("shared_b")), f1_g=col(g("gamma")), f1_b=col(g("beta")), f1_sel=choose(8))
    more_layouts(np, a, L, f, col, kt, three, choose, eh)
    return L


def kernel(**inputs):
    import numpy as _np
    import concourse.bacc as _bacc
    from concourse import mybir as _mybir
    from concourse.bass_utils import run_bass_kernel_spmd as _run

    nc = _bacc.Bacc("TRN2", target_bir_lowering=False, num_devices=1)
    arrays, views = {}, {}
    for name, parts in layouts(_np, inputs).items():
        cols, places, blocks = 0, {}, []
        for part, v in parts.items():
            places[part] = (cols, v.shape)
            v = v.reshape(v.shape[0], -1)
            full = _np.zeros((128, v.shape[1]), _np.float32)
            full[:v.shape[0]] = v
            blocks.append(full)
            cols += v.shape[1]
        packed = _np.ascontiguousarray(_np.concatenate(blocks, axis=1))
        arrays[f"in_{name}_dram"] = packed
        views[name] = (nc.dram_tensor(f"in_{name}_dram", packed.shape, _mybir.dt.float32, kind="ExternalInput").ap(), places)
    x = _np.ascontiguousarray(_np.asarray(inputs["L0_attn_x"]).reshape(2048, 128).T)
    arrays["in_x_dram"] = x
    x_dram = nc.dram_tensor("in_x_dram", x.shape, _mybir.dt.float32, kind="ExternalInput").ap()
    sel = _np.zeros((128, 32, 128), _mybir.dt.np(_mybir.dt.bfloat16))
    for r in range(96):
        sel[r, r % 32, :] = 1
    arrays["in_sel_dram"] = sel
    sel_dram = nc.dram_tensor("in_sel_dram", sel.shape, _mybir.dt.bfloat16, kind="ExternalInput").ap()
    out_dram = nc.dram_tensor("out_0_dram", (128, 2048), _mybir.dt.float32, kind="ExternalOutput").ap()
    program(nc, views, x_dram, sel_dram, out_dram)
    r = _run(nc, [arrays], core_ids=[0])
    return _np.ascontiguousarray(r.results[0]["out_0_dram"].T).reshape(2, 1024, 128)
```
